# Optimizing a Trainium2 kernel written in Bass

```python
import numpy as np
import jax
import jax.numpy as jnp

def _softmax(x, axis=-1):
    return jax.nn.softmax(x, axis=axis)

def _gelu(x):
    return jax.nn.gelu(x, approximate=True)

def _silu(x):
    return jax.nn.silu(x)

def _sigmoid(x):
    return jax.nn.sigmoid(x)

def _layernorm(x, axis=-1, eps=1e-05):
    m = jnp.mean(x, axis=axis, keepdims=True)
    v = jnp.var(x, axis=axis, keepdims=True)
    return (x - m) / jnp.sqrt(v + eps)

def _scatter_add(tgt, idx, src, axis=0):
    return tgt.at[idx].add(src)

def _segment_sum(src, seg, n):
    return jax.ops.segment_sum(src, seg, n)
kernel_name = 'mk_gnn_preln_d4_gnn_r8_1630f1'

def setup_inputs(seed: int=0):
    np.random.seed(seed)
    _w = jnp.asarray

    def _rec_inputs():
        import jax
        import jax.numpy as jnp
        _gk = jax.random.key(seed)
        x = -0.0005121 + 1.001 * jax.random.normal(jax.random.fold_in(_gk, 1), (12500, 32), jnp.float32)
        src = jax.random.randint(jax.random.fold_in(_gk, 2), (200000,), 0, 12500, jnp.int32)
        dst = jax.random.randint(jax.random.fold_in(_gk, 3), (200000,), 0, 12500, jnp.int32)
        _o = jnp.argsort(dst, stable=True)
        src = src[_o]
        dst = dst[_o]
        edge_attr_3 = 0.000549083 + 1.00031 * jax.random.normal(jax.random.fold_in(_gk, 12), (200000, 3), jnp.float32)
        edge_attr_5 = -0.000325185 + 1.00005 * jax.random.normal(jax.random.fold_in(_gk, 13), (200000, 5), jnp.float32)
        edge_type_86 = jax.random.randint(jax.random.fold_in(_gk, 15), (200000,), 0, 86, jnp.int32)
        edge_weight1 = 0.000452788 + 0.999756 * jax.random.normal(jax.random.fold_in(_gk, 16), (200000, 1), jnp.float32)
        return (x, src, dst, edge_attr_3, edge_attr_5, edge_type_86, edge_weight1)
    x, src, dst, edge_attr_3, edge_attr_5, edge_type_86, edge_weight1 = _rec_inputs()

    def _L0_gnn_setup():
        import jax, jax.numpy as jnp
        import numpy as np
        N_NODES = 12500
        N_EDGES = 200000
        IN_F = 32
        HID = 128

        def _gcn_norm(edge_index, n_nodes):
            loops = jnp.arange(n_nodes, dtype=edge_index.dtype)
            src = jnp.concatenate([edge_index[0], loops])
            dst = jnp.concatenate([edge_index[1], loops])
            ones = jnp.ones(src.shape[0], dtype=jnp.float32)
            deg = jax.ops.segment_sum(ones, dst, num_segments=n_nodes)
            deg_inv_sqrt = jnp.where(deg > 0, jax.lax.rsqrt(deg), 0.0)
            norm = deg_inv_sqrt[src] * deg_inv_sqrt[dst]
            return (src, dst, norm)

        def _gcn_conv(x, src, dst, norm, W, b, n_nodes):
            h = x @ W
            msg = h[src] * norm[:, None]
            out = jax.ops.segment_sum(msg, dst, num_segments=n_nodes)
            return out + b
        key = jax.random.key(seed)
        ks = jax.random.split(key, 8)
        x = jax.random.normal(ks[0], (N_NODES, IN_F), dtype=jnp.float32)
        edge_index = jax.random.randint(ks[1], (2, N_EDGES), 0, N_NODES, dtype=jnp.int64)
        W1 = jax.random.normal(ks[2], (IN_F, HID), dtype=jnp.float32) / np.sqrt(IN_F)
        b1 = jnp.zeros((HID,), dtype=jnp.float32)
        W2 = jax.random.normal(ks[3], (HID, HID), dtype=jnp.float32) / np.sqrt(HID)
        b2 = jnp.zeros((HID,), dtype=jnp.float32)
        W3 = jax.random.normal(ks[4], (HID, IN_F), dtype=jnp.float32) / np.sqrt(HID)
        b3 = jnp.zeros((IN_F,), dtype=jnp.float32)
        return {'x': x, 'edge_index': edge_index, 'W1': W1, 'b1': b1, 'W2': W2, 'b2': b2, 'W3': W3, 'b3': b3}
    _L0_gnn_all = _L0_gnn_setup()
    _L0_gnn_in = {k: v for k, v in _L0_gnn_all.items() if k in ('W1', 'b1', 'W2', 'b2', 'W3', 'b3')}
    del _L0_gnn_all

    def _L1_gnn_setup():
        import jax, jax.numpy as jnp
        import numpy as np
        N_NODES = 12500
        N_EDGES = 400000
        D_IN = 32
        N_HEADS = 4
        D_HEAD = 8
        key = jax.random.key(seed)
        k1, k2, k3, k4, k5, k6, k7 = jax.random.split(key, 7)
        scale = 1.0 / np.sqrt(D_IN)
        x = jax.random.normal(k1, (N_NODES, D_IN), dtype=jnp.float32)
        Wq = jax.random.normal(k2, (D_IN, N_HEADS * D_HEAD), dtype=jnp.float32) * scale
        Wk = jax.random.normal(k3, (D_IN, N_HEADS * D_HEAD), dtype=jnp.float32) * scale
        Wv = jax.random.normal(k4, (D_IN, N_HEADS * D_HEAD), dtype=jnp.float32) * scale
        Wo = jax.random.normal(k5, (N_HEADS * D_HEAD, D_IN), dtype=jnp.float32) * scale
        src = jax.random.randint(k6, (N_EDGES,), 0, N_NODES)
        dst = jax.random.randint(k7, (N_EDGES,), 0, N_NODES)
        edge_index = jnp.stack([src, dst], axis=0).astype(jnp.int64)
        return {'x': x, 'Wq': Wq, 'Wk': Wk, 'Wv': Wv, 'Wo': Wo, 'edge_index': edge_index}
    _L1_gnn_all = _L1_gnn_setup()
    _L1_gnn_in = {k: v for k, v in _L1_gnn_all.items() if k in ('Wq', 'Wk', 'Wv', 'Wo')}
    del _L1_gnn_all

    def _L2_gnn_setup():
        import jax, jax.numpy as jnp
        import numpy as np
        N_NODES = 6250
        N_EDGES = 100000
        INP_DIM = 32
        OUT_DIM = 32
        ATTN_DIM = 32
        NUM_RELS = 86
        NUM_BASES = 16
        GAMMA = 0.0
        key = jax.random.key(seed)
        ks = jax.random.split(key, 12)
        return {'h': jax.random.normal(ks[0], (N_NODES, INP_DIM), jnp.float32), 'weight': jax.random.normal(ks[1], (NUM_BASES, INP_DIM, OUT_DIM), jnp.float32), 'w_comp': jax.random.normal(ks[2], (NUM_RELS, NUM_BASES), jnp.float32), 'self_loop_weight': jax.random.normal(ks[3], (INP_DIM, OUT_DIM), jnp.float32), 'A1_w': jax.random.normal(ks[4], (ATTN_DIM, INP_DIM), jnp.float32), 'A1_b': jax.random.normal(ks[5], (ATTN_DIM,), jnp.float32), 'A2_w': jax.random.normal(ks[6], (ATTN_DIM, INP_DIM), jnp.float32), 'A2_b': jax.random.normal(ks[7], (ATTN_DIM,), jnp.float32), 'rel_emb': jax.random.normal(ks[8], (NUM_RELS, ATTN_DIM), jnp.float32), 'src': jax.random.randint(ks[9], (N_EDGES,), 0, N_NODES, jnp.int32), 'dst': jax.random.randint(ks[10], (N_EDGES,), 0, N_NODES, jnp.int32), 'etype': jax.random.randint(ks[11], (N_EDGES,), 0, NUM_RELS, jnp.int32)}
    _L2_gnn_all = _L2_gnn_setup()
    _L2_gnn_in = {k: v for k, v in _L2_gnn_all.items() if k in ('weight', 'w_comp', 'self_loop_weight', 'A1_w', 'A1_b', 'A2_w', 'A2_b', 'rel_emb')}
    del _L2_gnn_all

    def _L3_gnn_setup():
        import jax, jax.numpy as jnp
        import numpy as np
        import math
        M = 8
        COMBOS = [(0, 0, 0), (0, 1, 1), (1, 0, 1), (1, 1, 0), (1, 1, 1), (2, 1, 1)]

        def _cg_coeff(j1, m1, j2, m2, j3, m3):
            if m3 != m1 + m2:
                return 0.0
            f = math.factorial
            vmin = max(0, j2 - j3 - m1, j1 + m2 - j3)
            vmax = min(j1 + j2 - j3, j1 - m1, j2 + m2)
            pref = (2 * j3 + 1) * f(j3 + j1 - j2) * f(j3 - j1 + j2) * f(j1 + j2 - j3) / f(j1 + j2 + j3 + 1)
            pref *= f(j3 + m3) * f(j3 - m3) * f(j1 - m1) * f(j1 + m1) * f(j2 - m2) * f(j2 + m2)
            s = 0.0
            for v in range(vmin, vmax + 1):
                s += (-1) ** v / (f(v) * f(j1 + j2 - j3 - v) * f(j1 - m1 - v) * f(j2 + m2 - v) * f(j3 - j2 + m1 + v) * f(j3 - j1 - m2 + v))
            return math.sqrt(pref) * s

        def _su2_cg(l1, l2, l3):
            C = np.zeros((2 * l1 + 1, 2 * l2 + 1, 2 * l3 + 1), dtype=np.complex128)
            for m1 in range(-l1, l1 + 1):
                for m2 in range(-l2, l2 + 1):
                    m3 = m1 + m2
                    if -l3 <= m3 <= l3:
                        C[m1 + l1, m2 + l2, m3 + l3] = _cg_coeff(l1, m1, l2, m2, l3, m3)
            return C

        def _qmat(l):
            q = np.zeros((2 * l + 1, 2 * l + 1), dtype=np.complex128)
            for m in range(-l, 0):
                q[l + m, l + abs(m)] = 1 / np.sqrt(2)
                q[l + m, l - abs(m)] = -1j / np.sqrt(2)
            q[l, l] = 1.0
            for m in range(1, l + 1):
                q[l + m, l + abs(m)] = (-1) ** m / np.sqrt(2)
                q[l + m, l - abs(m)] = 1j * (-1) ** m / np.sqrt(2)
            return (-1j) ** l * q

        def _so3_cg(l1, l2, l3):
            C = np.einsum('ij,kl,mn,ikn->jlm', _qmat(l1), _qmat(l2), np.conj(_qmat(l3)).T, _su2_cg(l1, l2, l3))
            assert np.abs(C.imag).max() < 1e-06
            C = C.real
            return C / np.linalg.norm(C)
        CG = {c: jnp.asarray(_so3_cg(*c), dtype=jnp.float32) for c in COMBOS}
        N, E = (12500, 200000)
        ks = jax.random.split(jax.random.key(seed), 6)
        return {'node_irreps': jax.random.normal(ks[0], (N, 4 * M), jnp.float32), 'edge_index': jax.random.randint(ks[1], (2, E), 0, N, dtype=jnp.int32), 'sh0': jax.random.normal(ks[2], (E, 1), jnp.float32), 'sh1': jax.random.normal(ks[3], (E, 3), jnp.float32), 'sh2': jax.random.normal(ks[4], (E, 5), jnp.float32), 'W': jax.random.normal(ks[5], (len(COMBOS), M, M), jnp.float32)}
    _L3_gnn_all = _L3_gnn_setup()
    _L3_gnn_in = {k: v for k, v in _L3_gnn_all.items() if k in ('W',)}
    del _L3_gnn_all
    return {'x': x, 'src': src, 'dst': dst, 'edge_attr_3': edge_attr_3, 'edge_attr_5': edge_attr_5, 'edge_type_86': edge_type_86, 'edge_weight1': edge_weight1, 'L0_gnn_W1': _L0_gnn_in['W1'], 'L0_gnn_b1': _L0_gnn_in['b1'], 'L0_gnn_W2': _L0_gnn_in['W2'], 'L0_gnn_b2': _L0_gnn_in['b2'], 'L0_gnn_W3': _L0_gnn_in['W3'], 'L0_gnn_b3': _L0_gnn_in['b3'], 'L1_gnn_Wq': _L1_gnn_in['Wq'], 'L1_gnn_Wk': _L1_gnn_in['Wk'], 'L1_gnn_Wv': _L1_gnn_in['Wv'], 'L1_gnn_Wo': _L1_gnn_in['Wo'], 'L2_gnn_weight': _L2_gnn_in['weight'], 'L2_gnn_w_comp': _L2_gnn_in['w_comp'], 'L2_gnn_self_loop_weight': _L2_gnn_in['self_loop_weight'], 'L2_gnn_A1_w': _L2_gnn_in['A1_w'], 'L2_gnn_A1_b': _L2_gnn_in['A1_b'], 'L2_gnn_A2_w': _L2_gnn_in['A2_w'], 'L2_gnn_A2_b': _L2_gnn_in['A2_b'], 'L2_gnn_rel_emb': _L2_gnn_in['rel_emb'], 'L3_gnn_W': _L3_gnn_in['W']}

def reference(x, src, dst, edge_attr_3, edge_attr_5, edge_type_86, edge_weight1, L0_gnn_W1, L0_gnn_b1, L0_gnn_W2, L0_gnn_b2, L0_gnn_W3, L0_gnn_b3, L1_gnn_Wq, L1_gnn_Wk, L1_gnn_Wv, L1_gnn_Wo, L2_gnn_weight, L2_gnn_w_comp, L2_gnn_self_loop_weight, L2_gnn_A1_w, L2_gnn_A1_b, L2_gnn_A2_w, L2_gnn_A2_b, L2_gnn_rel_emb, L3_gnn_W):
    import jax
    import jax.numpy as jnp

    def _L0_gnn_ref(x, edge_index, W1, b1, W2, b2, W3, b3):
        import jax, jax.numpy as jnp
        import numpy as np
        N_NODES = 12500
        N_EDGES = 200000
        IN_F = 32
        HID = 128

        def _gcn_norm(edge_index, n_nodes):
            loops = jnp.arange(n_nodes, dtype=edge_index.dtype)
            src = jnp.concatenate([edge_index[0], loops])
            dst = jnp.concatenate([edge_index[1], loops])
            ones = jnp.ones(src.shape[0], dtype=jnp.float32)
            deg = jax.ops.segment_sum(ones, dst, num_segments=n_nodes)
            deg_inv_sqrt = jnp.where(deg > 0, jax.lax.rsqrt(deg), 0.0)
            norm = deg_inv_sqrt[src] * deg_inv_sqrt[dst]
            return (src, dst, norm)

        def _gcn_conv(x, src, dst, norm, W, b, n_nodes):
            h = x @ W
            msg = h[src] * norm[:, None]
            out = jax.ops.segment_sum(msg, dst, num_segments=n_nodes)
            return out + b
        n = x.shape[0]
        src, dst, norm = _gcn_norm(edge_index, n)
        h = jax.nn.relu(_gcn_conv(x, src, dst, norm, W1, b1, n))
        h = jax.nn.relu(_gcn_conv(h, src, dst, norm, W2, b2, n))
        h = jax.nn.relu(_gcn_conv(h, src, dst, norm, W3, b3, n))
        return h

    def _L1_gnn_ref(x, Wq, Wk, Wv, Wo, edge_index):
        import jax, jax.numpy as jnp
        import numpy as np
        N_NODES = 12500
        N_EDGES = 400000
        D_IN = 32
        N_HEADS = 4
        D_HEAD = 8
        N = x.shape[0]
        src, dst = (edge_index[0], edge_index[1])
        q = (x @ Wq).reshape(N, N_HEADS, D_HEAD)
        k = (x @ Wk).reshape(N, N_HEADS, D_HEAD)
        v = (x @ Wv).reshape(N, N_HEADS, D_HEAD)
        inv_sqrt_d = jnp.asarray(1.0 / np.sqrt(D_HEAD), dtype=x.dtype)
        scores = jnp.einsum('ehd,ehd->eh', q[dst], k[src]) * inv_sqrt_d
        m = jax.ops.segment_max(scores, dst, num_segments=N)
        m = jnp.where(jnp.isfinite(m), m, jnp.zeros_like(m))
        e = jnp.exp(scores - m[dst])
        denom = jax.ops.segment_sum(e, dst, num_segments=N)
        msg = jax.ops.segment_sum(e[:, :, None] * v[src], dst, num_segments=N)
        attn_out = msg / jnp.maximum(denom, 1e-16)[:, :, None]
        out = attn_out.reshape(N, N_HEADS * D_HEAD) @ Wo
        return x + out

    def _L2_gnn_ref(h, weight, w_comp, self_loop_weight, A1_w, A1_b, A2_w, A2_b, rel_emb, src, dst, etype):
        import jax, jax.numpy as jnp
        import numpy as np
        N_NODES = 6250
        N_EDGES = 100000
        INP_DIM = 32
        OUT_DIM = 32
        ATTN_DIM = 32
        NUM_RELS = 86
        NUM_BASES = 16
        GAMMA = 0.0
        E = src.shape[0]
        N = h.shape[0]
        x = h[src]
        y = h[dst]
        c = w_comp[etype]
        xb = jnp.einsum('ei,bio->ebo', x, weight)
        msg = jnp.einsum('eb,ebo->eo', c, xb)
        x_hat = x @ A1_w.T + A1_b
        y_hat = y @ A2_w.T + A2_b + rel_emb[etype]
        scale = jnp.sqrt(jnp.asarray(INP_DIM, h.dtype))
        a = jnp.tanh(jax.nn.relu(jnp.sum(x_hat * y_hat, axis=-1) / scale))
        a = jnp.where(a > GAMMA, a, jnp.zeros_like(a))
        nei = jax.ops.segment_sum(a[:, None] * msg, dst, num_segments=N)
        last_e = jax.ops.segment_max(jnp.arange(E, dtype=jnp.int32), dst, num_segments=N)
        last_e = jnp.clip(last_e, 0, E - 1)
        curr = h[src[last_e]] @ self_loop_weight
        in_deg = jax.ops.segment_sum(jnp.ones((E,), h.dtype), dst, num_segments=N)
        h_new = jnp.where((in_deg > 0)[:, None], nei + curr, jnp.zeros_like(nei))
        return jax.nn.relu(h_new)

    def _L3_gnn_ref(node_irreps, edge_index, sh0, sh1, sh2, W):
        import jax, jax.numpy as jnp
        import numpy as np
        import math
        M = 8
        COMBOS = [(0, 0, 0), (0, 1, 1), (1, 0, 1), (1, 1, 0), (1, 1, 1), (2, 1, 1)]

        def _cg_coeff(j1, m1, j2, m2, j3, m3):
            if m3 != m1 + m2:
                return 0.0
            f = math.factorial
            vmin = max(0, j2 - j3 - m1, j1 + m2 - j3)
            vmax = min(j1 + j2 - j3, j1 - m1, j2 + m2)
            pref = (2 * j3 + 1) * f(j3 + j1 - j2) * f(j3 - j1 + j2) * f(j1 + j2 - j3) / f(j1 + j2 + j3 + 1)
            pref *= f(j3 + m3) * f(j3 - m3) * f(j1 - m1) * f(j1 + m1) * f(j2 - m2) * f(j2 + m2)
            s = 0.0
            for v in range(vmin, vmax + 1):
                s += (-1) ** v / (f(v) * f(j1 + j2 - j3 - v) * f(j1 - m1 - v) * f(j2 + m2 - v) * f(j3 - j2 + m1 + v) * f(j3 - j1 - m2 + v))
            return math.sqrt(pref) * s

        def _su2_cg(l1, l2, l3):
            C = np.zeros((2 * l1 + 1, 2 * l2 + 1, 2 * l3 + 1), dtype=np.complex128)
            for m1 in range(-l1, l1 + 1):
                for m2 in range(-l2, l2 + 1):
                    m3 = m1 + m2
                    if -l3 <= m3 <= l3:
                        C[m1 + l1, m2 + l2, m3 + l3] = _cg_coeff(l1, m1, l2, m2, l3, m3)
            return C

        def _qmat(l):
            q = np.zeros((2 * l + 1, 2 * l + 1), dtype=np.complex128)
            for m in range(-l, 0):
                q[l + m, l + abs(m)] = 1 / np.sqrt(2)
                q[l + m, l - abs(m)] = -1j / np.sqrt(2)
            q[l, l] = 1.0
            for m in range(1, l + 1):
                q[l + m, l + abs(m)] = (-1) ** m / np.sqrt(2)
                q[l + m, l - abs(m)] = 1j * (-1) ** m / np.sqrt(2)
            return (-1j) ** l * q

        def _so3_cg(l1, l2, l3):
            C = np.einsum('ij,kl,mn,ikn->jlm', _qmat(l1), _qmat(l2), np.conj(_qmat(l3)).T, _su2_cg(l1, l2, l3))
            assert np.abs(C.imag).max() < 1e-06
            C = C.real
            return C / np.linalg.norm(C)
        CG = {c: jnp.asarray(_so3_cg(*c), dtype=jnp.float32) for c in COMBOS}
        N, E = (node_irreps.shape[0], edge_index.shape[1])
        src = node_irreps[edge_index[0]]
        feats = {0: src[:, :M][:, :, None], 1: src[:, M:].reshape(E, M, 3)}
        sh = {0: sh0, 1: sh1, 2: sh2}
        msg = {0: jnp.zeros((E, M, 1), node_irreps.dtype), 1: jnp.zeros((E, M, 3), node_irreps.dtype)}
        for idx, (le, ln, lo) in enumerate(COMBOS):
            base = jnp.einsum('ijk,ei,emj->emk', CG[le, ln, lo], sh[le], feats[ln])
            msg[lo] = msg[lo] + jnp.einsum('io,eik->eok', W[idx], base)
        tgt = edge_index[1]
        agg0 = jax.ops.segment_sum(msg[0].reshape(E, M), tgt, num_segments=N)
        agg1 = jax.ops.segment_sum(msg[1].reshape(E, 3 * M), tgt, num_segments=N)
        return jnp.concatenate([agg0, agg1], axis=1)
    edge_index = jnp.stack([src, dst])
    h = jnp.maximum(_layernorm(x, axis=-1), 0.0)
    x = x + _L0_gnn_ref(h, edge_index, L0_gnn_W1, L0_gnn_b1, L0_gnn_W2, L0_gnn_b2, L0_gnn_W3, L0_gnn_b3)
    h = jnp.maximum(_layernorm(x, axis=-1), 0.0)
    x = x + _L1_gnn_ref(h, L1_gnn_Wq, L1_gnn_Wk, L1_gnn_Wv, L1_gnn_Wo, edge_index)
    h = jnp.maximum(_layernorm(x, axis=-1), 0.0)
    x = x + _L2_gnn_ref(h, L2_gnn_weight, L2_gnn_w_comp, L2_gnn_self_loop_weight, L2_gnn_A1_w, L2_gnn_A1_b, L2_gnn_A2_w, L2_gnn_A2_b, L2_gnn_rel_emb, src, dst, edge_type_86)
    h = jnp.maximum(_layernorm(x, axis=-1), 0.0)
    x = x + _L3_gnn_ref(h, edge_index, edge_weight1, edge_attr_3, edge_attr_5, L3_gnn_W)
    return x

_drawn_inputs = setup_inputs


def setup_inputs(seed=0):
    import zlib

    import numpy as np

    out = dict(_drawn_inputs(seed))
    spreads = {'L0_gnn_b1': (0.0, 0.1), 'L0_gnn_b2': (0.0, 0.1), 'L0_gnn_b3': (0.0, 0.1)}
    factors = {}
    for name, (base, spread) in spreads.items():
        noise = np.random.default_rng([zlib.crc32(name.encode()), seed]).standard_normal(out[name].shape)
        drawn = base * np.exp(spread * noise) if base else spread * noise
        out[name] = jnp.asarray(drawn.astype(out[name].dtype))
    for name, factor in factors.items():
        out[name] = (out[name] * factor).astype(out[name].dtype)
    return out
```

```python
import math
from contextlib import ExitStack

import numpy as np
import concourse.bass as bass
from concourse import mybir

F32 = mybir.dt.float32
I32 = mybir.dt.int32
U32 = mybir.dt.uint32
ALU = mybir.AluOpType
ACT = mybir.ActivationFunctionType
AX_X = mybir.AxisListType.X

P = 128
N_NODES = 12500
N_EDGES = 200000
D = 32
HID = 128
HEADS, DHEAD = 4, 8
N_REL, N_BASES = 86, 16
J = -(-N_NODES // P)
JP = 104
T = -(-N_EDGES // P)
REC = 16
R_SRC, R_DST, R_NEXT, R_TYPE, R_SH, R_REL, R_LAST = 0, 1, 2, 3, 4, 13, 14
N_SH = 9
G = 8
R = 4
BLOCKS = -(-(T + J - 1) // P)
S = BLOCKS * P
ITERS = S // (G * R)
GROUPS = S // G
BIG = 1e30
LAST_TILE_ROWS = N_NODES - (J - 1) * P
PAD_DST = J * P - 1
DMA = 16


def _node_rows(table, j0, j1):
    return table[j0 * P:j1 * P, :].rearrange("(j p) f -> p j f", p=P)


class Chain:

    def __init__(self, engine, semaphore):
        self.engine, self.semaphore, self.value = engine, semaphore, 0

    def link(self, instruction):
        self.value += 1
        instruction.then_inc(self.semaphore, 1)
        self.engine.wait_ge(self.semaphore, self.value)


def _scope(nc, ctx, name):
    def sb(n, shape, dt=F32):
        return ctx.enter_context(nc.sbuf_tensor(f"{name}_{n}", shape, dt))

    def psum(n, shape, dt=F32):
        return ctx.enter_context(nc.psum_tensor(f"{name}_{n}", shape, dt))

    held = []

    def clear():
        nc.clear_and_free_semaphores(held)
        nc.all_engine_barrier()

    def sem(n):
        if not held:
            ctx.callback(clear)
        held.append(nc.alloc_semaphore(f"{name}_{n}"))
        return held[-1]

    return sb, psum, sem


def constants(nc, k):
    with ExitStack() as ctx:
        sb, _, sem = _scope(nc, ctx, "const")
        row = sb("row", [P, 1])
        made = sem("made")
        with nc.Block() as block:
            @block.gpsimd
            def _(pool):
                nc.gpsimd.iota(k["iota"][:], pattern=[[1, P]], base=0, channel_multiplier=0,
                               allow_small_or_imprecise_dtypes=True).then_inc(made, 1)
                nc.gpsimd.iota(row[:], pattern=[[0, 1]], base=0, channel_multiplier=1,
                               allow_small_or_imprecise_dtypes=True).then_inc(made, 1)
                nc.gpsimd.iota(k["step_no"][:], pattern=[[P, BLOCKS]], base=0, channel_multiplier=1,
                               allow_small_or_imprecise_dtypes=True).then_inc(made, 1)

            @block.vector
            def _(dve):
                nc.vector.memset(k["ones"][:], 1.0)
                dve.wait_ge(made, 3)
                nc.vector.tensor_scalar(k["ident"][:], k["iota"][:], row[:, 0:1], None, ALU.is_equal)


def edge_records(nc, io, dram):
    C = -(-T * P // P)
    LAST = N_EDGES - (P - 1) * C
    CH = C // 3
    assert C == T and CH * 3 == C
    with ExitStack() as ctx:
        sb, _, sem = _scope(nc, ctx, "rec")
        fields = [("src", I32, 1, 0, 0), ("dst", I32, 1, 0, PAD_DST), ("next", I32, 1, 1, PAD_DST),
                  ("type", I32, 1, 0, 0), ("sh0", F32, 1, 0, 0), ("sh1", F32, 3, 0, 0), ("sh2", F32, 5, 0, 0)]
        source = {"src": io["src"], "dst": io["dst"], "next": io["dst"], "type": io["edge_type_86"],
                  "sh0": io["edge_weight1"], "sh1": io["edge_attr_3"], "sh2": io["edge_attr_5"]}
        held = {n: sb(n, [P, C * w], dt) for n, dt, w, _, _ in fields}
        rec = [sb(f"rec{i}", [P, CH, REC]) for i in range(2)]
        padded, loaded = sem("padded"), sem("loaded")
        joined_dve, joined_act = sem("joined_dve"), sem("joined_act")
        stored = [sem(f"stored{i}") for i in range(2)]
        out = dram["rec"].rearrange("t (e f) -> (t e f)", f=REC).rearrange("(p w) -> p w", p=P)
        with nc.Block() as block:
            @block.sync
            def _(sp):
                sp.wait_ge(padded, len(fields))
                n = 0
                for name, _, w, shift, _ in fields:
                    flat = source[name]
                    if len(flat.shape) == 2:
                        flat = flat.rearrange("e w -> (e w)")
                    for p0, p1 in ((0, 112), (112, P - 1)):
                        a, b = (p0 * C + shift) * w, (p1 * C + shift) * w
                        sp.dma_start(held[name][p0:p1, :], flat[a:b].rearrange("(p c) -> p c", p=p1 - p0)).then_inc(loaded, DMA)
                    a = ((P - 1) * C + shift) * w
                    sp.dma_start(held[name][P - 1:P, 0:(LAST - shift) * w],
                                 flat[a:N_EDGES * w].rearrange("(p c) -> p c", p=1)).then_inc(loaded, DMA)
                for i in range(3):
                    sp.wait_ge(joined_dve, i + 1)
                    sp.wait_ge(joined_act, i + 1)
                    sp.dma_start(out[:, i * CH * REC:(i + 1) * CH * REC],
                                 rec[i % 2][:].rearrange("p c f -> p (c f)")).then_inc(stored[i % 2], DMA)
                sp.wait_ge(stored[0], 2 * DMA)
                sp.wait_ge(stored[1], DMA)

            @block.vector
            def _(dve):
                for name, _, w, shift, value in fields:
                    nc.vector.memset(held[name][:, (LAST - shift) * w:C * w], value).then_inc(padded, 1)
                for i in range(2):
                    nc.vector.memset(rec[i][:, :, R_SH + N_SH:REC], 0.0)
                dve.wait_ge(loaded, 3 * len(fields) * DMA)
                for i in range(3):
                    if i >= 2:
                        dve.wait_ge(stored[i % 2], DMA)
                    for f, name in ((R_SRC, "src"), (R_DST, "dst"), (R_NEXT, "next"), (R_TYPE, "type"), (R_SH, "sh0")):
                        last = nc.vector.tensor_copy(rec[i % 2][:, :, f], held[name][:, i * CH:(i + 1) * CH])
                    last.then_inc(joined_dve, 1)

            @block.scalar
            def _(act):
                act.wait_ge(loaded, 3 * len(fields) * DMA)
                for i in range(3):
                    if i >= 2:
                        act.wait_ge(stored[i % 2], DMA)
                    nc.scalar.copy(rec[i % 2][:, :, R_SH + 1:R_SH + 4],
                                   held["sh1"][:, 3 * i * CH:3 * (i + 1) * CH].rearrange("p (c w) -> p c w", w=3))
                    nc.scalar.copy(rec[i % 2][:, :, R_SH + 4:R_SH + 9],
                                   held["sh2"][:, 5 * i * CH:5 * (i + 1) * CH].rearrange("p (c w) -> p c w", w=5)).then_inc(joined_act, 1)


def merge_path(nc, k, dram):
    CUT = [(c, min(c + 512, T)) for c in range(0, T, 512)]
    with ExitStack() as ctx:
        sb, psum, sem = _scope(nc, ctx, "path")
        last_dst = sb("last_dst", [1, T])
        node_tile = sb("node_tile", [1, T], I32)
        done_at = sb("done_at", [1, T])
        tile_no = sb("tile_no", [1, T])
        done_all = sb("done_all", [P, T])
        before = sb("before", [P, T])
        j_row = sb("j_row", [1, S + 8])
        inc_row = sb("inc_row", [1, S + 8])
        keep_row = sb("keep_row", [1, S])
        weight = sb("weight", [1, G])
        parts = sb("parts", [1, GROUPS, G])
        word = sb("word", [1, GROUPS])
        spread = psum("spread", [P, 4, 512])
        loaded, numbered, ready, shown, chain_sem, j_out, j_in, keep_shown = (
            sem(n) for n in ("loaded", "numbered", "ready", "shown", "chain", "j_out", "j_in", "keep_shown"))
        with nc.Block() as block:
            @block.sync
            def _(sp):
                with nc.allow_non_contiguous_dma("one word of each edge tile"):
                    sp.dma_start(last_dst[:], dram["rec"][:, (P - 1) * REC + R_DST:(P - 1) * REC + R_DST + 1]
                                 .rearrange("t o -> o t")).then_inc(loaded, DMA)
                    sp.wait_ge(ready, 2)
                    sp.dma_start(dram["j"].rearrange("o (b p) -> p (o b)", p=P), k["j_of"][:]).then_inc(j_out, DMA)
                    sp.wait_ge(j_out, DMA)
                    sp.dma_start(j_row[:, 0:S], dram["j"]).then_inc(j_in, DMA)

            @block.gpsimd
            def _(pool):
                nc.gpsimd.iota(tile_no[:], pattern=[[1, T]], base=0, channel_multiplier=0,
                               allow_small_or_imprecise_dtypes=True).then_inc(numbered, 1)

            @block.vector
            def _(dve):
                chain = Chain(dve, chain_sem)
                dve.wait_ge(loaded, DMA)
                dve.wait_ge(numbered, 1)
                chain.link(nc.vector.tensor_copy(node_tile[:], last_dst[:]))
                chain.link(nc.vector.tensor_single_scalar(node_tile[:], node_tile[:], 7, op=ALU.arith_shift_right))
                nc.vector.tensor_tensor(done_at[:], node_tile[:], tile_no[:], ALU.add).then_inc(ready, 1)
                dve.wait_ge(shown, 1)
                for n, (a, b) in enumerate(CUT):
                    last = nc.vector.tensor_copy(done_all[:, a:b], spread[:, n, 0:b - a])
                chain.link(last)
                for b in range(BLOCKS):
                    chain.link(nc.vector.tensor_scalar(before[:], done_all[:], k["step_no"][:, b:b + 1], 0.0,
                                                       ALU.is_lt, ALU.add, accum_out=k["t_of"][:, b:b + 1]))
                chain.link(nc.vector.tensor_single_scalar(k["t_of"][:], k["t_of"][:], float(T - 1), op=ALU.min))
                nc.vector.tensor_copy(k["t_index"][:], k["t_of"][:])
                nc.vector.tensor_tensor(k["j_of"][:], k["step_no"][:], k["t_of"][:], ALU.subtract).then_inc(ready, 1)
                for g in range(G):
                    nc.vector.memset(weight[:, g:g + 1], float(2 ** (7 + g)))
                chain.link(nc.vector.memset(j_row[:, S:S + 8], float(S - T + 1)))
                dve.wait_ge(j_in, DMA)
                dve.wait_ge(ready, 2)
                chain.link(nc.vector.tensor_tensor(inc_row[:, 0:S], j_row[:, 1:S + 1], j_row[:, 0:S], ALU.subtract))
                nc.vector.memset(keep_row[:, 0:1], 0.0)
                nc.vector.tensor_scalar(keep_row[:, 1:S], inc_row[:, 0:S - 1], -1.0, 1.0, ALU.mult, ALU.add).then_inc(ready, 1)
                chain.link(nc.vector.tensor_tensor(parts[:], inc_row[:, 0:S].rearrange("o (g k) -> o g k", k=G),
                                                   weight[:].unsqueeze(1).to_broadcast([1, GROUPS, G]), ALU.mult))
                chain.link(nc.vector.tensor_reduce(word[:], parts[:], axis=AX_X, op=ALU.add))
                chain.link(nc.vector.tensor_tensor(word[:], word[:], j_row[:, 0:S].rearrange("o (g k) -> o g k", k=G)[:, :, 0], ALU.add))
                nc.vector.tensor_copy(k["words"][:], word[:])
                dve.wait_ge(keep_shown, 1)
                for n in range(4):
                    w = S // 4
                    nc.vector.tensor_copy(k["keep"][:, n * w:(n + 1) * w], spread[:, n, 0:w])

            @block.tensor
            def _(pe):
                pe.wait_ge(ready, 1)
                for n, (a, b) in enumerate(CUT):
                    last = nc.tensor.matmul(spread[:, n, 0:b - a], k["ones"][0:1, :], done_at[:, a:b], start=True, stop=True)
                last.then_inc(shown, 1)
                pe.wait_ge(ready, 3)
                for n in range(4):
                    w = S // 4
                    last = nc.tensor.matmul(spread[:, n, 0:w], k["ones"][0:1, :], keep_row[:, n * w:(n + 1) * w], start=True, stop=True)
                last.then_inc(keep_shown, 1)


def step_tables(nc, k, dram):
    with ExitStack() as ctx:
        sb, psum, sem = _scope(nc, ctx, "table")
        index = sb("index", [P, 1], U32)
        tile = sb("tile", [P, P, REC])
        flag = sb("flag", [P, P])
        j128 = sb("j128", [P, BLOCKS])
        sh = sb("sh", [P, P, N_SH])
        turned = psum("turned", [P, 4, P])
        turned_sh = psum("turned_sh", [P, 12, P])
        released = sem("released")
        indexed, gathered, filled, flipped, taken_dve, taken_act, chain_sem, sh_out, t_out = (
            sem(n) for n in ("indexed", "gathered", "filled", "flipped", "taken_dve", "taken_act", "chain", "sh_out", "t_out"))
        with nc.Block() as block:
            @block.gpsimd
            def _(pool):
                with pool.Fori(0, BLOCKS) as b:
                    pool.wait_ge(indexed, b + 1)
                    pool.wait_ge(flipped, b)
                    pool.wait_ge(t_out, b * 2 * DMA)
                    pool.sem_inc(released, 1)
                    nc.gpsimd.indirect_dma_start(
                        out=tile[:].rearrange("p e f -> p (e f)"), out_offset=None, in_=dram["rec"],
                        in_offset=bass.IndirectOffsetOnAxis(ap=index[:, 0:1], axis=0)).then_inc(gathered, DMA)

            @block.vector
            def _(dve):
                nc.vector.memset(k["stat"][:, :, 0], 1.0)
                nc.vector.memset(k["drel"][:, S:S + G], -1.0)
                nc.vector.tensor_single_scalar(j128[:], k["j_of"][:], float(P), op=ALU.mult).then_inc(chain_sem, 1)
                dve.wait_ge(chain_sem, 1)
                with dve.Fori(0, BLOCKS) as b:
                    dve.wait_ge(gathered, b * DMA)
                    nc.vector.tensor_copy(index[:], k["t_index"][:, bass.ds(b, 1)]).then_inc(indexed, 1)
                    dve.wait_ge(gathered, (b + 1) * DMA)
                    nc.vector.tensor_scalar(tile[:, :, R_REL], tile[:, :, R_DST], j128[:, bass.ds(b, 1)], None, ALU.subtract)
                    nc.vector.tensor_tensor(flag[:], tile[:, :, R_DST], tile[:, :, R_NEXT], ALU.not_equal).then_inc(chain_sem, 1)
                    dve.wait_ge(chain_sem, b + 2)
                    nc.vector.scalar_tensor_tensor(out=tile[:, :, R_LAST], in0=tile[:, :, R_SRC], scalar=1.0, in1=flag[:],
                                                   op0=ALU.add, op1=ALU.mult).then_inc(filled, 1)
                    dve.wait_ge(flipped, b + 1)
                    at = bass.ds(b * P, P)
                    nc.vector.tensor_copy(k["src"][:, at], turned[:, 0, :])
                    nc.vector.tensor_copy(k["drel"][:, at], turned[:, 1, :])
                    nc.vector.tensor_copy(k["type"][:, at], turned[:, 2, :])
                    nc.vector.tensor_copy(k["stat"][:, at, 1], turned[:, 3, :]).then_inc(taken_dve, 1)

            @block.tensor
            def _(pe):
                with pe.Fori(0, BLOCKS) as b:
                    pe.wait_ge(filled, b + 1)
                    pe.wait_ge(taken_dve, b)
                    pe.wait_ge(taken_act, b)
                    for n, f in enumerate((R_SRC, R_REL, R_TYPE, R_LAST)):
                        nc.tensor.transpose(turned[:, n, :], tile[:, :, f], k["ident"][:])
                    for f in range(N_SH):
                        last = nc.tensor.transpose(turned_sh[:, f, :], tile[:, :, R_SH + f], k["ident"][:])
                    last.then_inc(flipped, 1)

            @block.scalar
            def _(act):
                with act.Fori(0, BLOCKS) as b:
                    act.wait_ge(flipped, b + 1)
                    act.wait_ge(sh_out, b * DMA)
                    for f0, f1 in ((0, 4), (4, 8), (8, 9)):
                        last = nc.scalar.copy(sh[:, :, f0:f1].rearrange("p s f -> p f s"), turned_sh[:, f0:f1, :])
                    last.then_inc(taken_act, 1)

            @block.sync
            def _(sp):
                with sp.Fori(0, BLOCKS) as b, nc.allow_non_contiguous_dma("one field of the records"):
                    sp.wait_ge(filled, b + 1)
                    sp.dma_start(dram["dst_t"][:, bass.ds(b * P, P)], tile[:, :, R_DST]).then_inc(t_out, DMA)
                    sp.dma_start(dram["drel_t"][:, bass.ds(b * P, P)], tile[:, :, R_REL]).then_inc(t_out, DMA)
                    sp.wait_ge(taken_act, b + 1)
                    sp.dma_start(dram["sh"][:, bass.ds(b * P * N_SH, P * N_SH)], sh[:].rearrange("p s f -> p (s f)")).then_inc(sh_out, DMA)
                sp.wait_ge(sh_out, BLOCKS * DMA)
                sp.wait_ge(t_out, 2 * BLOCKS * DMA)


def node_statistics(nc, k):
    with ExitStack() as ctx:
        sb, psum, sem = _scope(nc, ctx, "stat")
        onehot = [sb(f"onehot{h}", [P, G, P]) for h in range(2)]
        per_step = sb("per_step", [P, 2, S])
        of_tile = sb("of_tile", [P, BLOCKS, JP])
        by_step = sb("by_step", [P, 2, 4, P])
        sums = psum("sums", [P, 2, 512])
        flipped_ps = psum("flipped_ps", [P, 2, 4, P])
        total = psum("total", [P, 2, 512])
        made, summed, taken, selected, flipped, copied, totalled, chain_sem = (
            sem(n) for n in ("made", "summed", "taken", "selected", "flipped", "copied", "totalled", "chain"))
        CUT = [(b, min(b + 4, BLOCKS)) for b in range(0, BLOCKS, 4)]
        with nc.Block() as block:
            @block.vector
            def _(dve):
                chain = Chain(dve, chain_sem)
                for b in range(BLOCKS):
                    nc.vector.tensor_scalar(of_tile[:, b, :], k["iota"][:, 0:JP], k["j_of"][:, b:b + 1], None,
                                            ALU.is_equal).then_inc(selected, 1)
                with dve.Fori(0, GROUPS // 2) as i:
                    for h in range(2):
                        dve.wait_ge(summed, 2 * i)
                        _one_hot(nc, k, onehot[h], (i * 2 + h) * G).then_inc(made, 1)
                dve.wait_ge(totalled, 1)
                chain.link(nc.vector.tensor_single_scalar(k["degree"][:], total[:, 0, 0:JP], 1.0, op=ALU.mult))
                chain.link(nc.vector.tensor_scalar(k["last"][:], total[:, 1, 0:JP], -1.0, 0.0, ALU.add, ALU.max))
                nc.vector.tensor_copy(k["last_index"][:], k["last"][:])
                chain.link(nc.vector.tensor_single_scalar(k["dinv"][:], k["degree"][:], 1.0, op=ALU.add))
                chain.link(nc.vector.reciprocal(k["dinv"][:], k["dinv"][:]))

            @block.tensor
            def _(pe):
                with pe.Fori(0, GROUPS // 2) as i:
                    for h in range(2):
                        pe.wait_ge(made, 2 * i + h + 1)
                        pe.wait_ge(taken, i * 2)
                        for g in range(G):
                            last = nc.tensor.matmul(sums[:, h, 2 * g:2 * g + 2], onehot[h][:, g, :],
                                                    k["stat"][:, bass.ds((i * 2 + h) * G + g, 1), :].rearrange("p s w -> p (s w)"),
                                                    start=True, stop=True)
                        last.then_inc(summed, 1)
                pe.wait_ge(taken, GROUPS)
                pe.wait_ge(selected, BLOCKS)
                for n, (a, b) in enumerate(CUT):
                    if n >= 2:
                        pe.wait_ge(copied, n - 1)
                    for w in range(2):
                        for q in range(a, b):
                            last = nc.tensor.transpose(flipped_ps[:, w, q - a, :], per_step[:, w, q * P:(q + 1) * P], k["ident"][:])
                    last.then_inc(flipped, 1)
                    pe.wait_ge(copied, n + 1)
                    for w in range(2):
                        for q in range(a, b):
                            last = nc.tensor.matmul(total[:, w, 0:JP], by_step[:, w, q - a, :], of_tile[:, q, :],
                                                    start=(q == 0), stop=(q == BLOCKS - 1))
                last.then_inc(totalled, 1)

            @block.scalar
            def _(act):
                with act.Fori(0, GROUPS // 2) as i:
                    for h in range(2):
                        act.wait_ge(summed, 2 * i + h + 1)
                        nc.scalar.copy(per_step[:, :, bass.ds((i * 2 + h) * G, G)],
                                       sums[:, h, 0:2 * G].rearrange("p (s w) -> p w s", w=2)).then_inc(taken, 1)
                for n, (a, b) in enumerate(CUT):
                    act.wait_ge(flipped, n + 1)
                    nc.scalar.copy(by_step[:, :, 0:b - a, :], flipped_ps[:, :, 0:b - a, :]).then_inc(copied, 1)
        with nc.Block() as block:
            @block.scalar
            def _(act):
                nc.scalar.activation(k["dinv"][:], k["dinv"][:], ACT.Sqrt)


def _one_hot(nc, k, out, first):
    return nc.vector.tensor_tensor(out[:], k["iota"][:].unsqueeze(1).to_broadcast([P, G, P]),
                                   k["drel"][:, bass.ds(first, G)].unsqueeze(2).to_broadcast([P, G, P]), ALU.is_equal)


def _tile_registers(nc, engine, k, group):
    word = engine.value_load(k["words"][0:1, bass.ds(group, 1)], min_val=0, max_val=(1 << (7 + G)) - 1)
    tiles = [engine.snap(nc.s_assert_within(word & 127, 0, JP - 1, skip_runtime_bounds_check_because="a node tile"))]
    for g in range(1, G):
        tiles.append(engine.snap(nc.s_assert_within(tiles[-1] + ((word >> (6 + g)) & 1), 0, JP - 1,
                                                    skip_runtime_bounds_check_because="a node tile")))
    return tiles, [(word >> (7 + g)) & 1 for g in range(G)]


def _save_tiles(nc, sp, k, sums, totals, acc_step, checked, saved, width):
    with sp.Fori(0, ITERS) as i:
        for q in range(R):
            tiles, is_last = _tile_registers(nc, sp, k, i * R + q)
            sp.wait_ge(acc_step, (i * R + q + 2) * G)
            sp.sem_inc(checked, 1)
            for g in range(G):
                sp.dma_start(totals[:, bass.ds(tiles[g] * width, width)], sums[:, q, g, :],
                             cond=is_last[g]).then_inc(saved[q], DMA)
    for q in range(R):
        sp.wait_ge(saved[q], ITERS * G * DMA)


def _stage_indices(nc, act, k, staged, gathered, indexed):
    with act.Fori(0, ITERS) as i:
        for q in range(R):
            act.wait_ge(gathered[q], i * G * DMA)
            nc.scalar.copy(staged[:, q, :], k["src"][:, bass.ds((i * R + q) * G, G)]).then_inc(indexed, 1)


def _gather_rows(nc, pool, table, staged, ring, indexed, free, released, gathered):
    with pool.Fori(0, ITERS) as i:
        for q in range(R):
            pool.wait_ge(indexed, i * R + q + 1)
            for s in free:
                pool.wait_ge(s[q], i)
            pool.sem_inc(released, 1)
            for g in range(G):
                nc.gpsimd.indirect_dma_start(
                    out=ring[:, q, g, :], out_offset=None, in_=table,
                    in_offset=bass.IndirectOffsetOnAxis(ap=staged[:, q, g:g + 1], axis=0)).then_inc(gathered[q], DMA)


def _clear_sums(nc, sums, acc_step):
    nc.vector.memset(sums[:, R - 1, G - 1, :], 0.0).then_inc(acc_step, G)


def _running_sums(nc, dve, k, i, q, sums, partial, acc_step, saved):
    dve.wait_ge(saved[q], i * G * DMA)
    for g in range(G):
        before = sums[:, q, g - 1, :] if g else sums[:, (q - 1) % R, G - 1, :]
        dve.wait_ge(acc_step, (i * R + q + 1) * G + g)
        nc.vector.scalar_tensor_tensor(
            out=sums[:, q, g, :], in0=before, scalar=k["keep"][:, bass.ds((i * R + q) * G + g, 1)],
            in1=partial(g), op0=ALU.mult, op1=ALU.add).then_inc(acc_step, 1)


def sum_pass(nc, k, name, table, totals, width):
    with ExitStack() as ctx:
        sb, psum, sem = _scope(nc, ctx, name)
        staged = sb("staged", [P, R, G], U32)
        ring = sb("ring", [P, R, G, width])
        onehot = [sb(f"onehot{h}", [P, G, P]) for h in range(2)]
        sums = sb("sums", [P, R, G, width])
        partial = psum("partial", [P, 2, max(512, G * width)])
        indexed, made, acc_step, released = sem("indexed"), sem("made"), sem("acc_step"), sem("released")
        gathered = [sem(f"gathered{q}") for q in range(R)]
        summed = [sem(f"summed{q}") for q in range(R)]
        saved = [sem(f"saved{q}") for q in range(R)]
        checked = sem("checked")
        with nc.Block() as block:
            @block.scalar
            def _(act):
                _stage_indices(nc, act, k, staged, gathered, indexed)

            @block.gpsimd
            def _(pool):
                _gather_rows(nc, pool, table, staged, ring, indexed, [summed], released, gathered)

            @block.vector
            def _(dve):
                _clear_sums(nc, sums, acc_step)
                _one_hot(nc, k, onehot[0], 0).then_inc(made, 1)
                with dve.Fori(0, ITERS) as i:
                    for q in range(R):
                        dve.wait_ge(summed[(q - 1) % R], i + (q >= 1))
                        _one_hot(nc, k, onehot[(q + 1) % 2], (i * R + q + 1) * G).then_inc(made, 1)
                        dve.wait_ge(summed[q], i + 1)
                        _running_sums(nc, dve, k, i, q, sums,
                                      lambda g: partial[:, q % 2, g * width:(g + 1) * width],
                                      acc_step, saved)

            @block.tensor
            def _(pe):
                with pe.Fori(0, ITERS) as i:
                    for q in range(R):
                        pe.wait_ge(made, i * R + q + 1)
                        pe.wait_ge(gathered[q], (i + 1) * G * DMA)
                        pe.wait_ge(acc_step, (i * R + q) * G)
                        for g in range(G):
                            last = nc.tensor.matmul(partial[:, q % 2, g * width:(g + 1) * width],
                                                    onehot[q % 2][:, g, :], ring[:, q, g, :], start=True, stop=True)
                        last.then_inc(summed[q], 1)

            @block.sync
            def _(sp):
                _save_tiles(nc, sp, k, sums, totals, acc_step, checked, saved, width)


def load_x(nc, io, k):
    with ExitStack() as ctx:
        _, _, sem = _scope(nc, ctx, "x")
        cleared, loaded = sem("cleared"), sem("loaded")
        with nc.Block() as block:
            @block.vector
            def _(dve):
                nc.vector.memset(k["x"][:], 0.0).then_inc(cleared, 1)

            @block.sync
            def _(sp):
                sp.wait_ge(cleared, 1)
                sp.dma_start(k["x"][:, 0:J - 1, :], _node_rows(io["x"], 0, J - 1)).then_inc(loaded, DMA)
                sp.dma_start(k["x"][0:LAST_TILE_ROWS, J - 1, :], io["x"][(J - 1) * P:N_NODES, :]).then_inc(loaded, DMA)
                sp.wait_ge(loaded, 2 * DMA)


def _spread(a, n):
    return a.unsqueeze(2).to_broadcast([P, JP, n])


def norm_relu(nc, k, name, h):
    x = k["x"]
    with ExitStack() as ctx:
        sb, _, sem = _scope(nc, ctx, name)
        centered = sb("centered", [P, JP, D])
        mean = sb("mean", [P, JP])
        var = sb("var", [P, JP])
        rooted, chain_sem, summed = sem("rooted"), sem("chain"), sem("summed")
        with nc.Block() as block:
            @block.vector
            def _(dve):
                chain = Chain(dve, chain_sem)
                chain.link(nc.vector.tensor_reduce(mean[:], x[:], axis=AX_X, op=ALU.add))
                chain.link(nc.vector.tensor_single_scalar(mean[:], mean[:], 1.0 / D, op=ALU.mult))
                chain.link(nc.vector.tensor_tensor(centered[:], x[:], _spread(mean[:], D), ALU.subtract))
                chain.link(nc.vector.tensor_tensor(h[:], centered[:], centered[:], ALU.mult))
                chain.link(nc.vector.tensor_reduce(var[:], h[:], axis=AX_X, op=ALU.add))
                nc.vector.tensor_scalar(var[:], var[:], 1.0 / D, 1e-5, ALU.mult, ALU.add).then_inc(summed, 1)
                dve.wait_ge(rooted, 1)
                chain.link(nc.vector.reciprocal(var[:], var[:]))
                chain.link(nc.vector.tensor_tensor(centered[:], centered[:], _spread(var[:], D), ALU.mult))
                nc.vector.tensor_single_scalar(h[:], centered[:], 0.0, op=ALU.max)

            @block.scalar
            def _(act):
                act.wait_ge(summed, 1)
                nc.scalar.activation(var[:], var[:], ACT.Sqrt).then_inc(rooted, 1)


def store_table(nc, name, table, a, width):
    with ExitStack() as ctx:
        _, _, sem = _scope(nc, ctx, name)
        stored = sem("stored")
        with nc.Block() as block:
            @block.sync
            def _(sp):
                sp.dma_start(_node_rows(table, 0, J), a[:, 0:J, 0:width]).then_inc(stored, DMA)
                sp.wait_ge(stored, DMA)


def load_totals(nc, name, totals, a, width):
    with ExitStack() as ctx:
        _, _, sem = _scope(nc, ctx, name)
        loaded, cleared = sem("loaded"), sem("cleared")
        with nc.Block() as block:
            @block.gpsimd
            def _(pool):
                nc.gpsimd.memset(a[:, J:JP, :], 0.0)

            @block.sync
            def _(sp):
                sp.dma_start(a[:, 0:J, :], totals[:, 0:J * width].rearrange("p (j f) -> p j f", f=width)).then_inc(loaded, DMA)
                sp.wait_ge(loaded, DMA)


def node_linear(nc, k, name, source, n, parts, weights, out, load=None):
    width = parts * P
    fo = weights.shape[2]
    assert n % 2 == 0
    from_dram = load
    with ExitStack() as ctx:
        sb, psum, sem = _scope(nc, ctx, name)
        chunk = [sb(f"chunk{h}", [P, width]) for h in range(2)]
        turned = [sb(f"turned{h}", [P, parts, P]) for h in range(2)]
        flipped_ps = psum("flipped_ps", [P, 2, 4, P])
        product = psum("product", [P, 2, 512])
        staged = [sem(f"staged{h}") for h in range(2)]
        flipped = [sem(f"flipped{h}") for h in range(2)]
        copied = [sem(f"copied{h}") for h in range(2)]
        multiplied = [sem(f"multiplied{h}") for h in range(2)]
        taken = [sem(f"taken{h}") for h in range(2)]
        per_stage = DMA if from_dram else 1
        with nc.Block() as block:
            if from_dram:
                @block.sync
                def _(sp):
                    with sp.Fori(0, n // 2) as i:
                        for h in range(2):
                            sp.wait_ge(flipped[h], i)
                            sp.dma_start(chunk[h][:], source[:, bass.ds((i * 2 + h) * width, width)]).then_inc(staged[h], DMA)
            else:
                @block.gpsimd
                def _(pool):
                    with pool.Fori(0, n // 2) as i:
                        for h in range(2):
                            pool.wait_ge(flipped[h], i)
                            nc.gpsimd.tensor_copy(chunk[h][:], source[:, bass.ds((i * 2 + h) * width, width)]).then_inc(staged[h], 1)

            @block.tensor
            def _(pe):
                with pe.Fori(0, n // 2) as i:
                    for h in range(2):
                        pe.wait_ge(staged[h], (i + 1) * per_stage)
                        pe.wait_ge(copied[h], i)
                        for c in range(parts):
                            last = nc.tensor.transpose(flipped_ps[:, h, c, :], chunk[h][:, c * P:(c + 1) * P], k["ident"][:])
                        last.then_inc(flipped[h], 1)
                    for h in range(2):
                        pe.wait_ge(copied[h], i + 1)
                        pe.wait_ge(taken[h], i)
                        for c in range(parts):
                            last = nc.tensor.matmul(product[:, h, 0:fo], turned[h][:, c, :], weights[:, c, :],
                                                    start=(c == 0), stop=(c == parts - 1))
                        last.then_inc(multiplied[h], 1)

            @block.scalar
            def _(act):
                with act.Fori(0, n // 2) as i:
                    for h in range(2):
                        act.wait_ge(flipped[h], i + 1)
                        act.wait_ge(multiplied[h], i)
                        nc.scalar.copy(turned[h][:], flipped_ps[:, h, 0:parts, :]).then_inc(copied[h], 1)

            @block.vector
            def _(dve):
                with dve.Fori(0, n // 2) as i:
                    for h in range(2):
                        dve.wait_ge(multiplied[h], i + 1)
                        nc.vector.tensor_copy(out[:, bass.ds((i * 2 + h) * fo, fo)], product[:, h, 0:fo]).then_inc(taken[h], 1)


def load_diagonal(nc, name, w, pieces):
    with ExitStack() as ctx:
        _, _, sem = _scope(nc, ctx, name)
        cleared, loaded = sem("cleared"), sem("loaded")
        with nc.Block() as block:
            @block.vector
            def _(dve):
                nc.vector.memset(w[:], 0.0).then_inc(cleared, 1)

            @block.sync
            def _(sp):
                sp.wait_ge(cleared, 1)
                for q in range(4):
                    at = 0
                    for piece in pieces:
                        f = piece.shape[1]
                        sp.dma_start(w[D * q:D * (q + 1), q, at:at + f], piece).then_inc(loaded, DMA)
                        at += f
                sp.wait_ge(loaded, 4 * len(pieces) * DMA)


def load_rows(nc, name, pairs):
    with ExitStack() as ctx:
        _, _, sem = _scope(nc, ctx, name)
        loaded = sem("loaded")
        with nc.Block() as block:
            @block.sync
            def _(sp):
                for a, b in pairs:
                    sp.dma_start(a, b).then_inc(loaded, DMA)
                sp.wait_ge(loaded, len(pairs) * DMA)


def on_vector(nc, name, steps):
    with ExitStack() as ctx:
        _, _, sem = _scope(nc, ctx, name)
        chain_sem = sem("chain")
        with nc.Block() as block:
            @block.vector
            def _(dve):
                chain = Chain(dve, chain_sem)
                for step in steps:
                    chain.link(step())


def gcn(nc, io, k, dram):
    v = nc.vector
    with ExitStack() as ctx:
        sb, _, _ = _scope(nc, ctx, "gcn")
        h = sb("h", [P, JP, D])
        norm_relu(nc, k, "gcn_norm", h)
        on_vector(nc, "gcn_scale0", [lambda: v.tensor_tensor(h[:], h[:], _spread(k["dinv"][:], D), ALU.mult)])
        store_table(nc, "gcn_table0", dram["tab32"], h, D)
        sum_pass(nc, k, "gcn_sum0", dram["tab32"], dram["totals"], D)
        with ExitStack() as inner:
            sbi, _, _ = _scope(nc, inner, "gcn1")
            sums = sbi("sums", [P, JP, D])
            wide = sbi("wide", [P, JP, HID])
            w1 = sbi("w1", [P, 1, 4 * HID])
            b1 = sbi("b1", [P, HID])
            load_totals(nc, "gcn_load0", dram["totals"], sums, D)
            load_diagonal(nc, "gcn_w1", w1[:].rearrange("p o (q f) -> p (o q) f", q=4), [io["L0_gnn_W1"]])
            load_rows(nc, "gcn_b1", [(b1[:], io["L0_gnn_b1"].unsqueeze(0).to_broadcast([P, HID]))])
            on_vector(nc, "gcn_self0", [lambda: v.tensor_tensor(sums[:], sums[:], h[:], ALU.add)])
            node_linear(nc, k, "gcn_lin1", sums[:].rearrange("p j f -> p (j f)"), JP // 4, 1, w1, wide[:].rearrange("p j f -> p (j f)"))
            on_vector(nc, "gcn_act1", [
                lambda: v.tensor_tensor(wide[:], wide[:], _spread(k["dinv"][:], HID), ALU.mult),
                lambda: v.tensor_tensor(wide[:], wide[:], b1[:].unsqueeze(1).to_broadcast([P, JP, HID]), ALU.add),
                lambda: v.tensor_single_scalar(wide[:], wide[:], 0.0, op=ALU.max),
                lambda: v.tensor_tensor(wide[:], wide[:], _spread(k["dinv"][:], HID), ALU.mult)])
            store_table(nc, "gcn_table1", dram["tab128"], wide, HID)
        sum_pass(nc, k, "gcn_sum1", dram["tab128"], dram["totals"], HID)
        with ExitStack() as inner:
            sbi, _, _ = _scope(nc, inner, "gcn2")
            sums = sbi("sums", [P, JP, HID])
            w2 = sbi("w2", [P, 1, HID])
            w3 = sbi("w3", [P, 1, D])
            b2 = sbi("b2", [P, HID])
            load_totals(nc, "gcn_load1", dram["totals"], sums, HID)
            load_rows(nc, "gcn_w2", [(w2[:, 0, :], io["L0_gnn_W2"]), (w3[:, 0, :], io["L0_gnn_W3"]),
                                     (b2[:], io["L0_gnn_b2"].unsqueeze(0).to_broadcast([P, HID]))])
            load_wide = sbi("own", [P, 14, HID])
            with ExitStack() as inner2:
                _, _, sem = _scope(nc, inner2, "gcn_self1")
                fetched, added = sem("fetched"), sem("added")
                with nc.Block() as block:
                    @block.sync
                    def _(sp):
                        for c in range(J // 14):
                            sp.wait_ge(added, c)
                            sp.dma_start(load_wide[:], _node_rows(dram["tab128"], 14 * c, 14 * (c + 1))).then_inc(fetched, DMA)

                    @block.vector
                    def _(dve):
                        for c in range(J // 14):
                            dve.wait_ge(fetched, (c + 1) * DMA)
                            at = slice(14 * c, 14 * (c + 1))
                            v.tensor_tensor(sums[:, at, :], sums[:, at, :], load_wide[:], ALU.add).then_inc(added, 1)
            flat = sums[:].rearrange("p j f -> p (j f)")
            node_linear(nc, k, "gcn_lin2", flat, J, 1, w2, flat)
            on_vector(nc, "gcn_act2", [
                lambda: v.tensor_tensor(sums[:], sums[:], _spread(k["dinv"][:], HID), ALU.mult),
                lambda: v.tensor_tensor(sums[:], sums[:], b2[:].unsqueeze(1).to_broadcast([P, JP, HID]), ALU.add),
                lambda: v.tensor_single_scalar(sums[:], sums[:], 0.0, op=ALU.max),
                lambda: v.tensor_tensor(sums[:], sums[:], _spread(k["dinv"][:], HID), ALU.mult),
                lambda: v.memset(h[:], 0.0)])
            node_linear(nc, k, "gcn_lin3", flat, J, 1, w3, h[:].rearrange("p j f -> p (j f)"))
            store_table(nc, "gcn_table2", dram["tab32"], h, D)
        sum_pass(nc, k, "gcn_sum2", dram["tab32"], dram["totals"], D)
        sums = sb("sums2", [P, JP, D])
        b3 = sb("b3", [P, D])
        load_totals(nc, "gcn_load2", dram["totals"], sums, D)
        load_rows(nc, "gcn_b3", [(b3[:], io["L0_gnn_b3"].unsqueeze(0).to_broadcast([P, D]))])
        on_vector(nc, "gcn_out", [
            lambda: v.tensor_tensor(sums[:], sums[:], h[:], ALU.add),
            lambda: v.tensor_tensor(sums[:], sums[:], _spread(k["dinv"][:], D), ALU.mult),
            lambda: v.tensor_tensor(sums[:], sums[:], b3[:].unsqueeze(1).to_broadcast([P, JP, D]), ALU.add),
            lambda: v.tensor_single_scalar(sums[:], sums[:], 0.0, op=ALU.max),
            lambda: v.tensor_tensor(k["x"][:], k["x"][:], sums[:], ALU.add)])


def score_pass(nc, k, dram, q_nodes, score):
    with ExitStack() as ctx:
        sb, psum, sem = _scope(nc, ctx, "score")
        staged = sb("staged", [P, R, G], U32)
        ring = sb("ring", [P, R, G, 2 * D])
        onehot = [sb(f"onehot{h}", [P, G, P]) for h in range(2)]
        onehot_t = [sb(f"onehot_t{h}", [P, G, P]) for h in range(2)]
        product = [sb(f"product{h}", [P, G, D]) for h in range(2)]
        flipped_ps = psum("flipped_ps", [P, 2, G, P])
        q_edge = psum("q_edge", [P, 2, 512])
        indexed, made, reduced, released = sem("indexed"), sem("made"), sem("reduced"), sem("released")
        looked_up = [sem(f"looked_up{q}") for q in range(R)]
        gathered = [sem(f"gathered{q}") for q in range(R)]
        flipped = [sem(f"flipped{q}") for q in range(R)]
        turned = [sem(f"turned{q}") for q in range(R)]
        used = [sem(f"used{q}") for q in range(R)]
        spilled = [sem(f"spilled{q}") for q in range(R)]
        with nc.Block() as block:
            @block.scalar
            def _(act):
                with act.Fori(0, ITERS) as i:
                    for q in range(R):
                        act.wait_ge(gathered[q], i * G * DMA)
                        nc.scalar.copy(staged[:, q, :], k["src"][:, bass.ds((i * R + q) * G, G)]).then_inc(indexed, 1)
                        act.wait_ge(flipped[q], i + 1)
                        act.wait_ge(looked_up[(q - 2) % R], i + (q >= 2))
                        nc.scalar.copy(onehot_t[q % 2][:], flipped_ps[:, q % 2, :, :]).then_inc(turned[q], 1)

            @block.gpsimd
            def _(pool):
                with pool.Fori(0, ITERS) as i:
                    for q in range(R):
                        pool.wait_ge(indexed, i * R + q + 1)
                        pool.wait_ge(used[q], i)
                        pool.wait_ge(spilled[q], i * DMA)
                        pool.sem_inc(released, 1)
                        for g in range(G):
                            nc.gpsimd.indirect_dma_start(
                                out=ring[:, q, g, :], out_offset=None, in_=dram["tab64"],
                                in_offset=bass.IndirectOffsetOnAxis(ap=staged[:, q, g:g + 1], axis=0)).then_inc(gathered[q], DMA)

            @block.vector
            def _(dve):
                _one_hot(nc, k, onehot[0], 0).then_inc(made, 1)
                with dve.Fori(0, ITERS) as i:
                    for q in range(R):
                        dve.wait_ge(flipped[(q - 1) % R], i + (q >= 1))
                        _one_hot(nc, k, onehot[(q + 1) % 2], (i * R + q + 1) * G).then_inc(made, 1)
                        dve.wait_ge(looked_up[q], i + 1)
                        dve.wait_ge(gathered[q], (i + 1) * G * DMA)
                        nc.vector.tensor_tensor(product[q % 2][:], q_edge[:, q % 2, 0:G * D].rearrange("p (g f) -> p g f", f=D),
                                                ring[:, q, :, 0:D], ALU.mult).then_inc(used[q], 1)
                        dve.wait_ge(used[q], i + 1)
                        nc.vector.tensor_reduce(score[:, bass.ds((i * R + q) * G, G), :],
                                                product[q % 2][:].rearrange("p g (h d) -> p g h d", d=DHEAD),
                                                axis=AX_X, op=ALU.add).then_inc(reduced, 1)

            @block.tensor
            def _(pe):
                with pe.Fori(0, ITERS) as i:
                    for q in range(R):
                        pe.wait_ge(made, i * R + q + 1)
                        pe.wait_ge(turned[(q - 2) % R], i + (q >= 2))
                        for g in range(G):
                            last = nc.tensor.transpose(flipped_ps[:, q % 2, g, :], onehot[q % 2][:, g, :], k["ident"][:])
                        last.then_inc(flipped[q], 1)
                        tiles, _ = _tile_registers(nc, pe, k, i * R + q)
                        pe.wait_ge(turned[q], i + 1)
                        pe.wait_ge(used[(q - 2) % R], i + (q >= 2))
                        for g in range(G):
                            last = nc.tensor.matmul(q_edge[:, q % 2, g * D:(g + 1) * D], onehot_t[q % 2][:, g, :],
                                                    q_nodes[:, bass.ds(tiles[g] * D, D)], start=True, stop=True)
                        last.then_inc(looked_up[q], 1)

            @block.sync
            def _(sp):
                with sp.Fori(0, ITERS) as i:
                    for q in range(R):
                        sp.wait_ge(gathered[q], (i + 1) * G * DMA)
                        sp.dma_start(dram["kv"][:, bass.ds((i * R + q) * G * 2 * D, G * 2 * D)],
                                     ring[:, q, :, :].rearrange("p g f -> p (g f)")).then_inc(spilled[q], DMA)
                for q in range(R):
                    sp.wait_ge(spilled[q], ITERS * DMA)


def softmax_weights(nc, k, dram, score):
    SE = BLOCKS * P
    with ExitStack() as ctx:
        sb, psum, sem = _scope(nc, ctx, "softmax")
        dst = sb("dst", [P, BLOCKS, P])
        rel = sb("rel", [P, BLOCKS, P])
        reset = sb("reset", [P, BLOCKS, P])
        by_step = sb("by_step", [P, HEADS, BLOCKS, P])
        back = sb("back", [P, BLOCKS, P])
        edge_of = sb("edge_of", [P, BLOCKS, 4, HEADS])
        carry = [sb(f"carry{n}", [HEADS, S]) for n in range(4)]
        resets = [sb(f"resets{n}", [HEADS, S]) for n in range(3)]
        spread = sb("spread", [P, BLOCKS, 2, HEADS])
        loaded = sem("loaded")
        with nc.Block() as block:
            @block.sync
            def _(sp):
                sp.dma_start(dst[:].rearrange("p b e -> p (b e)"), dram["dst_t"]).then_inc(loaded, DMA)
                sp.dma_start(rel[:].rearrange("p b e -> p (b e)"), dram["drel_t"]).then_inc(loaded, DMA)
                sp.wait_ge(loaded, 2 * DMA)
        v = nc.vector

        def limits(a):
            return lambda: v.tensor_scalar(a, a, 2 * BIG, -BIG, ALU.mult, ALU.add)

        on_vector(nc, "softmax_valid", [
            lambda: v.tensor_single_scalar(reset[:], rel[:], 0.0, op=ALU.is_ge),
            lambda: v.tensor_single_scalar(back[:], rel[:], float(P), op=ALU.is_lt),
            lambda: v.tensor_tensor(rel[:], reset[:], back[:], ALU.mult), limits(rel[:])])
        with ExitStack() as inner:
            _, psum_in, sem_in = _scope(nc, inner, "softmax_turn")
            turned = psum_in("turned", [P, 2, HEADS, P])
            flipped, taken = sem_in("flipped"), sem_in("taken")
            with nc.Block() as block:
                @block.tensor
                def _(pe):
                    for b in range(BLOCKS):
                        if b >= 2:
                            pe.wait_ge(taken, b - 1)
                        for h in range(HEADS):
                            last = nc.tensor.transpose(turned[:, b % 2, h, :], score[:, b * P:(b + 1) * P, h], k["ident"][:])
                        last.then_inc(flipped, 1)

                @block.vector
                def _(dve):
                    for b in range(BLOCKS):
                        dve.wait_ge(flipped, b + 1)
                        v.scalar_tensor_tensor(out=by_step[:, :, b, :], in0=turned[:, b % 2, :, :], scalar=1.0 / math.sqrt(DHEAD),
                                               in1=rel[:, b, :].unsqueeze(1).to_broadcast([P, HEADS, P]),
                                               op0=ALU.mult, op1=ALU.min).then_inc(taken, 1)
        tops = sb("tops", [P, HEADS, BLOCKS, P])
        flat = lambda a: a.rearrange("p b e -> p (b e)")
        steps = [lambda: v.memset(reset[:], 0.0),
                 lambda: v.tensor_tensor(reset[:, :, 1:P], dst[:, :, 1:P], dst[:, :, 0:P - 1], ALU.is_equal), limits(reset[:])]
        steps += [lambda h=h: v.tensor_tensor_scan(flat(tops[:, h]), flat(reset[:]), flat(by_step[:, h]), -BIG, ALU.min, ALU.max)
                  for h in range(HEADS)]
        steps += [lambda h=h: v.tensor_copy(edge_of[:, :, 0, h], tops[:, h, :, P - 1]) for h in range(HEADS)]
        steps += [lambda: v.memset(reset[:], 0.0),
                  lambda: v.tensor_tensor(reset[:, :, 0:P - 1], dst[:, :, 1:P], dst[:, :, 0:P - 1], ALU.is_equal), limits(reset[:])]
        for h in range(HEADS):
            steps += [lambda h=h: v.tensor_tensor_scan(flat(back[:])[:, ::-1], flat(reset[:])[:, ::-1], flat(by_step[:, h])[:, ::-1],
                                                       -BIG, ALU.min, ALU.max),
                      lambda h=h: v.tensor_copy(edge_of[:, :, 1, h], back[:, :, 0]),
                      lambda h=h: v.tensor_tensor(tops[:, h], tops[:, h], back[:], ALU.max),
                      lambda h=h: v.tensor_copy(edge_of[:, :, 2, h], dst[:, :, 0]),
                      lambda h=h: v.tensor_copy(edge_of[:, :, 3, h], dst[:, :, P - 1])]
        on_vector(nc, "softmax_scan", steps)
        with ExitStack() as inner:
            _, psum_in, sem_in = _scope(nc, inner, "softmax_rows")
            rows = psum_in("rows", [HEADS, 4, 4, P])
            flipped, taken = sem_in("flipped"), sem_in("taken")
            with nc.Block() as block:
                @block.tensor
                def _(pe):
                    for n in range(4):
                        if n:
                            pe.wait_ge(taken, n)
                        for b in range(BLOCKS):
                            last = nc.tensor.transpose(rows[:, b // 4, b % 4, :], edge_of[:, b, n, :], k["ident"][:])
                        last.then_inc(flipped, 1)

                @block.vector
                def _(dve):
                    for n in range(4):
                        dve.wait_ge(flipped, n + 1)
                        v.tensor_copy(carry[n][:], rows[:].rearrange("h a b e -> h (a b e)")[:, 0:S]).then_inc(taken, 1)
        last_max, first_max, first_dst, last_dst = (c[:] for c in carry)
        cont, whole, limit = (c[:] for c in resets)
        on_vector(nc, "softmax_carry", [
            lambda: v.tensor_tensor(whole, first_dst, last_dst, ALU.is_equal),
            lambda: v.memset(cont, 0.0),
            lambda: v.tensor_tensor(cont[:, 1:S], first_dst[:, 1:S], last_dst[:, 0:S - 1], ALU.is_equal),
            lambda: v.tensor_tensor(limit, whole, cont, ALU.mult), limits(limit),
            lambda: v.tensor_tensor_scan(first_dst, limit, last_max, -BIG, ALU.min, ALU.max),
            lambda: v.tensor_copy(limit, whole),
            lambda: v.memset(limit[:, S - 1:S], 0.0),
            lambda: v.tensor_tensor(limit[:, 0:S - 1], whole[:, 0:S - 1], cont[:, 1:S], ALU.mult), limits(limit),
            lambda: v.tensor_tensor_scan(last_dst[:, ::-1], limit[:, ::-1], first_max[:, ::-1], -BIG, ALU.min, ALU.max),
            limits(cont),
            lambda: v.memset(last_max, -BIG), lambda: v.memset(first_max, -BIG),
            lambda: v.tensor_tensor(last_max[:, 1:S], first_dst[:, 0:S - 1], cont[:, 1:S], ALU.min),
            lambda: v.tensor_tensor(first_max[:, 0:S - 1], last_dst[:, 1:S], cont[:, 1:S], ALU.min)])
        with ExitStack() as inner:
            _, psum_in, sem_in = _scope(nc, inner, "softmax_columns")
            columns = psum_in("columns", [P, BLOCKS, 2, HEADS])
            flipped = sem_in("flipped")
            with nc.Block() as block:
                @block.tensor
                def _(pe):
                    for b in range(BLOCKS):
                        for n in range(2):
                            last = nc.tensor.transpose(columns[:, b, n, :], carry[n][:, b * P:(b + 1) * P], k["ident"][0:HEADS, 0:HEADS])
                    last.then_inc(flipped, 1)

                @block.vector
                def _(dve):
                    dve.wait_ge(flipped, 1)
                    v.tensor_copy(spread[:], columns[:])
        steps = []
        for n, e in ((0, 0), (1, P - 1)):
            steps += [lambda e=e: v.tensor_tensor(reset[:], dst[:], dst[:, :, e:e + 1].to_broadcast([P, BLOCKS, P]), ALU.is_equal),
                      limits(reset[:])]
            steps += [lambda b=b, h=h, n=n: v.scalar_tensor_tensor(out=tops[:, h, b, :], in0=reset[:, b, :], scalar=spread[:, b, n, h:h + 1],
                                                                   in1=tops[:, h, b, :], op0=ALU.min, op1=ALU.max)
                      for b in range(BLOCKS) for h in range(HEADS)]
        steps += [lambda: v.tensor_tensor(by_step[:], by_step[:], tops[:], ALU.subtract)]
        on_vector(nc, "softmax_top", steps)
        with ExitStack() as inner:
            _, psum_in, sem_in = _scope(nc, inner, "softmax_exp")
            turned = psum_in("turned", [P, 2, HEADS, P])
            raised, flipped, taken = sem_in("raised"), sem_in("flipped"), sem_in("taken")
            with nc.Block() as block:
                @block.scalar
                def _(act):
                    for b in range(BLOCKS):
                        nc.scalar.activation(tops[:, :, b, :], by_step[:, :, b, :], ACT.Exp).then_inc(raised, 1)

                @block.tensor
                def _(pe):
                    for b in range(BLOCKS):
                        pe.wait_ge(raised, b + 1)
                        if b >= 2:
                            pe.wait_ge(taken, b - 1)
                        for h in range(HEADS):
                            last = nc.tensor.transpose(turned[:, b % 2, h, :], tops[:, h, b, :], k["ident"][:])
                        last.then_inc(flipped, 1)

                @block.vector
                def _(dve):
                    for b in range(BLOCKS):
                        dve.wait_ge(flipped, b + 1)
                        v.tensor_copy(score[:, b * P:(b + 1) * P, :], turned[:, b % 2, :, :].rearrange("p h e -> p e h")).then_inc(taken, 1)


def value_pass(nc, k, dram, weight):
    width = D + HEADS
    with ExitStack() as ctx:
        sb, psum, sem = _scope(nc, ctx, "value")
        ring = sb("ring", [P, R, G, 2 * D])
        message = [sb(f"message{h}", [P, G, width]) for h in range(2)]
        onehot = [sb(f"onehot{h}", [P, G, P]) for h in range(2)]
        sums = sb("sums", [P, R, G, width])
        partial = psum("partial", [P, 2, 512])
        made, acc_step = sem("made"), sem("acc_step")
        loaded = [sem(f"loaded{q}") for q in range(R)]
        summed = [sem(f"summed{q}") for q in range(R)]
        used = [sem(f"used{q}") for q in range(R)]
        saved = [sem(f"saved{q}") for q in range(R)]
        checked = sem("checked")
        with nc.Block() as block:
            @block.scalar
            def _(act):
                with act.Fori(0, ITERS) as i:
                    for q in range(R):
                        act.wait_ge(used[q], i)
                        act.dma_start(ring[:, q, :, :].rearrange("p g f -> p (g f)"),
                                      dram["kv"][:, bass.ds((i * R + q) * G * 2 * D, G * 2 * D)]).then_inc(loaded[q], DMA)

            @block.gpsimd
            def _(pool):
                with pool.Fori(0, ITERS) as i:
                    for q in range(R):
                        pool.wait_ge(summed[(q - 2) % R], i + (q >= 2))
                        pool.wait_ge(loaded[q], (i + 1) * DMA)
                        nc.gpsimd.tensor_tensor(
                            message[q % 2][:, :, 0:D].rearrange("p g (h d) -> p g h d", d=DHEAD),
                            ring[:, q, :, D:2 * D].rearrange("p g (h d) -> p g h d", d=DHEAD),
                            weight[:, bass.ds((i * R + q) * G, G), :].unsqueeze(3).to_broadcast([P, G, HEADS, DHEAD]), ALU.mult)
                        nc.gpsimd.tensor_copy(message[q % 2][:, :, D:width],
                                              weight[:, bass.ds((i * R + q) * G, G), :]).then_inc(used[q], 1)

            @block.vector
            def _(dve):
                _clear_sums(nc, sums, acc_step)
                _one_hot(nc, k, onehot[0], 0).then_inc(made, 1)
                with dve.Fori(0, ITERS) as i:
                    for q in range(R):
                        dve.wait_ge(summed[(q - 1) % R], i + (q >= 1))
                        _one_hot(nc, k, onehot[(q + 1) % 2], (i * R + q + 1) * G).then_inc(made, 1)
                        dve.wait_ge(summed[q], i + 1)
                        _running_sums(nc, dve, k, i, q, sums,
                                      lambda g: partial[:, q % 2, g * width:(g + 1) * width], acc_step, saved)

            @block.tensor
            def _(pe):
                with pe.Fori(0, ITERS) as i:
                    for q in range(R):
                        pe.wait_ge(made, i * R + q + 1)
                        pe.wait_ge(used[q], i + 1)
                        pe.wait_ge(acc_step, (i * R + q) * G)
                        for g in range(G):
                            last = nc.tensor.matmul(partial[:, q % 2, g * width:(g + 1) * width],
                                                    onehot[q % 2][:, g, :], message[q % 2][:, g, :], start=True, stop=True)
                        last.then_inc(summed[q], 1)

            @block.sync
            def _(sp):
                _save_tiles(nc, sp, k, sums, dram["totals"], acc_step, checked, saved, width)


def attention(nc, io, k, dram):
    v = nc.vector
    with ExitStack() as ctx:
        sb, _, _ = _scope(nc, ctx, "att")
        h = sb("h", [P, JP, D])
        flat_h = h[:].rearrange("p j f -> p (j f)")
        norm_relu(nc, k, "att_norm", h)
        on_vector(nc, "att_add_h", [lambda: v.tensor_tensor(k["x"][:], k["x"][:], h[:], ALU.add)])
        score = sb("score", [P, S, HEADS])
        with ExitStack() as inner:
            sbi, _, _ = _scope(nc, inner, "qkv")
            qkv = sbi("qkv", [P, JP, 3 * D])
            w = sbi("w", [P, 1, 4 * 3 * D])
            load_diagonal(nc, "qkv_w", w[:].rearrange("p o (q f) -> p (o q) f", q=4), [io["L1_gnn_Wq"], io["L1_gnn_Wk"], io["L1_gnn_Wv"]])
            node_linear(nc, k, "qkv_lin", flat_h, JP // 4, 1, w, qkv[:].rearrange("p j f -> p (j f)"))
            on_vector(nc, "qkv_q", [lambda: v.tensor_copy(h[:], qkv[:, :, 0:D])])
            store_table(nc, "qkv_table", dram["tab64"], qkv[:, :, D:3 * D], 2 * D)
        score_pass(nc, k, dram, flat_h, score)
        softmax_weights(nc, k, dram, score)
        value_pass(nc, k, dram, score)
        with ExitStack() as inner:
            sbi, _, _ = _scope(nc, inner, "wo")
            sums = sbi("sums", [P, JP, D + HEADS])
            w = sbi("w", [P, 1, 4 * D])
            load_totals(nc, "wo_load", dram["totals"], sums, D + HEADS)
            load_diagonal(nc, "wo_w", w[:].rearrange("p o (q f) -> p (o q) f", q=4), [io["L1_gnn_Wo"]])
            on_vector(nc, "wo_divide", [
                lambda: v.tensor_single_scalar(sums[:, :, D:D + HEADS], sums[:, :, D:D + HEADS], 1e-16, op=ALU.max),
                lambda: v.reciprocal(sums[:, :, D:D + HEADS], sums[:, :, D:D + HEADS]),
                lambda: v.tensor_tensor(h[:].rearrange("p j (h d) -> p j h d", d=DHEAD),
                                        sums[:, :, 0:D].rearrange("p j (h d) -> p j h d", d=DHEAD),
                                        sums[:, :, D:D + HEADS].unsqueeze(3).to_broadcast([P, JP, HEADS, DHEAD]), ALU.mult)])
            out = sums[:].rearrange("p j f -> p (j f)")[:, 0:JP * D]
            node_linear(nc, k, "wo_lin", flat_h, JP // 4, 1, w, out)
            on_vector(nc, "wo_add", [lambda: v.tensor_tensor(k["x"][:].rearrange("p j f -> p (j f)"),
                                                             k["x"][:].rearrange("p j f -> p (j f)"), out, ALU.add)])


def relation_pass(nc, k, dram, y_nodes, relations, current):
    G4, WIDTH, LOOK = 4, N_BASES * D, D + N_BASES
    with ExitStack() as ctx:
        sb, psum, sem = _scope(nc, ctx, "rel")
        staged = sb("staged", [P, R, G], U32)
        ring = sb("ring", [P, R, G, 2 * D])
        onehot = [sb(f"onehot{h}", [P, G4, P]) for h in range(2)]
        onehot_t = [sb(f"onehot_t{h}", [P, G4, P]) for h in range(2)]
        kind = [sb(f"kind{h}", [P, G4, N_REL]) for h in range(2)]
        kind_t = [sb(f"kind_t{h}", [N_REL, G4, P]) for h in range(2)]
        dots = sb("dots", [P, G4, D])
        gate = sb("gate", [P, 2, G4])
        coef = sb("coef", [P, G4, N_BASES])
        message = [sb(f"message{h}", [P, G4, WIDTH]) for h in range(2)]
        sums = sb("sums", [P, 2, G4, WIDTH])
        flipped_ps = psum("flipped_ps", [P, 2, G4, P])
        looked = psum("looked", [P, 512])
        partial = psum("partial", [P, G4, WIDTH])
        (indexed, made, flipped, turned, looked_up, logit, gated, messaged, summed, acc_step, work) = (
            sem(n) for n in ("indexed", "made", "flipped", "turned", "looked_up", "logit", "gated", "messaged", "summed", "acc_step", "work"))
        gathered = [sem(f"gathered{q}") for q in range(R)]
        used = [sem(f"used{q}") for q in range(R)]
        saved = [sem(f"saved{h}") for h in range(2)]
        own, released, checked = sem("own"), sem("released"), sem("checked")
        WORK = 3
        with nc.Block() as block:
            @block.scalar
            def _(act):
                with act.Fori(0, ITERS) as i:
                    for q in range(R):
                        act.wait_ge(gathered[q], i * G * DMA)
                        nc.scalar.copy(staged[:, q, :], k["src"][:, bass.ds((i * R + q) * G, G)]).then_inc(indexed, 1)
                        for h in range(2):
                            n = (i * R + q) * 2 + h
                            act.wait_ge(flipped, n + 1)
                            nc.scalar.copy(onehot_t[h][:], flipped_ps[:, 0, :, :])
                            nc.scalar.copy(kind_t[h][:], flipped_ps[0:N_REL, 1, :, :]).then_inc(turned, 1)
                            act.wait_ge(logit, n + 1)
                            nc.scalar.activation(gate[:, 1, :], gate[:, 0, :], ACT.Tanh, scale=1.0 / math.sqrt(D)).then_inc(gated, 1)

            @block.gpsimd
            def _(pool):
                with pool.Fori(0, ITERS) as i:
                    for q in range(R):
                        pool.wait_ge(indexed, i * R + q + 1)
                        pool.wait_ge(used[q], 2 * i)
                        pool.sem_inc(released, 1)
                        for g in range(G):
                            nc.gpsimd.indirect_dma_start(
                                out=ring[:, q, g, :], out_offset=None, in_=dram["tab64"],
                                in_offset=bass.IndirectOffsetOnAxis(ap=staged[:, q, g:g + 1], axis=0)).then_inc(gathered[q], DMA)
                for j in range(J):
                    nc.gpsimd.indirect_dma_start(
                        out=current[:, j, :], out_offset=None, in_=dram["tab32"],
                        in_offset=bass.IndirectOffsetOnAxis(ap=k["last_index"][:, j:j + 1], axis=0)).then_inc(own, DMA)
                pool.wait_ge(own, J * DMA)

            @block.vector
            def _(dve):
                nc.vector.memset(sums[:, 1, G4 - 1, :], 0.0).then_inc(acc_step, G4)
                with dve.Fori(0, ITERS) as i:
                    for q in range(R):
                        for h in range(2):
                            n = (i * R + q) * 2 + h
                            at = slice(h * G4, (h + 1) * G4)
                            first = (i * R + q) * G + h * G4
                            dve.wait_ge(flipped, n)
                            dve.wait_ge(summed, n)
                            nc.vector.tensor_tensor(onehot[h][:], k["iota"][:].unsqueeze(1).to_broadcast([P, G4, P]),
                                                    k["drel"][:, bass.ds(first, G4)].unsqueeze(2).to_broadcast([P, G4, P]), ALU.is_equal)
                            nc.vector.tensor_tensor(kind[h][:], k["iota"][:, 0:N_REL].unsqueeze(1).to_broadcast([P, G4, N_REL]),
                                                    k["type"][:, bass.ds(first, G4)].unsqueeze(2).to_broadcast([P, G4, N_REL]),
                                                    ALU.is_equal).then_inc(made, 1)
                            dve.wait_ge(looked_up, n + 1)
                            if h == 0:
                                dve.wait_ge(gathered[q], (i + 1) * G * DMA)
                            seen = looked[:, 0:G4 * LOOK].rearrange("p (g f) -> p g f", f=LOOK)
                            nc.vector.tensor_tensor(dots[:], seen[:, :, 0:D], ring[:, q, at, D:2 * D], ALU.mult).then_inc(work, 1)
                            dve.wait_ge(work, n * WORK + 1)
                            nc.vector.tensor_reduce(gate[:, 0, :], dots[:], axis=AX_X, op=ALU.add).then_inc(work, 1)
                            dve.wait_ge(work, n * WORK + 2)
                            nc.vector.tensor_single_scalar(gate[:, 0, :], gate[:, 0, :], 0.0, op=ALU.max).then_inc(logit, 1)
                            dve.wait_ge(gated, n + 1)
                            nc.vector.tensor_tensor(coef[:], seen[:, :, D:LOOK], gate[:, 1, :].unsqueeze(2).to_broadcast([P, G4, N_BASES]),
                                                    ALU.mult).then_inc(work, 1)
                            dve.wait_ge(work, n * WORK + 3)
                            for g in range(G4):
                                last = nc.vector.tensor_tensor(
                                    message[h][:, g, :].rearrange("p (b f) -> p b f", f=D),
                                    coef[:, g, :].unsqueeze(2).to_broadcast([P, N_BASES, D]),
                                    ring[:, q, h * G4 + g, 0:D].unsqueeze(1).to_broadcast([P, N_BASES, D]), ALU.mult)
                                last.then_inc(messaged, 1)
                            dve.wait_ge(messaged, (n + 1) * G4)
                            dve.sem_inc(used[q], 1)
                            dve.wait_ge(saved[h], (i * R + q) * G4 * DMA)
                            for g in range(G4):
                                before = sums[:, h, g - 1, :] if g else sums[:, 1 - h, G4 - 1, :]
                                dve.wait_ge(summed, n * 1 + 1)
                                dve.wait_ge(acc_step, (n + 1) * G4 + g)
                                nc.vector.scalar_tensor_tensor(
                                    out=sums[:, h, g, :], in0=before, scalar=k["keep"][:, bass.ds(first + g, 1)],
                                    in1=partial[:, g, :], op0=ALU.mult, op1=ALU.add).then_inc(acc_step, 1)

            @block.tensor
            def _(pe):
                with pe.Fori(0, ITERS) as i:
                    for q in range(R):
                        tiles, _ = _tile_registers(nc, pe, k, i * R + q)
                        for h in range(2):
                            n = (i * R + q) * 2 + h
                            pe.wait_ge(made, n + 1)
                            pe.wait_ge(turned, n)
                            for g in range(G4):
                                nc.tensor.transpose(flipped_ps[:, 0, g, :], onehot[h][:, g, :], k["ident"][:])
                                last = nc.tensor.transpose(flipped_ps[0:N_REL, 1, g, :], kind[h][:, g, :], k["ident"][:])
                            last.then_inc(flipped, 1)
                            pe.wait_ge(turned, n + 1)
                            pe.wait_ge(messaged, n * G4)
                            for g in range(G4):
                                out = looked[:, g * LOOK:(g + 1) * LOOK]
                                nc.tensor.matmul(out, kind_t[h][:, g, :], relations[:], start=True, stop=False)
                                last = nc.tensor.matmul(out, onehot_t[h][:, g, :], y_nodes[:, bass.ds(tiles[h * G4 + g] * LOOK, LOOK)],
                                                        start=False, stop=True)
                            last.then_inc(looked_up, 1)
                            pe.wait_ge(acc_step, (n + 1) * G4)
                            for g in range(G4):
                                pe.wait_ge(messaged, n * G4 + g + 1)
                                last = nc.tensor.matmul(partial[:, g, :], onehot[h][:, g, :], message[h][:, g, :], start=True, stop=True)
                            last.then_inc(summed, 1)

            @block.sync
            def _(sp):
                with sp.Fori(0, ITERS) as i:
                    for q in range(R):
                        tiles, is_last = _tile_registers(nc, sp, k, i * R + q)
                        for h in range(2):
                            sp.wait_ge(acc_step, ((i * R + q) * 2 + h + 2) * G4)
                            sp.sem_inc(checked, 1)
                            for g in range(G4):
                                sp.dma_start(dram["totals"][:, bass.ds(tiles[h * G4 + g] * WIDTH, WIDTH)], sums[:, h, g, :],
                                             cond=is_last[h * G4 + g]).then_inc(saved[h], DMA)
                for h in range(2):
                    sp.wait_ge(saved[h], GROUPS * G4 * DMA)


def relational(nc, io, k, dram):
    v = nc.vector
    with ExitStack() as ctx:
        sb, _, _ = _scope(nc, ctx, "rl")
        h = sb("h", [P, JP, D])
        flat_h = h[:].rearrange("p j f -> p (j f)")
        LOOK = D + N_BASES
        y_nodes = sb("y", [P, JP, LOOK])
        relations = sb("relations", [N_REL, LOOK])
        current = sb("current", [P, JP, D])
        norm_relu(nc, k, "rl_norm", h)
        with ExitStack() as inner:
            sbi, _, _ = _scope(nc, inner, "hat")
            both = sbi("both", [P, JP, 2 * D])
            w = sbi("w", [P, 1, 8 * D])
            bias = sbi("bias", [P, 2 * D])
            load_diagonal(nc, "hat_w", w[:].rearrange("p o (q f) -> p (o q) f", q=4), [io["A1_t"], io["A2_t"]])
            load_rows(nc, "hat_b", [(bias[:, 0:D], io["L2_gnn_A1_b"].unsqueeze(0).to_broadcast([P, D])),
                                    (bias[:, D:2 * D], io["L2_gnn_A2_b"].unsqueeze(0).to_broadcast([P, D])),
                                    (relations[:, 0:D], io["L2_gnn_rel_emb"]), (relations[:, D:LOOK], io["L2_gnn_w_comp"])])
            node_linear(nc, k, "hat_lin", flat_h, JP // 4, 1, w, both[:].rearrange("p j f -> p (j f)"))
            on_vector(nc, "hat_bias", [
                lambda: v.tensor_tensor(both[:], both[:], bias[:].unsqueeze(1).to_broadcast([P, JP, 2 * D]), ALU.add),
                lambda: v.memset(y_nodes[:], 0.0),
                lambda: v.tensor_copy(y_nodes[:, :, 0:D], both[:, :, D:2 * D]),
                lambda: v.tensor_copy(both[:, :, D:2 * D], both[:, :, 0:D]),
                lambda: v.tensor_copy(both[:, :, 0:D], h[:]),
                lambda: v.memset(current[:], 0.0)])
            store_table(nc, "hat_table", dram["tab64"], both, 2 * D)
            store_table(nc, "hat_rows", dram["tab32"], h, D)
        relation_pass(nc, k, dram, y_nodes[:].rearrange("p j f -> p (j f)"), relations, current)
        with ExitStack() as inner:
            sbi, _, _ = _scope(nc, inner, "rlo")
            own_w = sbi("own_w", [P, 1, 4 * D])
            w = sbi("w", [P, 4, D])
            out = sbi("out", [P, JP, D])
            has = sbi("has", [P, JP])
            load_diagonal(nc, "rlo_own_w", own_w[:].rearrange("p o (q f) -> p (o q) f", q=4), [io["L2_gnn_self_loop_weight"]])
            load_rows(nc, "rlo_w", [(w[:], io["L2_gnn_weight"].rearrange("b i o -> (b i) o").rearrange("(c p) o -> p c o", p=P))])
            node_linear(nc, k, "rlo_own", current[:].rearrange("p j f -> p (j f)"), JP // 4, 1, own_w, flat_h)
            on_vector(nc, "rlo_clear", [lambda: v.memset(out[:], 0.0)])
            node_linear(nc, k, "rlo_lin", dram["totals"], J, 4, w, out[:].rearrange("p j f -> p (j f)"), load=True)
            on_vector(nc, "rlo_out", [
                lambda: v.tensor_tensor(out[:], out[:], h[:], ALU.add),
                lambda: v.tensor_single_scalar(has[:], k["degree"][:], 0.0, op=ALU.is_gt),
                lambda: v.tensor_tensor(out[:], out[:], _spread(has[:], D), ALU.mult),
                lambda: v.tensor_single_scalar(out[:], out[:], 0.0, op=ALU.max),
                lambda: v.tensor_tensor(k["x"][:], k["x"][:], out[:], ALU.add)])


SH_WIDTH = 4 * D + 5 * 24


def harmonic_pass(nc, k, dram):
    with ExitStack() as ctx:
        sb, psum, sem = _scope(nc, ctx, "sh")
        staged = sb("staged", [P, R, G], U32)
        ring = sb("ring", [P, R, G, D])
        parts = sb("parts", [P, R, G, N_SH])
        onehot = [sb(f"onehot{h}", [P, G, P]) for h in range(2)]
        message = [sb(f"message{h}", [P, G, SH_WIDTH]) for h in range(2)]
        sums = sb("sums", [P, R, G, SH_WIDTH])
        partial = psum("partial", [P, 2, G, 256])
        indexed, made, acc_step, released = sem("indexed"), sem("made"), sem("acc_step"), sem("released")
        gathered = [sem(f"gathered{q}") for q in range(R)]
        loaded = [sem(f"loaded{q}") for q in range(R)]
        summed = [sem(f"summed{q}") for q in range(R)]
        used = [sem(f"used{q}") for q in range(R)]
        saved = [sem(f"saved{q}") for q in range(R)]
        checked = sem("checked")
        with nc.Block() as block:
            @block.scalar
            def _(act):
                with act.Fori(0, ITERS) as i:
                    for q in range(R):
                        act.wait_ge(gathered[q], i * G * DMA)
                        nc.scalar.copy(staged[:, q, :], k["src"][:, bass.ds((i * R + q) * G, G)]).then_inc(indexed, 1)
                        act.wait_ge(used[q], i)
                        act.dma_start(parts[:, q, :, :].rearrange("p g f -> p (g f)"),
                                      dram["sh"][:, bass.ds((i * R + q) * G * N_SH, G * N_SH)]).then_inc(loaded[q], DMA)

            @block.gpsimd
            def _(pool):
                _gather_rows(nc, pool, dram["tab32"], staged, ring, indexed, [used], released, gathered)

            @block.vector
            def _(dve):
                _clear_sums(nc, sums, acc_step)
                with dve.Fori(0, ITERS) as i:
                    for q in range(R):
                        dve.wait_ge(summed[(q - 2) % R], i + (q >= 2))
                        _one_hot(nc, k, onehot[q % 2], (i * R + q) * G).then_inc(made, 1)
                        dve.wait_ge(loaded[q], (i + 1) * DMA)
                        dve.wait_ge(gathered[q], (i + 1) * G * DMA)
                        m = message[q % 2]
                        nc.vector.tensor_tensor(m[:, :, 0:4 * D].rearrange("p g (c f) -> p g c f", f=D),
                                                parts[:, q, :, 0:4].unsqueeze(3).to_broadcast([P, G, 4, D]),
                                                ring[:, q, :, :].unsqueeze(2).to_broadcast([P, G, 4, D]), ALU.mult)
                        nc.vector.tensor_tensor(m[:, :, 4 * D:SH_WIDTH].rearrange("p g (c f) -> p g c f", f=24),
                                                parts[:, q, :, 4:N_SH].unsqueeze(3).to_broadcast([P, G, 5, 24]),
                                                ring[:, q, :, 8:D].unsqueeze(2).to_broadcast([P, G, 5, 24]), ALU.mult).then_inc(used[q], 1)
                        dve.wait_ge(summed[q], i + 1)
                        _running_sums(nc, dve, k, i, q, sums, lambda g: partial[:, q % 2, g, 0:SH_WIDTH], acc_step, saved)

            @block.tensor
            def _(pe):
                with pe.Fori(0, ITERS) as i:
                    for q in range(R):
                        pe.wait_ge(made, i * R + q + 1)
                        pe.wait_ge(used[q], i + 1)
                        pe.wait_ge(acc_step, (i * R + q) * G)
                        for g in range(G):
                            last = nc.tensor.matmul(partial[:, q % 2, g, 0:SH_WIDTH], onehot[q % 2][:, g, :],
                                                    message[q % 2][:, g, :], start=True, stop=True)
                        last.then_inc(summed[q], 1)

            @block.sync
            def _(sp):
                _save_tiles(nc, sp, k, sums, dram["totals"], acc_step, checked, saved, SH_WIDTH)


def tensor_product(nc, io, k, dram, out):
    v = nc.vector
    with ExitStack() as ctx:
        sb, _, _ = _scope(nc, ctx, "tp")
        with ExitStack() as inner:
            sbi, _, _ = _scope(nc, inner, "tph")
            h = sbi("h", [P, JP, D])
            norm_relu(nc, k, "tp_norm", h)
            store_table(nc, "tp_table", dram["tab32"], h, D)
        harmonic_pass(nc, k, dram)
        with ExitStack() as inner:
            sbi, psi, _ = _scope(nc, inner, "mix")
            pick = sbi("pick", [8, 2 * P])
            w_all = sbi("w_all", [8, 6 * 8])
            cg = sbi("cg", [P, 14])
            row_w = sbi("row_w", [P, 2, 6 * 8])
            mix = sbi("mix", [P, 2, D])
            sums = sbi("sums", [P, JP, 2 * P])
            delta = sbi("delta", [P, JP, D])
            picked = psi("picked", [P, 2, 64])
            load_rows(nc, "mix_in", [(pick[:], io["pick"]), (cg[:], io["cg"]),
                                     (w_all[:].rearrange("i (c o) -> i c o", o=8), io["L3_gnn_W"].rearrange("c i o -> i c o"))])
            with ExitStack() as inner2:
                _, _, sem = _scope(nc, inner2, "mix_pick")
                ready, taken = sem("ready"), sem("taken")
                with nc.Block() as block:
                    @block.tensor
                    def _(pe):
                        for c in range(2):
                            last = nc.tensor.matmul(picked[:, c, 0:48], pick[:, c * P:(c + 1) * P], w_all[:], start=True, stop=True)
                        last.then_inc(ready, 1)

                    @block.vector
                    def _(dve):
                        v.memset(mix[:], 0.0).then_inc(taken, 1)
                        v.memset(sums[:], 0.0).then_inc(taken, 1)
                        v.memset(delta[:], 0.0).then_inc(taken, 1)
                        dve.wait_ge(ready, 1)
                        v.tensor_copy(row_w[:], picked[:, :, 0:48])

            def add(c, n, combo, lo):
                to = mix[:, c, 0:8] if lo is None else mix[:, c, 8:D].rearrange("p (o k) -> p o k", k=3)[:, :, lo]
                return lambda: v.scalar_tensor_tensor(out=to, in0=row_w[:, c, 8 * combo:8 * combo + 8], scalar=cg[:, n:n + 1], in1=to,
                                                      op0=ALU.mult, op1=ALU.add)
            on_vector(nc, "mix_add", [add(c, n, combo, lo) for n, (c, combo, lo) in enumerate(MIX_TERMS)])
            with ExitStack() as inner2:
                _, _, sem = _scope(nc, inner2, "mix_load")
                loaded = sem("loaded")
                with nc.Block() as block:
                    @block.sync
                    def _(sp):
                        sp.dma_start(sums[:, 0:J, 0:SH_WIDTH], dram["totals"][:, 0:J * SH_WIDTH].rearrange("p (j f) -> p j f", f=SH_WIDTH)).then_inc(loaded, DMA)
                        sp.wait_ge(loaded, DMA)
            node_linear(nc, k, "mix_lin", sums[:].rearrange("p j f -> p (j f)"), J, 2, mix, delta[:].rearrange("p j f -> p (j f)"))
            on_vector(nc, "mix_x", [lambda: v.tensor_tensor(k["x"][:], k["x"][:], delta[:], ALU.add)])
        with ExitStack() as inner:
            _, _, sem = _scope(nc, inner, "out")
            stored = sem("stored")
            with nc.Block() as block:
                @block.sync
                def _(sp):
                    sp.dma_start(_node_rows(out, 0, J - 1), k["x"][:, 0:J - 1, :]).then_inc(stored, DMA)
                    sp.dma_start(out[(J - 1) * P:N_NODES, :], k["x"][0:LAST_TILE_ROWS, J - 1, :]).then_inc(stored, DMA)
                    sp.wait_ge(stored, 2 * DMA)


def _clebsch_gordan(l1, l2, l3):
    def su2(j1, m1, j2, m2, j3, m3):
        if m3 != m1 + m2:
            return 0.0
        f = math.factorial
        low = max(0, j2 - j3 - m1, j1 + m2 - j3)
        high = min(j1 + j2 - j3, j1 - m1, j2 + m2)
        pref = (2 * j3 + 1) * f(j3 + j1 - j2) * f(j3 - j1 + j2) * f(j1 + j2 - j3) / f(j1 + j2 + j3 + 1)
        pref *= f(j3 + m3) * f(j3 - m3) * f(j1 - m1) * f(j1 + m1) * f(j2 - m2) * f(j2 + m2)
        return math.sqrt(pref) * sum((-1) ** n / (f(n) * f(j1 + j2 - j3 - n) * f(j1 - m1 - n) * f(j2 + m2 - n)
                                                 * f(j3 - j2 + m1 + n) * f(j3 - j1 - m2 + n)) for n in range(low, high + 1))

    def real(l):
        q = np.zeros((2 * l + 1, 2 * l + 1), complex)
        for m in range(-l, 0):
            q[l + m, l - m] = 1 / np.sqrt(2)
            q[l + m, l + m] = -1j / np.sqrt(2)
        q[l, l] = 1.0
        for m in range(1, l + 1):
            q[l + m, l + m] = (-1) ** m / np.sqrt(2)
            q[l + m, l - m] = 1j * (-1) ** m / np.sqrt(2)
        return (-1j) ** l * q

    c = np.zeros((2 * l1 + 1, 2 * l2 + 1, 2 * l3 + 1), complex)
    for m1 in range(-l1, l1 + 1):
        for m2 in range(-l2, l2 + 1):
            if -l3 <= m1 + m2 <= l3:
                c[m1 + l1, m2 + l2, m1 + m2 + l3] = su2(l1, m1, l2, m2, l3, m1 + m2)
    c = np.einsum("ij,kl,mn,ikn->jlm", real(l1), real(l2), np.conj(real(l3)).T, c).real
    return c / np.linalg.norm(c)


MIX_TERMS = ([(0, 0, None)] + [(0, 1, o) for o in range(3)] + [(0, 2, o) for o in range(3)] + [(0, 3, None)]
             + [(0, 4, o) for o in range(3)] + [(1, 5, o) for o in range(3)])


def mixing_constants():
    combos = [(0, 0, 0), (0, 1, 1), (1, 0, 1), (1, 1, 0), (1, 1, 1), (2, 1, 1)]
    coefficients = [_clebsch_gordan(*c) for c in combos]
    pick = np.zeros((8, 2 * P), np.float32)
    cg = np.zeros((P, len(MIX_TERMS)), np.float32)
    for row in range(2 * P):
        if row < P:
            part, f = divmod(row, D)
            degree, component = (0, 0) if part == 0 else (1, part - 1)
        else:
            if row >= P + 120:
                continue
            component, f = divmod(row - P, 24)
            degree, f = 2, f + 8
        vector = f >= 8
        channel, direction = divmod(f - 8, 3) if vector else (f, 0)
        pick[channel, row] = 1.0
        for n, (chunk, combo, o) in enumerate(MIX_TERMS):
            le, ln, _ = combos[combo]
            if chunk == row // P and le == degree and ln == int(vector):
                cg[row % P, n] = coefficients[combo][component, direction, o or 0]
    return pick, cg


def gnn_kernel(nc, io, out):
    dram = scratch(nc)
    with ExitStack() as ctx:
        k = tables(nc, ctx)
        constants(nc, k)
        edge_records(nc, io, dram)
        merge_path(nc, k, dram)
        with ExitStack() as inner:
            k["stat"] = inner.enter_context(nc.sbuf_tensor("k_stat", [P, S, 2], F32))
            step_tables(nc, k, dram)
            node_statistics(nc, k)
        load_x(nc, io, k)
        gcn(nc, io, k, dram)
        attention(nc, io, k, dram)
        relational(nc, io, k, dram)
        tensor_product(nc, io, k, dram, out)


def tables(nc, ctx):
    def sb(n, shape, dt=F32):
        return ctx.enter_context(nc.sbuf_tensor(f"k_{n}", shape, dt))
    k = {"iota": sb("iota", [P, P]), "ident": sb("ident", [P, P]), "ones": sb("ones", [P, P]),
         "step_no": sb("step_no", [P, BLOCKS]), "t_of": sb("t_of", [P, BLOCKS]), "j_of": sb("j_of", [P, BLOCKS]),
         "t_index": sb("t_index", [P, BLOCKS], U32), "keep": sb("keep", [P, S]),
         "words": sb("words", [1, GROUPS], I32), "src": sb("src", [P, S], U32),
         "drel": sb("drel", [P, S + G]), "type": sb("type", [P, S]),
         "x": sb("x", [P, JP, D]), "degree": sb("degree", [P, JP]), "last": sb("last", [P, JP]),
         "last_index": sb("last_index", [P, JP], U32), "dinv": sb("dinv", [P, JP])}
    return k


def scratch(nc):
    def d(n, shape, dt=F32):
        return nc.dram_tensor(f"scratch_{n}", shape, dt, kind="Internal").ap()
    return {"rec": d("rec", [T, P * REC]), "j": d("j", [1, S]), "dst_t": d("dst_t", [P, S]), "drel_t": d("drel_t", [P, S]),
            "sh": d("sh", [P, S * N_SH]), "tab32": d("tab32", [J * P, D]), "tab64": d("tab64", [J * P, 2 * D]),
            "tab128": d("tab128", [J * P, HID]), "totals": d("totals", [P, JP * 512]), "kv": d("kv", [P, S * 2 * D])}


def kernel(**inputs):
    import concourse.bacc as bacc
    from concourse.bass_utils import run_bass_kernel_spmd as run

    nc = bacc.Bacc("TRN2", target_bir_lowering=False, num_devices=1)
    given = {n: np.ascontiguousarray(a) for n, a in inputs.items() if n not in ("L2_gnn_A1_w", "L2_gnn_A2_w")}
    given["A1_t"] = np.ascontiguousarray(np.asarray(inputs["L2_gnn_A1_w"]).T)
    given["A2_t"] = np.ascontiguousarray(np.asarray(inputs["L2_gnn_A2_w"]).T)
    given["pick"], given["cg"] = mixing_constants()
    arrays = {f"in_{n}": a for n, a in given.items()}
    io = {n: nc.dram_tensor(f"in_{n}", a.shape, mybir.dt.from_np(a.dtype), kind="ExternalInput").ap() for n, a in given.items()}
    out = nc.dram_tensor("out_x", (N_NODES, D), F32, kind="ExternalOutput").ap()
    gnn_kernel(nc, io, out)
    return run(nc, [arrays], core_ids=[0]).results[0]["out_x"]
```

```python
import math
from contextlib import ExitStack

import numpy as np
import concourse.bass as bass
from concourse import mybir

F32 = mybir.dt.float32
I32 = mybir.dt.int32
U32 = mybir.dt.uint32
ALU = mybir.AluOpType
ACT = mybir.ActivationFunctionType
AX_X = mybir.AxisListType.X

P = 128
N_NODES = 12500
N_EDGES = 200000
D = 32
HID = 128
HEADS, DHEAD = 4, 8
N_REL, N_BASES = 86, 16
J = -(-N_NODES // P)
JP = 104
T = -(-N_EDGES // P)
REC = 16
R_SRC, R_DST, R_NEXT, R_TYPE, R_SH, R_REL, R_LAST = 0, 1, 2, 3, 4, 13, 14
N_SH = 9
G = 8
R = 4
BLOCKS = -(-(T + J - 1) // P)
S = BLOCKS * P
ITERS = S // (G * R)
GROUPS = S // G
TILES = J + S - (T + J - 1)
LEAD = (R - 1) * G
BANK = 512
BIG = 1e30
LAST_TILE_ROWS = N_NODES - (J - 1) * P
PAD_DST = J * P - 1
DMA = 16


def _node_rows(table, j0, j1):
    return table[j0 * P:j1 * P, :].rearrange("(j p) f -> p j f", p=P)


class Chain:

    def __init__(self, engine, semaphore):
        self.engine, self.semaphore, self.value = engine, semaphore, 0

    def link(self, instruction):
        self.value += 1
        instruction.then_inc(self.semaphore, 1)
        self.engine.wait_ge(self.semaphore, self.value)


def _scope(nc, ctx, name):
    def sb(n, shape, dt=F32):
        return ctx.enter_context(nc.sbuf_tensor(f"{name}_{n}", shape, dt))

    def psum(n, shape, dt=F32):
        return ctx.enter_context(nc.psum_tensor(f"{name}_{n}", shape, dt))

    held = []

    def clear():
        nc.clear_and_free_semaphores(held)
        nc.all_engine_barrier()

    def sem(n):
        if not held:
            ctx.callback(clear)
        held.append(nc.alloc_semaphore(f"{name}_{n}"))
        return held[-1]

    return sb, psum, sem


def constants(nc, k):
    with ExitStack() as ctx:
        sb, _, sem = _scope(nc, ctx, "const")
        row = sb("row", [P, 1])
        made = sem("made")
        with nc.Block() as block:
            @block.gpsimd
            def _(pool):
                nc.gpsimd.iota(k["iota"][:], pattern=[[1, P]], base=0, channel_multiplier=0,
                               allow_small_or_imprecise_dtypes=True).then_inc(made, 1)
                nc.gpsimd.iota(row[:], pattern=[[0, 1]], base=0, channel_multiplier=1,
                               allow_small_or_imprecise_dtypes=True).then_inc(made, 1)
                nc.gpsimd.iota(k["step_no"][:], pattern=[[P, BLOCKS]], base=0, channel_multiplier=1,
                               allow_small_or_imprecise_dtypes=True).then_inc(made, 1)

            @block.vector
            def _(dve):
                nc.vector.memset(k["ones"][:], 1.0)
                nc.vector.memset(k["zeros"][:], 0.0)
                dve.wait_ge(made, 3)
                nc.vector.tensor_scalar(k["ident"][:], k["iota"][:], row[:, 0:1], None, ALU.is_equal)


def edge_records(nc, io, dram):
    C = -(-T * P // P)
    LAST = N_EDGES - (P - 1) * C
    CH = C // 3
    assert C == T and CH * 3 == C
    with ExitStack() as ctx:
        sb, _, sem = _scope(nc, ctx, "rec")
        fields = [("src", I32, 1, 0, 0), ("dst", I32, 1, 0, PAD_DST), ("next", I32, 1, 1, PAD_DST),
                  ("type", I32, 1, 0, 0), ("sh0", F32, 1, 0, 0), ("sh1", F32, 3, 0, 0), ("sh2", F32, 5, 0, 0)]
        source = {"src": io["src"], "dst": io["dst"], "next": io["dst"], "type": io["edge_type_86"],
                  "sh0": io["edge_weight1"], "sh1": io["edge_attr_3"], "sh2": io["edge_attr_5"]}
        held = {n: sb(n, [P, C * w], dt) for n, dt, w, _, _ in fields}
        rec = [sb(f"rec{i}", [P, CH, REC]) for i in range(2)]
        padded, loaded = sem("padded"), sem("loaded")
        joined_dve, joined_act = sem("joined_dve"), sem("joined_act")
        stored = [sem(f"stored{i}") for i in range(2)]
        out = dram["rec"].rearrange("t (e f) -> (t e f)", f=REC).rearrange("(p w) -> p w", p=P)
        with nc.Block() as block:
            @block.sync
            def _(sp):
                sp.wait_ge(padded, len(fields))
                n = 0
                for name, _, w, shift, _ in fields:
                    flat = source[name]
                    if len(flat.shape) == 2:
                        flat = flat.rearrange("e w -> (e w)")
                    for p0, p1 in ((0, 112), (112, P - 1)):
                        a, b = (p0 * C + shift) * w, (p1 * C + shift) * w
                        sp.dma_start(held[name][p0:p1, :], flat[a:b].rearrange("(p c) -> p c", p=p1 - p0)).then_inc(loaded, DMA)
                    a = ((P - 1) * C + shift) * w
                    sp.dma_start(held[name][P - 1:P, 0:(LAST - shift) * w],
                                 flat[a:N_EDGES * w].rearrange("(p c) -> p c", p=1)).then_inc(loaded, DMA)
                for i in range(3):
                    sp.wait_ge(joined_dve, i + 1)
                    sp.wait_ge(joined_act, i + 1)
                    sp.dma_start(out[:, i * CH * REC:(i + 1) * CH * REC],
                                 rec[i % 2][:].rearrange("p c f -> p (c f)")).then_inc(stored[i % 2], DMA)
                sp.wait_ge(stored[0], 2 * DMA)
                sp.wait_ge(stored[1], DMA)

            @block.vector
            def _(dve):
                for name, _, w, shift, value in fields:
                    nc.vector.memset(held[name][:, (LAST - shift) * w:C * w], value).then_inc(padded, 1)
                for i in range(2):
                    nc.vector.memset(rec[i][:, :, R_SH + N_SH:REC], 0.0)
                dve.wait_ge(loaded, 3 * len(fields) * DMA)
                for i in range(3):
                    if i >= 2:
                        dve.wait_ge(stored[i % 2], DMA)
                    for f, name in ((R_SRC, "src"), (R_DST, "dst"), (R_NEXT, "next"), (R_TYPE, "type"), (R_SH, "sh0")):
                        last = nc.vector.tensor_copy(rec[i % 2][:, :, f], held[name][:, i * CH:(i + 1) * CH])
                    last.then_inc(joined_dve, 1)

            @block.scalar
            def _(act):
                act.wait_ge(loaded, 3 * len(fields) * DMA)
                for i in range(3):
                    if i >= 2:
                        act.wait_ge(stored[i % 2], DMA)
                    nc.scalar.copy(rec[i % 2][:, :, R_SH + 1:R_SH + 4],
                                   held["sh1"][:, 3 * i * CH:3 * (i + 1) * CH].rearrange("p (c w) -> p c w", w=3))
                    nc.scalar.copy(rec[i % 2][:, :, R_SH + 4:R_SH + 9],
                                   held["sh2"][:, 5 * i * CH:5 * (i + 1) * CH].rearrange("p (c w) -> p c w", w=5)).then_inc(joined_act, 1)


def merge_path(nc, k, dram):
    CUT = [(c, min(c + 512, T)) for c in range(0, T, 512)]
    with ExitStack() as ctx:
        sb, psum, sem = _scope(nc, ctx, "path")
        last_dst = sb("last_dst", [1, T])
        node_tile = sb("node_tile", [1, T], I32)
        done_at = sb("done_at", [1, T])
        tile_no = sb("tile_no", [1, T])
        done_all = sb("done_all", [P, T])
        before = sb("before", [P, T])
        j_row = sb("j_row", [1, S + 8])
        inc_row = sb("inc_row", [1, S + 8])
        weight = sb("weight", [1, G])
        parts = sb("parts", [1, GROUPS, G])
        word = sb("word", [1, GROUPS])
        tile_row = sb("tile_row", [1, T])
        tile_all = sb("tile_all", [P, T])
        ends = sb("ends", [P, 2])
        spread = psum("spread", [P, 4, BANK])
        spread_tile = psum("spread_tile", [P, 4, BANK])
        ends_int = sb("ends_int", [P, 1], I32)
        loaded, numbered, ready, shown, chain_sem, j_out, j_in = (
            sem(n) for n in ("loaded", "numbered", "ready", "shown", "chain", "j_out", "j_in"))
        with nc.Block() as block:
            @block.sync
            def _(sp):
                with nc.allow_non_contiguous_dma("one word of each edge tile"):
                    sp.dma_start(last_dst[:], dram["rec"][:, (P - 1) * REC + R_DST:(P - 1) * REC + R_DST + 1]
                                 .rearrange("t o -> o t")).then_inc(loaded, DMA)
                    sp.wait_ge(ready, 3)
                    sp.dma_start(dram["j"].rearrange("o (b p) -> p (o b)", p=P), k["j_of"][:]).then_inc(j_out, DMA)
                    sp.dma_start(dram["ends"].rearrange("o p -> p o"), ends_int[:]).then_inc(j_out, DMA)
                    sp.wait_ge(j_out, 2 * DMA)
                    sp.dma_start(j_row[:, 0:S], dram["j"]).then_inc(j_in, DMA)
                    sp.dma_start(k["ends"][:], dram["ends"]).then_inc(j_in, DMA)

            @block.gpsimd
            def _(pool):
                nc.gpsimd.iota(tile_no[:], pattern=[[1, T]], base=0, channel_multiplier=0,
                               allow_small_or_imprecise_dtypes=True).then_inc(numbered, 1)

            @block.vector
            def _(dve):
                chain = Chain(dve, chain_sem)
                dve.wait_ge(loaded, DMA)
                dve.wait_ge(numbered, 1)
                chain.link(nc.vector.tensor_copy(node_tile[:], last_dst[:]))
                chain.link(nc.vector.tensor_single_scalar(node_tile[:], node_tile[:], 7, op=ALU.arith_shift_right))
                nc.vector.tensor_copy(tile_row[:], node_tile[:])
                nc.vector.tensor_tensor(done_at[:], node_tile[:], tile_no[:], ALU.add).then_inc(ready, 1)
                dve.wait_ge(shown, 1)
                for n, (a, b) in enumerate(CUT):
                    nc.vector.tensor_copy(tile_all[:, a:b], spread_tile[:, n, 0:b - a])
                    last = nc.vector.tensor_copy(done_all[:, a:b], spread[:, n, 0:b - a])
                chain.link(last)
                chain.link(nc.vector.tensor_scalar(before[:], tile_all[:], k["step_no"][:, 0:1], 0.0,
                                                   ALU.is_le, ALU.add, accum_out=ends[:, 0:1]))
                chain.link(nc.vector.tensor_scalar(ends[:, 1:2], ends[:, 0:1], float(T - 1), float(LEAD + 1), ALU.min, ALU.add))
                chain.link(nc.vector.tensor_tensor(ends[:, 0:1], ends[:, 1:2], k["step_no"][:, 0:1], ALU.add))
                nc.vector.tensor_copy(ends_int[:], ends[:, 0:1]).then_inc(ready, 1)
                for b in range(BLOCKS):
                    chain.link(nc.vector.tensor_scalar(before[:], done_all[:], k["step_no"][:, b:b + 1], 0.0,
                                                       ALU.is_lt, ALU.add, accum_out=k["t_of"][:, b:b + 1]))
                chain.link(nc.vector.tensor_single_scalar(k["t_of"][:], k["t_of"][:], float(T - 1), op=ALU.min))
                nc.vector.tensor_copy(k["t_index"][:], k["t_of"][:])
                nc.vector.tensor_tensor(k["j_of"][:], k["step_no"][:], k["t_of"][:], ALU.subtract).then_inc(ready, 1)
                for g in range(G):
                    nc.vector.memset(weight[:, g:g + 1], float(2 ** (7 + g)))
                chain.link(nc.vector.memset(j_row[:, S:S + 8], float(S - T + 1)))
                dve.wait_ge(j_in, 2 * DMA)
                chain.link(nc.vector.tensor_tensor(inc_row[:, 0:S], j_row[:, 1:S + 1], j_row[:, 0:S], ALU.subtract))
                chain.link(nc.vector.tensor_tensor(parts[:], inc_row[:, 0:S].rearrange("o (g k) -> o g k", k=G),
                                                   weight[:].unsqueeze(1).to_broadcast([1, GROUPS, G]), ALU.mult))
                chain.link(nc.vector.tensor_reduce(word[:], parts[:], axis=AX_X, op=ALU.add))
                chain.link(nc.vector.tensor_tensor(word[:], word[:], j_row[:, 0:S].rearrange("o (g k) -> o g k", k=G)[:, :, 0], ALU.add))
                nc.vector.memset(k["words"][:, GROUPS:GROUPS + 1], 0)
                nc.vector.tensor_copy(k["words"][:, 0:GROUPS], word[:])

            @block.tensor
            def _(pe):
                pe.wait_ge(ready, 1)
                for n, (a, b) in enumerate(CUT):
                    nc.tensor.matmul(spread_tile[:, n, 0:b - a], k["ones"][0:1, :], tile_row[:, a:b], start=True, stop=True)
                    last = nc.tensor.matmul(spread[:, n, 0:b - a], k["ones"][0:1, :], done_at[:, a:b], start=True, stop=True)
                last.then_inc(shown, 1)


def step_tables(nc, k, dram):
    with ExitStack() as ctx:
        sb, psum, sem = _scope(nc, ctx, "table")
        index = sb("index", [P, 1], U32)
        tile = sb("tile", [P, P, REC])
        flag = sb("flag", [P, P])
        j128 = sb("j128", [P, BLOCKS])
        sh = sb("sh", [P, P, N_SH])
        turned = psum("turned", [P, 4, P])
        turned_sh = psum("turned_sh", [P, 12, P])
        released = sem("released")
        indexed, gathered, filled, flipped, taken_dve, taken_act, chain_sem, sh_out, t_out = (
            sem(n) for n in ("indexed", "gathered", "filled", "flipped", "taken_dve", "taken_act", "chain", "sh_out", "t_out"))
        with nc.Block() as block:
            @block.gpsimd
            def _(pool):
                with pool.Fori(0, BLOCKS) as b:
                    pool.wait_ge(indexed, b + 1)
                    pool.wait_ge(flipped, b)
                    pool.wait_ge(t_out, b * 2 * DMA)
                    pool.sem_inc(released, 1)
                    nc.gpsimd.indirect_dma_start(
                        out=tile[:].rearrange("p e f -> p (e f)"), out_offset=None, in_=dram["rec"],
                        in_offset=bass.IndirectOffsetOnAxis(ap=index[:, 0:1], axis=0)).then_inc(gathered, DMA)

            @block.vector
            def _(dve):
                nc.vector.memset(k["stat"][:, :, 0], 1.0)
                nc.vector.memset(k["drel"][:, S:S + G], -1.0)
                nc.vector.memset(k["type"][:, S:S + G], 0.0)
                nc.vector.memset(k["src"][:, S:S + R * G], 0)
                nc.vector.tensor_single_scalar(j128[:], k["j_of"][:], float(P), op=ALU.mult).then_inc(chain_sem, 1)
                dve.wait_ge(chain_sem, 1)
                with dve.Fori(0, BLOCKS) as b:
                    dve.wait_ge(gathered, b * DMA)
                    nc.vector.tensor_copy(index[:], k["t_index"][:, bass.ds(b, 1)]).then_inc(indexed, 1)
                    dve.wait_ge(gathered, (b + 1) * DMA)
                    nc.vector.tensor_scalar(tile[:, :, R_REL], tile[:, :, R_DST], j128[:, bass.ds(b, 1)], None, ALU.subtract)
                    nc.vector.tensor_tensor(flag[:], tile[:, :, R_DST], tile[:, :, R_NEXT], ALU.not_equal).then_inc(chain_sem, 1)
                    dve.wait_ge(chain_sem, b + 2)
                    nc.vector.scalar_tensor_tensor(out=tile[:, :, R_LAST], in0=tile[:, :, R_SRC], scalar=1.0, in1=flag[:],
                                                   op0=ALU.add, op1=ALU.mult).then_inc(filled, 1)
                    dve.wait_ge(flipped, b + 1)
                    at = bass.ds(b * P, P)
                    nc.vector.tensor_copy(k["src"][:, at], turned[:, 0, :])
                    nc.vector.tensor_copy(k["drel"][:, at], turned[:, 1, :])
                    nc.vector.tensor_copy(k["type"][:, at], turned[:, 2, :])
                    nc.vector.tensor_copy(k["stat"][:, at, 1], turned[:, 3, :]).then_inc(taken_dve, 1)

            @block.tensor
            def _(pe):
                with pe.Fori(0, BLOCKS) as b:
                    pe.wait_ge(filled, b + 1)
                    pe.wait_ge(taken_dve, b)
                    pe.wait_ge(taken_act, b)
                    for n, f in enumerate((R_SRC, R_REL, R_TYPE, R_LAST)):
                        nc.tensor.transpose(turned[:, n, :], tile[:, :, f], k["ident"][:])
                    for f in range(N_SH):
                        last = nc.tensor.transpose(turned_sh[:, f, :], tile[:, :, R_SH + f], k["ident"][:])
                    last.then_inc(flipped, 1)

            @block.scalar
            def _(act):
                with act.Fori(0, BLOCKS) as b:
                    act.wait_ge(flipped, b + 1)
                    act.wait_ge(sh_out, b * DMA)
                    for f0, f1 in ((0, 4), (4, 8), (8, 9)):
                        last = nc.scalar.copy(sh[:, :, f0:f1].rearrange("p s f -> p f s"), turned_sh[:, f0:f1, :])
                    last.then_inc(taken_act, 1)

            @block.sync
            def _(sp):
                with sp.Fori(0, BLOCKS) as b, nc.allow_non_contiguous_dma("one field of the records"):
                    sp.wait_ge(filled, b + 1)
                    sp.dma_start(dram["dst_t"][:, bass.ds(b * P, P)], tile[:, :, R_DST]).then_inc(t_out, DMA)
                    sp.dma_start(dram["drel_t"][:, bass.ds(b * P, P)], tile[:, :, R_REL]).then_inc(t_out, DMA)
                    sp.wait_ge(taken_act, b + 1)
                    sp.dma_start(dram["sh"][:, bass.ds(b * P * N_SH, P * N_SH)], sh[:].rearrange("p s f -> p (s f)")).then_inc(sh_out, DMA)
                sp.dma_start(dram["sh"][:, S * N_SH:(S + R * G) * N_SH], k["zeros"][:, 0:R * G * N_SH]).then_inc(sh_out, DMA)
                sp.wait_ge(sh_out, (BLOCKS + 1) * DMA)
                sp.wait_ge(t_out, 2 * BLOCKS * DMA)


def _one_hot(nc, k, out, first, n=G):
    return nc.vector.tensor_tensor(out[:], k["iota"][:].unsqueeze(1).to_broadcast([P, n, P]),
                                   k["drel"][:, bass.ds(first, n)].unsqueeze(2).to_broadcast([P, n, P]), ALU.is_equal)


def _tile_registers(nc, engine, k, group):
    word = engine.value_load(k["words"][0:1, bass.ds(group, 1)], min_val=0, max_val=(1 << (7 + G)) - 1)
    tiles = [engine.snap(nc.s_assert_within(word & 127, 0, JP - 1, skip_runtime_bounds_check_because="a node tile"))]
    for g in range(1, G + 1):
        tiles.append(engine.snap(nc.s_assert_within(tiles[-1] + ((word >> (6 + g)) & 1), 0, JP - 1,
                                                    skip_runtime_bounds_check_because="a node tile")))
    return tiles


def _add_step(nc, pe, tile, accumulator, width, cleared, added, onehot, rows):
    pe.wait_ge(cleared, tile + 1)
    nc.tensor.matmul(accumulator[:, bass.ds((tile & 1) * BANK, width)], onehot, rows,
                     start=False, stop=True, skip_group_check=True).then_inc(added, 1)


def _take_tiles(nc, act, k, accumulator, width, cleared, added, copied, checked, target, before_copy=None):
    for h in range(2):
        nc.scalar.copy(accumulator[:, h * BANK:h * BANK + width], k["zeros"][:, 0:width]).then_inc(cleared, 1)
    with act.Fori(0, TILES // 2) as i:
        for h in range(2):
            end = act.value_load(k["ends"][0:1, bass.ds(i * 2 + h, 1)], min_val=1, max_val=S + LEAD)
            act.wait_ge(added, end)
            if before_copy:
                before_copy(i, h)
            act.sem_inc(checked, 1)
            nc.scalar.copy(target(i, h), accumulator[:, h * BANK:h * BANK + width]).then_inc(copied, 1)
            act.wait_ge(copied, i * 2 + h + 1)
            nc.scalar.copy(accumulator[:, h * BANK:h * BANK + width], k["zeros"][:, 0:width]).then_inc(cleared, 1)


def _take_if_last(nc, act, k, step, tile, ends, accumulator, taken, width, cleared, added, copied, checked, saved):
    with act.If(ends > 0):
        act.wait_ge(added, step + 1 + LEAD)
        act.wait_ge(saved, tile * DMA)
        act.sem_inc(checked, 1)
        nc.scalar.copy(taken[:, bass.ds((tile & 1) * BANK, width)],
                       accumulator[:, bass.ds((tile & 1) * BANK, width)]).then_inc(copied, 1)
        act.wait_ge(copied, tile + 1)
        act.sem_inc(checked, 1)
        nc.scalar.copy(accumulator[:, bass.ds((tile & 1) * BANK, width)], k["zeros"][:, 0:width]).then_inc(cleared, 1)


def _save_tiles(sp, taken, totals, width, copied, saved, passed):
    sp.sem_inc(saved, DMA)
    with sp.Fori(0, TILES // 2) as i:
        for h in range(2):
            sp.wait_ge(copied, i * 2 + h + 1)
            sp.dma_start(totals[:, bass.ds((i * 2 + h) * width, width)],
                         taken[:, h * BANK:h * BANK + width]).then_inc(saved, DMA)
            sp.wait_ge(saved, (i * 2 + h + 2) * DMA)
            sp.sem_inc(passed, 1)


def _stage(nc, k, staged, group, slot):
    return nc.vector.tensor_copy(staged[:, slot, :], k["src"][:, bass.ds(group * G, G)])


def _gather_rows(nc, pool, table, staged, ring, indexed, released, gathered, slot_waits):
    with pool.Fori(0, ITERS) as i:
        for q in range(R):
            pool.wait_ge(indexed, i * R + q + 1)
            slot_waits(i, q)
            pool.sem_inc(released, 1)
            for g in range(G):
                nc.gpsimd.indirect_dma_start(
                    out=ring[:, q, g, :], out_offset=None, in_=table,
                    in_offset=bass.IndirectOffsetOnAxis(ap=staged[:, q, g:g + 1], axis=0)).then_inc(gathered[q], DMA)


def sum_pass(nc, k, name, table, sums, width, rows=None):
    with ExitStack() as ctx:
        sb, psum, sem = _scope(nc, ctx, name)
        if rows is None:
            staged = sb("staged", [P, R, G], U32)
            ring = sb("ring", [P, R, G, width])
            gathered = [sem(f"gathered{q}") for q in range(R)]
        onehot = [sb(f"onehot{h}", [P, G, P]) for h in range(2)]
        accumulator = psum("accumulator", [P, 2 * BANK])
        indexed, made, released, added, cleared, copied, checked = (
            sem(n) for n in ("indexed", "made", "released", "added", "cleared", "copied", "checked"))
        with nc.Block() as block:
            if rows is None:
                @block.gpsimd
                def _(pool):
                    _gather_rows(nc, pool, table, staged, ring, indexed, released, gathered,
                                 lambda i, q: pool.wait_ge(added, (i * R + q) * G))

            @block.vector
            def _(dve):
                if rows is None:
                    for q in range(R - 1):
                        _stage(nc, k, staged, q, q).then_inc(indexed, 1)
                _one_hot(nc, k, onehot[0], 0).then_inc(made, 1)
                with dve.Fori(0, ITERS) as i:
                    for q in range(R):
                        dve.wait_ge(added, (i * R + q) * G + LEAD)
                        _one_hot(nc, k, onehot[(q + 1) % 2], (i * R + q + 1) * G).then_inc(made, 1)
                        if rows is None:
                            _stage(nc, k, staged, i * R + q + R - 1, (q + R - 1) % R).then_inc(indexed, 1)

            @block.tensor
            def _(pe):
                pe.sem_inc(added, LEAD)
                with pe.Fori(0, ITERS) as i:
                    for q in range(R):
                        tiles = _tile_registers(nc, pe, k, i * R + q)
                        pe.wait_ge(made, i * R + q + 1)
                        if rows is None:
                            pe.wait_ge(gathered[q], (i + 1) * G * DMA)
                        for g in range(G):
                            row = ring[:, q, g, :] if rows is None else (
                                rows[:, bass.ds((i * R + q) * G + g, 1), :].rearrange("p s w -> p (s w)"))
                            _add_step(nc, pe, tiles[g], accumulator, width, cleared, added, onehot[q % 2][:, g, :], row)

            @block.scalar
            def _(act):
                _take_tiles(nc, act, k, accumulator, width, cleared, added, copied, checked,
                            lambda i, h: sums[:, bass.ds(i * 2 + h, 1), :].rearrange("p j f -> p (j f)"))


def node_statistics(nc, k):
    with ExitStack() as ctx:
        sb, _, sem = _scope(nc, ctx, "stat")
        total = sb("total", [P, JP, 2])
        last = sb("last", [P, JP])
        chain_sem, inverted = sem("chain"), sem("inverted")
        on_vector(nc, "stat_clear", [lambda: nc.vector.memset(total[:], 0.0)])
        sum_pass(nc, k, "stat_sum", None, total, 2, rows=k["stat"])
        with nc.Block() as block:
            @block.vector
            def _(dve):
                chain = Chain(dve, chain_sem)
                nc.vector.tensor_copy(k["degree"][:], total[:, :, 0])
                chain.link(nc.vector.tensor_scalar(last[:], total[:, :, 1], -1.0, 0.0, ALU.add, ALU.max))
                nc.vector.tensor_copy(k["last_index"][:], last[:])
                chain.link(nc.vector.tensor_single_scalar(k["dinv"][:], total[:, :, 0], 1.0, op=ALU.add))
                nc.vector.reciprocal(k["dinv"][:], k["dinv"][:]).then_inc(inverted, 1)

            @block.scalar
            def _(act):
                act.wait_ge(inverted, 1)
                nc.scalar.activation(k["dinv"][:], k["dinv"][:], ACT.Sqrt)


def load_x(nc, io, k):
    with ExitStack() as ctx:
        _, _, sem = _scope(nc, ctx, "x")
        cleared, loaded = sem("cleared"), sem("loaded")
        with nc.Block() as block:
            @block.vector
            def _(dve):
                nc.vector.memset(k["x"][:], 0.0).then_inc(cleared, 1)

            @block.sync
            def _(sp):
                sp.wait_ge(cleared, 1)
                sp.dma_start(k["x"][:, 0:J - 1, :], _node_rows(io["x"], 0, J - 1)).then_inc(loaded, DMA)
                sp.dma_start(k["x"][0:LAST_TILE_ROWS, J - 1, :], io["x"][(J - 1) * P:N_NODES, :]).then_inc(loaded, DMA)
                sp.wait_ge(loaded, 2 * DMA)


def _spread(a, n):
    return a.unsqueeze(2).to_broadcast([P, JP, n])


def norm_relu(nc, k, name, h):
    x = k["x"]
    with ExitStack() as ctx:
        sb, _, sem = _scope(nc, ctx, name)
        centered = sb("centered", [P, JP, D])
        mean = sb("mean", [P, JP])
        var = sb("var", [P, JP])
        rooted, chain_sem, summed = sem("rooted"), sem("chain"), sem("summed")
        with nc.Block() as block:
            @block.vector
            def _(dve):
                chain = Chain(dve, chain_sem)
                chain.link(nc.vector.tensor_reduce(mean[:], x[:], axis=AX_X, op=ALU.add))
                chain.link(nc.vector.tensor_single_scalar(mean[:], mean[:], 1.0 / D, op=ALU.mult))
                chain.link(nc.vector.tensor_tensor(centered[:], x[:], _spread(mean[:], D), ALU.subtract))
                chain.link(nc.vector.tensor_tensor(h[:], centered[:], centered[:], ALU.mult))
                chain.link(nc.vector.tensor_reduce(var[:], h[:], axis=AX_X, op=ALU.add))
                nc.vector.tensor_scalar(var[:], var[:], 1.0 / D, 1e-5, ALU.mult, ALU.add).then_inc(summed, 1)
                dve.wait_ge(rooted, 1)
                chain.link(nc.vector.reciprocal(var[:], var[:]))
                chain.link(nc.vector.tensor_tensor(centered[:], centered[:], _spread(var[:], D), ALU.mult))
                nc.vector.tensor_single_scalar(h[:], centered[:], 0.0, op=ALU.max)

            @block.scalar
            def _(act):
                act.wait_ge(summed, 1)
                nc.scalar.activation(var[:], var[:], ACT.Sqrt).then_inc(rooted, 1)


def store_table(nc, name, table, a, width):
    with ExitStack() as ctx:
        _, _, sem = _scope(nc, ctx, name)
        stored = sem("stored")
        with nc.Block() as block:
            @block.sync
            def _(sp):
                sp.dma_start(_node_rows(table, 0, J), a[:, 0:J, 0:width]).then_inc(stored, DMA)
                sp.wait_ge(stored, DMA)


def node_linear(nc, k, name, source, n, parts, weights, out, load=None):
    width = parts * P
    fo = weights.shape[2]
    assert n % 2 == 0
    from_dram = load
    with ExitStack() as ctx:
        sb, psum, sem = _scope(nc, ctx, name)
        chunk = [sb(f"chunk{h}", [P, width]) for h in range(2)]
        turned = [sb(f"turned{h}", [P, parts, P]) for h in range(2)]
        flipped_ps = psum("flipped_ps", [P, 2, 4, P])
        product = psum("product", [P, 2, 512])
        staged = [sem(f"staged{h}") for h in range(2)]
        flipped = [sem(f"flipped{h}") for h in range(2)]
        copied = [sem(f"copied{h}") for h in range(2)]
        multiplied = [sem(f"multiplied{h}") for h in range(2)]
        taken = [sem(f"taken{h}") for h in range(2)]
        per_stage = DMA if from_dram else 1
        with nc.Block() as block:
            if from_dram:
                @block.sync
                def _(sp):
                    with sp.Fori(0, n // 2) as i:
                        for h in range(2):
                            sp.wait_ge(flipped[h], i)
                            sp.dma_start(chunk[h][:], source[:, bass.ds((i * 2 + h) * width, width)]).then_inc(staged[h], DMA)
            else:
                @block.gpsimd
                def _(pool):
                    with pool.Fori(0, n // 2) as i:
                        for h in range(2):
                            pool.wait_ge(flipped[h], i)
                            nc.gpsimd.tensor_copy(chunk[h][:], source[:, bass.ds((i * 2 + h) * width, width)]).then_inc(staged[h], 1)

            @block.tensor
            def _(pe):
                with pe.Fori(0, n // 2) as i:
                    for h in range(2):
                        pe.wait_ge(staged[h], (i + 1) * per_stage)
                        pe.wait_ge(copied[h], i)
                        for c in range(parts):
                            last = nc.tensor.transpose(flipped_ps[:, h, c, :], chunk[h][:, c * P:(c + 1) * P], k["ident"][:])
                        last.then_inc(flipped[h], 1)
                    for h in range(2):
                        pe.wait_ge(copied[h], i + 1)
                        pe.wait_ge(taken[h], i)
                        for c in range(parts):
                            last = nc.tensor.matmul(product[:, h, 0:fo], turned[h][:, c, :], weights[:, c, :],
                                                    start=(c == 0), stop=(c == parts - 1))
                        last.then_inc(multiplied[h], 1)

            @block.scalar
            def _(act):
                with act.Fori(0, n // 2) as i:
                    for h in range(2):
                        act.wait_ge(flipped[h], i + 1)
                        act.wait_ge(multiplied[h], i)
                        nc.scalar.copy(turned[h][:], flipped_ps[:, h, 0:parts, :]).then_inc(copied[h], 1)

            @block.vector
            def _(dve):
                with dve.Fori(0, n // 2) as i:
                    for h in range(2):
                        dve.wait_ge(multiplied[h], i + 1)
                        nc.vector.tensor_copy(out[:, bass.ds((i * 2 + h) * fo, fo)], product[:, h, 0:fo]).then_inc(taken[h], 1)


def load_diagonal(nc, name, w, pieces):
    with ExitStack() as ctx:
        _, _, sem = _scope(nc, ctx, name)
        cleared, loaded = sem("cleared"), sem("loaded")
        with nc.Block() as block:
            @block.vector
            def _(dve):
                nc.vector.memset(w[:], 0.0).then_inc(cleared, 1)

            @block.sync
            def _(sp):
                sp.wait_ge(cleared, 1)
                for q in range(4):
                    at = 0
                    for piece in pieces:
                        f = piece.shape[1]
                        sp.dma_start(w[D * q:D * (q + 1), q, at:at + f], piece).then_inc(loaded, DMA)
                        at += f
                sp.wait_ge(loaded, 4 * len(pieces) * DMA)


def load_rows(nc, name, pairs):
    with ExitStack() as ctx:
        _, _, sem = _scope(nc, ctx, name)
        loaded = sem("loaded")
        with nc.Block() as block:
            @block.sync
            def _(sp):
                for a, b in pairs:
                    sp.dma_start(a, b).then_inc(loaded, DMA)
                sp.wait_ge(loaded, len(pairs) * DMA)


def on_vector(nc, name, steps):
    with ExitStack() as ctx:
        _, _, sem = _scope(nc, ctx, name)
        chain_sem = sem("chain")
        with nc.Block() as block:
            @block.vector
            def _(dve):
                chain = Chain(dve, chain_sem)
                for step in steps:
                    chain.link(step())


def gcn(nc, io, k, dram):
    v = nc.vector
    with ExitStack() as ctx:
        sb, _, _ = _scope(nc, ctx, "gcn")
        h = sb("h", [P, JP, D])
        norm_relu(nc, k, "gcn_norm", h)
        on_vector(nc, "gcn_scale0", [lambda: v.tensor_tensor(h[:], h[:], _spread(k["dinv"][:], D), ALU.mult)])
        store_table(nc, "gcn_table0", dram["tab32"], h, D)
        with ExitStack() as inner:
            sbi, _, _ = _scope(nc, inner, "gcn1")
            sums = sbi("sums", [P, JP, D])
            on_vector(nc, "gcn_clear0", [lambda: v.memset(sums[:, TILES:JP, :], 0.0)])
            sum_pass(nc, k, "gcn_sum0", dram["tab32"], sums, D)
            wide = sbi("wide", [P, JP, HID])
            w1 = sbi("w1", [P, 1, 4 * HID])
            b1 = sbi("b1", [P, HID])
            load_diagonal(nc, "gcn_w1", w1[:].rearrange("p o (q f) -> p (o q) f", q=4), [io["L0_gnn_W1"]])
            load_rows(nc, "gcn_b1", [(b1[:], io["L0_gnn_b1"].unsqueeze(0).to_broadcast([P, HID]))])
            on_vector(nc, "gcn_self0", [lambda: v.tensor_tensor(sums[:], sums[:], h[:], ALU.add)])
            node_linear(nc, k, "gcn_lin1", sums[:].rearrange("p j f -> p (j f)"), JP // 4, 1, w1, wide[:].rearrange("p j f -> p (j f)"))
            on_vector(nc, "gcn_act1", [
                lambda: v.tensor_tensor(wide[:], wide[:], _spread(k["dinv"][:], HID), ALU.mult),
                lambda: v.tensor_tensor(wide[:], wide[:], b1[:].unsqueeze(1).to_broadcast([P, JP, HID]), ALU.add),
                lambda: v.tensor_single_scalar(wide[:], wide[:], 0.0, op=ALU.max),
                lambda: v.tensor_tensor(wide[:], wide[:], _spread(k["dinv"][:], HID), ALU.mult)])
            store_table(nc, "gcn_table1", dram["tab128"], wide, HID)
        with ExitStack() as inner:
            sbi, _, _ = _scope(nc, inner, "gcn2")
            sums = sbi("sums", [P, JP, HID])
            on_vector(nc, "gcn_clear1", [lambda: v.memset(sums[:, TILES:JP, :], 0.0)])
            sum_pass(nc, k, "gcn_sum1", dram["tab128"], sums, HID)
            w2 = sbi("w2", [P, 1, HID])
            w3 = sbi("w3", [P, 1, D])
            b2 = sbi("b2", [P, HID])
            load_rows(nc, "gcn_w2", [(w2[:, 0, :], io["L0_gnn_W2"]), (w3[:, 0, :], io["L0_gnn_W3"]),
                                     (b2[:], io["L0_gnn_b2"].unsqueeze(0).to_broadcast([P, HID]))])
            load_wide = sbi("own", [P, 14, HID])
            with ExitStack() as inner2:
                _, _, sem = _scope(nc, inner2, "gcn_self1")
                fetched, added = sem("fetched"), sem("added")
                with nc.Block() as block:
                    @block.sync
                    def _(sp):
                        for c in range(J // 14):
                            sp.wait_ge(added, c)
                            sp.dma_start(load_wide[:], _node_rows(dram["tab128"], 14 * c, 14 * (c + 1))).then_inc(fetched, DMA)

                    @block.vector
                    def _(dve):
                        for c in range(J // 14):
                            dve.wait_ge(fetched, (c + 1) * DMA)
                            at = slice(14 * c, 14 * (c + 1))
                            v.tensor_tensor(sums[:, at, :], sums[:, at, :], load_wide[:], ALU.add).then_inc(added, 1)
            flat = sums[:].rearrange("p j f -> p (j f)")
            node_linear(nc, k, "gcn_lin2", flat, J, 1, w2, flat)
            on_vector(nc, "gcn_act2", [
                lambda: v.tensor_tensor(sums[:], sums[:], _spread(k["dinv"][:], HID), ALU.mult),
                lambda: v.tensor_tensor(sums[:], sums[:], b2[:].unsqueeze(1).to_broadcast([P, JP, HID]), ALU.add),
                lambda: v.tensor_single_scalar(sums[:], sums[:], 0.0, op=ALU.max),
                lambda: v.tensor_tensor(sums[:], sums[:], _spread(k["dinv"][:], HID), ALU.mult),
                lambda: v.memset(h[:], 0.0)])
            node_linear(nc, k, "gcn_lin3", flat, J, 1, w3, h[:].rearrange("p j f -> p (j f)"))
            store_table(nc, "gcn_table2", dram["tab32"], h, D)
        sums = sb("sums2", [P, JP, D])
        on_vector(nc, "gcn_clear2", [lambda: v.memset(sums[:, TILES:JP, :], 0.0)])
        sum_pass(nc, k, "gcn_sum2", dram["tab32"], sums, D)
        b3 = sb("b3", [P, D])
        load_rows(nc, "gcn_b3", [(b3[:], io["L0_gnn_b3"].unsqueeze(0).to_broadcast([P, D]))])
        on_vector(nc, "gcn_out", [
            lambda: v.tensor_tensor(sums[:], sums[:], h[:], ALU.add),
            lambda: v.tensor_tensor(sums[:], sums[:], _spread(k["dinv"][:], D), ALU.mult),
            lambda: v.tensor_tensor(sums[:], sums[:], b3[:].unsqueeze(1).to_broadcast([P, JP, D]), ALU.add),
            lambda: v.tensor_single_scalar(sums[:], sums[:], 0.0, op=ALU.max),
            lambda: v.tensor_tensor(k["x"][:], k["x"][:], sums[:], ALU.add)])


def score_pass(nc, k, dram, q_nodes, score):
    with ExitStack() as ctx:
        sb, psum, sem = _scope(nc, ctx, "score")
        staged = sb("staged", [P, R, G], U32)
        ring = sb("ring", [P, R, G, 2 * D])
        onehot = [sb(f"onehot{h}", [P, G, P]) for h in range(2)]
        onehot_t = [sb(f"onehot_t{h}", [P, G, P]) for h in range(2)]
        product = [sb(f"product{h}", [P, G, D]) for h in range(2)]
        flipped_ps = psum("flipped_ps", [P, 2, G, P])
        q_edge = psum("q_edge", [P, 2, 512])
        indexed, made, reduced, released = sem("indexed"), sem("made"), sem("reduced"), sem("released")
        looked_up = [sem(f"looked_up{q}") for q in range(R)]
        gathered = [sem(f"gathered{q}") for q in range(R)]
        flipped = [sem(f"flipped{q}") for q in range(R)]
        turned = [sem(f"turned{q}") for q in range(R)]
        used = [sem(f"used{q}") for q in range(R)]
        spilled = [sem(f"spilled{q}") for q in range(R)]
        with nc.Block() as block:
            @block.scalar
            def _(act):
                with act.Fori(0, ITERS) as i:
                    for q in range(R):
                        act.wait_ge(flipped[q], i + 1)
                        act.wait_ge(looked_up[(q - 2) % R], i + (q >= 2))
                        nc.scalar.copy(onehot_t[q % 2][:], flipped_ps[:, q % 2, :, :]).then_inc(turned[q], 1)

            @block.gpsimd
            def _(pool):
                with pool.Fori(0, ITERS) as i:
                    for q in range(R):
                        pool.wait_ge(indexed, i * R + q + 1)
                        pool.wait_ge(used[q], i)
                        pool.wait_ge(spilled[q], i * DMA)
                        pool.sem_inc(released, 1)
                        for g in range(G):
                            nc.gpsimd.indirect_dma_start(
                                out=ring[:, q, g, :], out_offset=None, in_=dram["tab64"],
                                in_offset=bass.IndirectOffsetOnAxis(ap=staged[:, q, g:g + 1], axis=0)).then_inc(gathered[q], DMA)

            @block.vector
            def _(dve):
                for q in range(R - 1):
                    _stage(nc, k, staged, q, q).then_inc(indexed, 1)
                _one_hot(nc, k, onehot[0], 0).then_inc(made, 1)
                with dve.Fori(0, ITERS) as i:
                    for q in range(R):
                        dve.wait_ge(flipped[(q - 1) % R], i + (q >= 1))
                        _one_hot(nc, k, onehot[(q + 1) % 2], (i * R + q + 1) * G).then_inc(made, 1)
                        _stage(nc, k, staged, i * R + q + R - 1, (q + R - 1) % R).then_inc(indexed, 1)
                        dve.wait_ge(looked_up[q], i + 1)
                        dve.wait_ge(gathered[q], (i + 1) * G * DMA)
                        nc.vector.tensor_tensor(product[q % 2][:], q_edge[:, q % 2, 0:G * D].rearrange("p (g f) -> p g f", f=D),
                                                ring[:, q, :, 0:D], ALU.mult).then_inc(used[q], 1)
                        dve.wait_ge(used[q], i + 1)
                        nc.vector.tensor_reduce(score[:, bass.ds((i * R + q) * G, G), :],
                                                product[q % 2][:].rearrange("p g (h d) -> p g h d", d=DHEAD),
                                                axis=AX_X, op=ALU.add).then_inc(reduced, 1)

            @block.tensor
            def _(pe):
                with pe.Fori(0, ITERS) as i:
                    for q in range(R):
                        pe.wait_ge(made, i * R + q + 1)
                        pe.wait_ge(turned[(q - 2) % R], i + (q >= 2))
                        for g in range(G):
                            last = nc.tensor.transpose(flipped_ps[:, q % 2, g, :], onehot[q % 2][:, g, :], k["ident"][:])
                        last.then_inc(flipped[q], 1)
                        tiles = _tile_registers(nc, pe, k, i * R + q)
                        pe.wait_ge(turned[q], i + 1)
                        pe.wait_ge(used[(q - 2) % R], i + (q >= 2))
                        for g in range(G):
                            last = nc.tensor.matmul(q_edge[:, q % 2, g * D:(g + 1) * D], onehot_t[q % 2][:, g, :],
                                                    q_nodes[:, bass.ds(tiles[g] * D, D)], start=True, stop=True)
                        last.then_inc(looked_up[q], 1)

            @block.sync
            def _(sp):
                with sp.Fori(0, ITERS) as i:
                    for q in range(R):
                        sp.wait_ge(gathered[q], (i + 1) * G * DMA)
                        sp.dma_start(dram["kv"][:, bass.ds((i * R + q) * G * 2 * D, G * 2 * D)],
                                     ring[:, q, :, :].rearrange("p g f -> p (g f)")).then_inc(spilled[q], DMA)
                for q in range(R):
                    sp.wait_ge(spilled[q], ITERS * DMA)


def softmax_weights(nc, k, dram, score):
    SE = BLOCKS * P
    with ExitStack() as ctx:
        sb, psum, sem = _scope(nc, ctx, "softmax")
        dst = sb("dst", [P, BLOCKS, P])
        rel = sb("rel", [P, BLOCKS, P])
        reset = sb("reset", [P, BLOCKS, P])
        by_step = sb("by_step", [P, HEADS, BLOCKS, P])
        back = sb("back", [P, BLOCKS, P])
        edge_of = sb("edge_of", [P, BLOCKS, 4, HEADS])
        carry = [sb(f"carry{n}", [HEADS, S]) for n in range(4)]
        resets = [sb(f"resets{n}", [HEADS, S]) for n in range(3)]
        spread = sb("spread", [P, BLOCKS, 2, HEADS])
        loaded = sem("loaded")
        with nc.Block() as block:
            @block.sync
            def _(sp):
                sp.dma_start(dst[:].rearrange("p b e -> p (b e)"), dram["dst_t"]).then_inc(loaded, DMA)
                sp.dma_start(rel[:].rearrange("p b e -> p (b e)"), dram["drel_t"]).then_inc(loaded, DMA)
                sp.wait_ge(loaded, 2 * DMA)
        v = nc.vector

        def limits(a):
            return lambda: v.tensor_scalar(a, a, 2 * BIG, -BIG, ALU.mult, ALU.add)

        on_vector(nc, "softmax_valid", [
            lambda: v.tensor_single_scalar(reset[:], rel[:], 0.0, op=ALU.is_ge),
            lambda: v.tensor_single_scalar(back[:], rel[:], float(P), op=ALU.is_lt),
            lambda: v.tensor_tensor(rel[:], reset[:], back[:], ALU.mult), limits(rel[:])])
        with ExitStack() as inner:
            _, psum_in, sem_in = _scope(nc, inner, "softmax_turn")
            turned = psum_in("turned", [P, 2, HEADS, P])
            flipped, taken = sem_in("flipped"), sem_in("taken")
            with nc.Block() as block:
                @block.tensor
                def _(pe):
                    for b in range(BLOCKS):
                        if b >= 2:
                            pe.wait_ge(taken, b - 1)
                        for h in range(HEADS):
                            last = nc.tensor.transpose(turned[:, b % 2, h, :], score[:, b * P:(b + 1) * P, h], k["ident"][:])
                        last.then_inc(flipped, 1)

                @block.vector
                def _(dve):
                    for b in range(BLOCKS):
                        dve.wait_ge(flipped, b + 1)
                        v.scalar_tensor_tensor(out=by_step[:, :, b, :], in0=turned[:, b % 2, :, :], scalar=1.0 / math.sqrt(DHEAD),
                                               in1=rel[:, b, :].unsqueeze(1).to_broadcast([P, HEADS, P]),
                                               op0=ALU.mult, op1=ALU.min).then_inc(taken, 1)
        tops = sb("tops", [P, HEADS, BLOCKS, P])
        flat = lambda a: a.rearrange("p b e -> p (b e)")
        steps = [lambda: v.memset(reset[:], 0.0),
                 lambda: v.tensor_tensor(reset[:, :, 1:P], dst[:, :, 1:P], dst[:, :, 0:P - 1], ALU.is_equal), limits(reset[:])]
        steps += [lambda h=h: v.tensor_tensor_scan(flat(tops[:, h]), flat(reset[:]), flat(by_step[:, h]), -BIG, ALU.min, ALU.max)
                  for h in range(HEADS)]
        steps += [lambda h=h: v.tensor_copy(edge_of[:, :, 0, h], tops[:, h, :, P - 1]) for h in range(HEADS)]
        steps += [lambda: v.memset(reset[:], 0.0),
                  lambda: v.tensor_tensor(reset[:, :, 0:P - 1], dst[:, :, 1:P], dst[:, :, 0:P - 1], ALU.is_equal), limits(reset[:])]
        for h in range(HEADS):
            steps += [lambda h=h: v.tensor_tensor_scan(flat(back[:])[:, ::-1], flat(reset[:])[:, ::-1], flat(by_step[:, h])[:, ::-1],
                                                       -BIG, ALU.min, ALU.max),
                      lambda h=h: v.tensor_copy(edge_of[:, :, 1, h], back[:, :, 0]),
                      lambda h=h: v.tensor_tensor(tops[:, h], tops[:, h], back[:], ALU.max),
                      lambda h=h: v.tensor_copy(edge_of[:, :, 2, h], dst[:, :, 0]),
                      lambda h=h: v.tensor_copy(edge_of[:, :, 3, h], dst[:, :, P - 1])]
        on_vector(nc, "softmax_scan", steps)
        with ExitStack() as inner:
            _, psum_in, sem_in = _scope(nc, inner, "softmax_rows")
            rows = psum_in("rows", [HEADS, 4, 4, P])
            flipped, taken = sem_in("flipped"), sem_in("taken")
            with nc.Block() as block:
                @block.tensor
                def _(pe):
                    for n in range(4):
                        if n:
                            pe.wait_ge(taken, n)
                        for b in range(BLOCKS):
                            last = nc.tensor.transpose(rows[:, b // 4, b % 4, :], edge_of[:, b, n, :], k["ident"][:])
                        last.then_inc(flipped, 1)

                @block.vector
                def _(dve):
                    for n in range(4):
                        dve.wait_ge(flipped, n + 1)
                        v.tensor_copy(carry[n][:], rows[:].rearrange("h a b e -> h (a b e)")[:, 0:S]).then_inc(taken, 1)
        last_max, first_max, first_dst, last_dst = (c[:] for c in carry)
        cont, whole, limit = (c[:] for c in resets)
        on_vector(nc, "softmax_carry", [
            lambda: v.tensor_tensor(whole, first_dst, last_dst, ALU.is_equal),
            lambda: v.memset(cont, 0.0),
            lambda: v.tensor_tensor(cont[:, 1:S], first_dst[:, 1:S], last_dst[:, 0:S - 1], ALU.is_equal),
            lambda: v.tensor_tensor(limit, whole, cont, ALU.mult), limits(limit),
            lambda: v.tensor_tensor_scan(first_dst, limit, last_max, -BIG, ALU.min, ALU.max),
            lambda: v.tensor_copy(limit, whole),
            lambda: v.memset(limit[:, S - 1:S], 0.0),
            lambda: v.tensor_tensor(limit[:, 0:S - 1], whole[:, 0:S - 1], cont[:, 1:S], ALU.mult), limits(limit),
            lambda: v.tensor_tensor_scan(last_dst[:, ::-1], limit[:, ::-1], first_max[:, ::-1], -BIG, ALU.min, ALU.max),
            limits(cont),
            lambda: v.memset(last_max, -BIG), lambda: v.memset(first_max, -BIG),
            lambda: v.tensor_tensor(last_max[:, 1:S], first_dst[:, 0:S - 1], cont[:, 1:S], ALU.min),
            lambda: v.tensor_tensor(first_max[:, 0:S - 1], last_dst[:, 1:S], cont[:, 1:S], ALU.min)])
        with ExitStack() as inner:
            _, psum_in, sem_in = _scope(nc, inner, "softmax_columns")
            columns = psum_in("columns", [P, BLOCKS, 2, HEADS])
            flipped = sem_in("flipped")
            with nc.Block() as block:
                @block.tensor
                def _(pe):
                    for b in range(BLOCKS):
                        for n in range(2):
                            last = nc.tensor.transpose(columns[:, b, n, :], carry[n][:, b * P:(b + 1) * P], k["ident"][0:HEADS, 0:HEADS])
                    last.then_inc(flipped, 1)

                @block.vector
                def _(dve):
                    dve.wait_ge(flipped, 1)
                    v.tensor_copy(spread[:], columns[:])
        steps = []
        for n, e in ((0, 0), (1, P - 1)):
            steps += [lambda e=e: v.tensor_tensor(reset[:], dst[:], dst[:, :, e:e + 1].to_broadcast([P, BLOCKS, P]), ALU.is_equal),
                      limits(reset[:])]
            steps += [lambda b=b, h=h, n=n: v.scalar_tensor_tensor(out=tops[:, h, b, :], in0=reset[:, b, :], scalar=spread[:, b, n, h:h + 1],
                                                                   in1=tops[:, h, b, :], op0=ALU.min, op1=ALU.max)
                      for b in range(BLOCKS) for h in range(HEADS)]
        steps += [lambda: v.tensor_tensor(by_step[:], by_step[:], tops[:], ALU.subtract)]
        on_vector(nc, "softmax_top", steps)
        with ExitStack() as inner:
            _, psum_in, sem_in = _scope(nc, inner, "softmax_exp")
            turned = psum_in("turned", [P, 2, HEADS, P])
            raised, flipped, taken = sem_in("raised"), sem_in("flipped"), sem_in("taken")
            with nc.Block() as block:
                @block.scalar
                def _(act):
                    for b in range(BLOCKS):
                        nc.scalar.activation(tops[:, :, b, :], by_step[:, :, b, :], ACT.Exp).then_inc(raised, 1)

                @block.tensor
                def _(pe):
                    for b in range(BLOCKS):
                        pe.wait_ge(raised, b + 1)
                        if b >= 2:
                            pe.wait_ge(taken, b - 1)
                        for h in range(HEADS):
                            last = nc.tensor.transpose(turned[:, b % 2, h, :], tops[:, h, b, :], k["ident"][:])
                        last.then_inc(flipped, 1)

                @block.vector
                def _(dve):
                    for b in range(BLOCKS):
                        dve.wait_ge(flipped, b + 1)
                        v.tensor_copy(score[:, b * P:(b + 1) * P, :], turned[:, b % 2, :, :].rearrange("p h e -> p e h")).then_inc(taken, 1)


def value_pass(nc, k, dram, weight, sums):
    width = D + HEADS
    with ExitStack() as ctx:
        sb, psum, sem = _scope(nc, ctx, "value")
        ring = sb("ring", [P, R, G, 2 * D])
        message = [sb(f"message{h}", [P, G, width]) for h in range(2)]
        onehot = [sb(f"onehot{h}", [P, G, P]) for h in range(2)]
        accumulator = psum("accumulator", [P, 2 * BANK])
        made, added, cleared, copied, checked, messaged = (
            sem(n) for n in ("made", "added", "cleared", "copied", "checked", "messaged"))
        loaded = [sem(f"loaded{q}") for q in range(R)]
        used = [sem(f"used{q}") for q in range(R)]
        with nc.Block() as block:
            @block.scalar
            def _(act):
                _take_tiles(nc, act, k, accumulator, width, cleared, added, copied, checked,
                            lambda i, h: sums[:, bass.ds(i * 2 + h, 1), :].rearrange("p j f -> p (j f)"))

            @block.sync
            def _(sp):
                with sp.Fori(0, ITERS) as i:
                    for q in range(R):
                        sp.wait_ge(used[q], i)
                        sp.dma_start(ring[:, q, :, :].rearrange("p g f -> p (g f)"),
                                     dram["kv"][:, bass.ds((i * R + q) * G * 2 * D, G * 2 * D)]).then_inc(loaded[q], DMA)

            @block.gpsimd
            def _(pool):
                with pool.Fori(0, ITERS) as i:
                    for q in range(R):
                        pool.wait_ge(added, (i * R + q + 2) * G)
                        pool.wait_ge(loaded[q], (i + 1) * DMA)
                        nc.gpsimd.tensor_tensor(
                            message[q % 2][:, :, 0:D].rearrange("p g (h d) -> p g h d", d=DHEAD),
                            ring[:, q, :, D:2 * D].rearrange("p g (h d) -> p g h d", d=DHEAD),
                            weight[:, bass.ds((i * R + q) * G, G), :].unsqueeze(3).to_broadcast([P, G, HEADS, DHEAD]),
                            ALU.mult).then_inc(used[q], 1)
                        nc.gpsimd.tensor_copy(message[q % 2][:, :, D:width],
                                              weight[:, bass.ds((i * R + q) * G, G), :]).then_inc(messaged, 1)

            @block.vector
            def _(dve):
                _one_hot(nc, k, onehot[0], 0).then_inc(made, 1)
                with dve.Fori(0, ITERS) as i:
                    for q in range(R):
                        dve.wait_ge(added, (i * R + q) * G + LEAD)
                        _one_hot(nc, k, onehot[(q + 1) % 2], (i * R + q + 1) * G).then_inc(made, 1)

            @block.tensor
            def _(pe):
                pe.sem_inc(added, LEAD)
                with pe.Fori(0, ITERS) as i:
                    for q in range(R):
                        tiles = _tile_registers(nc, pe, k, i * R + q)
                        pe.wait_ge(made, i * R + q + 1)
                        pe.wait_ge(messaged, i * R + q + 1)
                        for g in range(G):
                            _add_step(nc, pe, tiles[g], accumulator, width, cleared, added,
                                      onehot[q % 2][:, g, :], message[q % 2][:, g, :])


def attention(nc, io, k, dram):
    v = nc.vector
    with ExitStack() as ctx:
        sb, _, _ = _scope(nc, ctx, "att")
        h = sb("h", [P, JP, D])
        flat_h = h[:].rearrange("p j f -> p (j f)")
        norm_relu(nc, k, "att_norm", h)
        on_vector(nc, "att_add_h", [lambda: v.tensor_tensor(k["x"][:], k["x"][:], h[:], ALU.add)])
        score = sb("score", [P, S, HEADS])
        with ExitStack() as inner:
            sbi, _, _ = _scope(nc, inner, "qkv")
            qkv = sbi("qkv", [P, JP, 3 * D])
            w = sbi("w", [P, 1, 4 * 3 * D])
            load_diagonal(nc, "qkv_w", w[:].rearrange("p o (q f) -> p (o q) f", q=4), [io["L1_gnn_Wq"], io["L1_gnn_Wk"], io["L1_gnn_Wv"]])
            node_linear(nc, k, "qkv_lin", flat_h, JP // 4, 1, w, qkv[:].rearrange("p j f -> p (j f)"))
            on_vector(nc, "qkv_q", [lambda: v.tensor_copy(h[:], qkv[:, :, 0:D])])
            store_table(nc, "qkv_table", dram["tab64"], qkv[:, :, D:3 * D], 2 * D)
        score_pass(nc, k, dram, flat_h, score)
        softmax_weights(nc, k, dram, score)
        with ExitStack() as inner:
            sbi, _, _ = _scope(nc, inner, "wo")
            sums = sbi("sums", [P, JP, D + HEADS])
            on_vector(nc, "wo_clear", [lambda: v.memset(sums[:, TILES:JP, :], 0.0)])
            value_pass(nc, k, dram, score, sums)
            w = sbi("w", [P, 1, 4 * D])
            load_diagonal(nc, "wo_w", w[:].rearrange("p o (q f) -> p (o q) f", q=4), [io["L1_gnn_Wo"]])
            on_vector(nc, "wo_divide", [
                lambda: v.tensor_single_scalar(sums[:, :, D:D + HEADS], sums[:, :, D:D + HEADS], 1e-16, op=ALU.max),
                lambda: v.reciprocal(sums[:, :, D:D + HEADS], sums[:, :, D:D + HEADS]),
                lambda: v.tensor_tensor(h[:].rearrange("p j (h d) -> p j h d", d=DHEAD),
                                        sums[:, :, 0:D].rearrange("p j (h d) -> p j h d", d=DHEAD),
                                        sums[:, :, D:D + HEADS].unsqueeze(3).to_broadcast([P, JP, HEADS, DHEAD]), ALU.mult)])
            out = sums[:].rearrange("p j f -> p (j f)")[:, 0:JP * D]
            node_linear(nc, k, "wo_lin", flat_h, JP // 4, 1, w, out)
            on_vector(nc, "wo_add", [lambda: v.tensor_tensor(k["x"][:].rearrange("p j f -> p (j f)"),
                                                             k["x"][:].rearrange("p j f -> p (j f)"), out, ALU.add)])


def relation_pass(nc, k, dram, y_nodes, relations, current):
    H, WIDTH, LOOK = G // 2, N_BASES * D, D + N_BASES
    EARLY = R * G - G
    with ExitStack() as ctx:
        sb, psum, sem = _scope(nc, ctx, "rel")
        staged = sb("staged", [P, R, G], U32)
        ring = sb("ring", [P, R, G, 2 * D])
        onehot = [sb(f"onehot{m}", [P, H, P]) for m in range(4)]
        onehot_t = [sb(f"onehot_t{m}", [P, H, P]) for m in range(2)]
        kind = [sb(f"kind{m}", [P, H, N_REL]) for m in range(2)]
        kind_t = [sb(f"kind_t{m}", [N_REL, H, P]) for m in range(2)]
        dots = sb("dots", [P, H, D])
        logits = [sb(f"logits{m}", [P, H]) for m in range(2)]
        gate = [sb(f"gate{m}", [P, H]) for m in range(2)]
        coef = [sb(f"coef{m}", [P, H, N_BASES]) for m in range(2)]
        message = [sb(f"message{m}", [P, H, WIDTH]) for m in range(2)]
        taken = sb("taken", [P, 2 * BANK])
        flipped_ps = psum("flipped_ps", [P, 2, H, P])
        flipped_kind = psum("flipped_kind", [P, 1, H, P])
        looked = psum("looked", [P, 2, BANK])
        accumulator = psum("accumulator", [P, 2 * BANK])
        (indexed, released, made, flipped, turned, looked_up, logit, gated, weighed, messaged, added, cleared, copied,
         checked, passed, work, own) = (
            sem(n) for n in ("indexed", "released", "made", "flipped", "turned", "looked_up", "logit", "gated", "weighed",
                             "messaged", "added", "cleared", "copied", "checked", "passed", "work", "own"))
        gathered = [sem(f"gathered{q}") for q in range(R)]
        saved = sem("saved")

        def make_one_hots(dve, n, m):
            _one_hot(nc, k, onehot[m], n * H, H)
            nc.vector.tensor_tensor(kind[m % 2][:], k["iota"][:, 0:N_REL].unsqueeze(1).to_broadcast([P, H, N_REL]),
                                    k["type"][:, bass.ds(n * H, H)].unsqueeze(2).to_broadcast([P, H, N_REL]),
                                    ALU.is_equal).then_inc(made, 1)

        def make_logits(dve, n, m, q, h):
            dve.wait_ge(looked_up, n + 1)
            seen = looked[:, m % 2, 0:H * LOOK].rearrange("p (g f) -> p g f", f=LOOK)
            nc.vector.tensor_tensor(dots[:], seen[:, :, 0:D], ring[:, q, h * H:(h + 1) * H, D:2 * D], ALU.mult).then_inc(work, 1)
            dve.wait_ge(work, n * 2 + 1)
            nc.vector.tensor_reduce(logits[m % 2][:], dots[:], axis=AX_X, op=ALU.add).then_inc(work, 1)
            dve.wait_ge(work, n * 2 + 2)
            nc.vector.tensor_single_scalar(logits[m % 2][:], logits[m % 2][:], 0.0, op=ALU.max).then_inc(logit, 1)

        def make_messages(dve, n, m, q, h):
            dve.wait_ge(gated, n + 1)
            seen = looked[:, m % 2, 0:H * LOOK].rearrange("p (g f) -> p g f", f=LOOK)
            nc.vector.tensor_tensor(coef[m % 2][:], seen[:, :, D:LOOK], gate[m % 2][:].unsqueeze(2).to_broadcast([P, H, N_BASES]),
                                    ALU.mult).then_inc(weighed, 1)
            dve.wait_ge(weighed, n + 1)
            for g in range(H):
                nc.vector.tensor_tensor(
                    message[m % 2][:, g, :].rearrange("p (b f) -> p b f", f=D),
                    coef[m % 2][:, g, :].unsqueeze(2).to_broadcast([P, N_BASES, D]),
                    ring[:, q, h * H + g, 0:D].unsqueeze(1).to_broadcast([P, N_BASES, D]), ALU.mult).then_inc(messaged, 1)

        def flip(pe, n, m):
            pe.wait_ge(made, n + 1)
            for g in range(H):
                nc.tensor.transpose(flipped_ps[:, m % 2, g, :], onehot[m][:, g, :], k["ident"][:])
            for g in range(H):
                last = nc.tensor.transpose(flipped_kind[0:N_REL, 0, g, :], kind[m % 2][:, g, :], k["ident"][:])
            last.then_inc(flipped, 1)

        def look_up(pe, n, m, tiles):
            pe.wait_ge(turned, n + 1)
            for g in range(H):
                out = looked[:, m % 2, g * LOOK:(g + 1) * LOOK]
                nc.tensor.matmul(out, kind_t[m % 2][:, g, :], relations[:], start=True, stop=False)
                last = nc.tensor.matmul(out, onehot_t[m % 2][:, g, :], y_nodes[:, bass.ds(tiles[g] * LOOK, LOOK)],
                                        start=False, stop=True)
            last.then_inc(looked_up, 1)

        def turn(act, n, m):
            act.wait_ge(flipped, n + 1)
            nc.scalar.copy(onehot_t[m % 2][:], flipped_ps[:, m % 2, :, :])
            nc.scalar.copy(kind_t[m % 2][:], flipped_kind[0:N_REL, 0, :, :]).then_inc(turned, 1)

        def close_gate(act, n, m):
            act.wait_ge(logit, n + 1)
            nc.scalar.activation(gate[m % 2][:], logits[m % 2][:], ACT.Tanh, scale=1.0 / math.sqrt(D)).then_inc(gated, 1)

        with nc.Block() as block:
            @block.scalar
            def _(act):
                for h in range(2):
                    nc.scalar.copy(accumulator[:, h * BANK:(h + 1) * BANK], k["zeros"][:]).then_inc(cleared, 1)
                turn(act, 0, 0)
                turn(act, 1, 1)
                close_gate(act, 0, 0)
                with act.Fori(0, ITERS) as i:
                    for q in range(R):
                        tiles = _tile_registers(nc, act, k, i * R + q)
                        for h in range(2):
                            n, m = (i * R + q) * 2 + h, (q * 2 + h) % 4
                            act.wait_ge(looked_up, n + 1)
                            turn(act, n + 2, (m + 2) % 4)
                            close_gate(act, n + 1, (m + 1) % 4)
                            for g in range(h * H, h * H + H):
                                _take_if_last(nc, act, k, (i * R + q) * G + g, tiles[g], tiles[g + 1] - tiles[g], accumulator, taken,
                                              WIDTH, cleared, added, copied, checked, saved)

            @block.gpsimd
            def _(pool):
                _gather_rows(nc, pool, dram["tab64"], staged, ring, indexed, released, gathered,
                             lambda i, q: pool.wait_ge(messaged, (i * R + q) * G))
                pool.wait_ge(indexed, GROUPS + 1)
                for g in range(G):
                    nc.gpsimd.indirect_dma_start(
                        out=ring[:, 0, g, :], out_offset=None, in_=dram["tab64"],
                        in_offset=bass.IndirectOffsetOnAxis(ap=staged[:, 0, g:g + 1], axis=0)).then_inc(gathered[0], DMA)
                for j in range(J):
                    nc.gpsimd.indirect_dma_start(
                        out=current[:, j, :], out_offset=None, in_=dram["tab32"],
                        in_offset=bass.IndirectOffsetOnAxis(ap=k["last_index"][:, j:j + 1], axis=0)).then_inc(own, DMA)
                pool.wait_ge(own, J * DMA)
                pool.wait_ge(gathered[0], (ITERS + 1) * G * DMA)

            @block.vector
            def _(dve):
                dve.sem_inc(messaged, EARLY)
                for q in range(R - 1):
                    _stage(nc, k, staged, q, q).then_inc(indexed, 1)
                make_one_hots(dve, 0, 0)
                make_one_hots(dve, 1, 1)
                dve.wait_ge(gathered[0], G * DMA)
                make_logits(dve, 0, 0, 0, 0)
                with dve.Fori(0, ITERS) as i:
                    for q in range(R):
                        for h in range(2):
                            n, m = (i * R + q) * 2 + h, (q * 2 + h) % 4
                            dve.wait_ge(added, n * H + LEAD - H)
                            dve.wait_ge(flipped, n + 1)
                            make_one_hots(dve, n + 2, (m + 2) % 4)
                            if h == 1:
                                dve.wait_ge(gathered[(q + 1) % R], (i + 1 + (q == R - 1)) * G * DMA)
                            make_logits(dve, n + 1, (m + 1) % 4, (q + h) % R, 1 - h)
                            make_messages(dve, n, m, q, h)
                            if h == 0:
                                _stage(nc, k, staged, i * R + q + R - 1, (q + R - 1) % R).then_inc(indexed, 1)

            @block.tensor
            def _(pe):
                pe.sem_inc(added, LEAD)
                first = _tile_registers(nc, pe, k, 0)
                for n in range(2):
                    if n:
                        pe.wait_ge(turned, 1)
                    flip(pe, n, n)
                    look_up(pe, n, n, first[n * H:(n + 1) * H])
                with pe.Fori(0, ITERS) as i:
                    for q in range(R):
                        tiles = _tile_registers(nc, pe, k, i * R + q)
                        ahead = _tile_registers(nc, pe, k, i * R + q + 1)
                        for h in range(2):
                            n, m = (i * R + q) * 2 + h, (q * 2 + h) % 4
                            pe.wait_ge(turned, n + 2)
                            flip(pe, n + 2, (m + 2) % 4)
                            for g in range(H):
                                pe.wait_ge(messaged, n * H + g + 1 + EARLY)
                                _add_step(nc, pe, tiles[h * H + g], accumulator, WIDTH, cleared, added,
                                          onehot[m][:, g, :], message[m % 2][:, g, :])
                            pe.wait_ge(weighed, n + 1)
                            look_up(pe, n + 2, (m + 2) % 4, ahead[h * H:(h + 1) * H])

            @block.sync
            def _(sp):
                _save_tiles(sp, taken, dram["totals"], WIDTH, copied, saved, passed)


def relational(nc, io, k, dram):
    v = nc.vector
    with ExitStack() as ctx:
        sb, _, _ = _scope(nc, ctx, "rl")
        h = sb("h", [P, JP, D])
        flat_h = h[:].rearrange("p j f -> p (j f)")
        LOOK = D + N_BASES
        y_nodes = sb("y", [P, JP, LOOK])
        relations = sb("relations", [N_REL, LOOK])
        current = sb("current", [P, JP, D])
        norm_relu(nc, k, "rl_norm", h)
        with ExitStack() as inner:
            sbi, _, _ = _scope(nc, inner, "hat")
            both = sbi("both", [P, JP, 2 * D])
            w = sbi("w", [P, 1, 8 * D])
            bias = sbi("bias", [P, 2 * D])
            load_diagonal(nc, "hat_w", w[:].rearrange("p o (q f) -> p (o q) f", q=4), [io["A1_t"], io["A2_t"]])
            load_rows(nc, "hat_b", [(bias[:, 0:D], io["L2_gnn_A1_b"].unsqueeze(0).to_broadcast([P, D])),
                                    (bias[:, D:2 * D], io["L2_gnn_A2_b"].unsqueeze(0).to_broadcast([P, D])),
                                    (relations[:, 0:D], io["L2_gnn_rel_emb"]), (relations[:, D:LOOK], io["L2_gnn_w_comp"])])
            node_linear(nc, k, "hat_lin", flat_h, JP // 4, 1, w, both[:].rearrange("p j f -> p (j f)"))
            on_vector(nc, "hat_bias", [
                lambda: v.tensor_tensor(both[:], both[:], bias[:].unsqueeze(1).to_broadcast([P, JP, 2 * D]), ALU.add),
                lambda: v.memset(y_nodes[:], 0.0),
                lambda: v.tensor_copy(y_nodes[:, :, 0:D], both[:, :, D:2 * D]),
                lambda: v.tensor_copy(both[:, :, D:2 * D], both[:, :, 0:D]),
                lambda: v.tensor_copy(both[:, :, 0:D], h[:]),
                lambda: v.memset(current[:], 0.0)])
            store_table(nc, "hat_table", dram["tab64"], both, 2 * D)
            store_table(nc, "hat_rows", dram["tab32"], h, D)
        relation_pass(nc, k, dram, y_nodes[:].rearrange("p j f -> p (j f)"), relations, current)
        with ExitStack() as inner:
            sbi, _, _ = _scope(nc, inner, "rlo")
            own_w = sbi("own_w", [P, 1, 4 * D])
            w = sbi("w", [P, 4, D])
            out = sbi("out", [P, JP, D])
            has = sbi("has", [P, JP])
            load_diagonal(nc, "rlo_own_w", own_w[:].rearrange("p o (q f) -> p (o q) f", q=4), [io["L2_gnn_self_loop_weight"]])
            load_rows(nc, "rlo_w", [(w[:], io["L2_gnn_weight"].rearrange("b i o -> (b i) o").rearrange("(c p) o -> p c o", p=P))])
            node_linear(nc, k, "rlo_own", current[:].rearrange("p j f -> p (j f)"), JP // 4, 1, own_w, flat_h)
            on_vector(nc, "rlo_clear", [lambda: v.memset(out[:], 0.0)])
            node_linear(nc, k, "rlo_lin", dram["totals"], J, 4, w, out[:].rearrange("p j f -> p (j f)"), load=True)
            on_vector(nc, "rlo_out", [
                lambda: v.tensor_tensor(out[:], out[:], h[:], ALU.add),
                lambda: v.tensor_single_scalar(has[:], k["degree"][:], 0.0, op=ALU.is_gt),
                lambda: v.tensor_tensor(out[:], out[:], _spread(has[:], D), ALU.mult),
                lambda: v.tensor_single_scalar(out[:], out[:], 0.0, op=ALU.max),
                lambda: v.tensor_tensor(k["x"][:], k["x"][:], out[:], ALU.add)])


SH_WIDTH = 4 * D + 5 * 24


def harmonic_pass(nc, k, dram):
    with ExitStack() as ctx:
        sb, psum, sem = _scope(nc, ctx, "sh")
        staged = sb("staged", [P, R, G], U32)
        ring = sb("ring", [P, R, G, D])
        parts = sb("parts", [P, R, G, N_SH])
        onehot = [sb(f"onehot{h}", [P, G, P]) for h in range(2)]
        message = [sb(f"message{h}", [P, G, SH_WIDTH]) for h in range(2)]
        taken = sb("taken", [P, 2 * BANK])
        accumulator = psum("accumulator", [P, 2 * BANK])
        indexed, released, made, messaged, added, cleared, copied, checked, passed, saved = (
            sem(n) for n in ("indexed", "released", "made", "messaged", "added", "cleared", "copied", "checked", "passed", "saved"))
        gathered = [sem(f"gathered{q}") for q in range(R)]
        loaded = [sem(f"loaded{q}") for q in range(R)]

        def load_parts(act, group, slot):
            act.dma_start(parts[:, slot, :, :].rearrange("p g f -> p (g f)"),
                          dram["sh"][:, bass.ds(group * G * N_SH, G * N_SH)]).then_inc(loaded[slot], DMA)

        with nc.Block() as block:
            @block.scalar
            def _(act):
                for h in range(2):
                    nc.scalar.copy(accumulator[:, h * BANK:(h + 1) * BANK], k["zeros"][:]).then_inc(cleared, 1)
                for q in range(R - 1):
                    load_parts(act, q, q)
                with act.Fori(0, ITERS) as i:
                    for q in range(R):
                        act.wait_ge(messaged, i * R + q + R - 1)
                        act.sem_inc(checked, 1)
                        load_parts(act, i * R + q + R - 1, (q + R - 1) % R)
                        tiles = _tile_registers(nc, act, k, i * R + q)
                        for g in range(G):
                            _take_if_last(nc, act, k, (i * R + q) * G + g, tiles[g], tiles[g + 1] - tiles[g], accumulator, taken,
                                          SH_WIDTH, cleared, added, copied, checked, saved)
                for q in range(R - 1):
                    act.wait_ge(loaded[q], (ITERS + 1) * DMA)

            @block.gpsimd
            def _(pool):
                _gather_rows(nc, pool, dram["tab32"], staged, ring, indexed, released, gathered,
                             lambda i, q: pool.wait_ge(messaged, i * R + q))

            @block.vector
            def _(dve):
                dve.sem_inc(messaged, R - 1)
                nc.vector.memset(taken[:], 0.0)
                for q in range(R - 1):
                    _stage(nc, k, staged, q, q).then_inc(indexed, 1)
                with dve.Fori(0, ITERS) as i:
                    for q in range(R):
                        dve.wait_ge(added, (i * R + q) * G + LEAD - G)
                        _one_hot(nc, k, onehot[q % 2], (i * R + q) * G).then_inc(made, 1)
                        dve.wait_ge(loaded[q], (i + 1) * DMA)
                        dve.wait_ge(gathered[q], (i + 1) * G * DMA)
                        m = message[q % 2]
                        nc.vector.tensor_tensor(m[:, :, 0:4 * D].rearrange("p g (c f) -> p g c f", f=D),
                                                parts[:, q, :, 0:4].unsqueeze(3).to_broadcast([P, G, 4, D]),
                                                ring[:, q, :, :].unsqueeze(2).to_broadcast([P, G, 4, D]), ALU.mult)
                        nc.vector.tensor_tensor(m[:, :, 4 * D:SH_WIDTH].rearrange("p g (c f) -> p g c f", f=24),
                                                parts[:, q, :, 4:N_SH].unsqueeze(3).to_broadcast([P, G, 5, 24]),
                                                ring[:, q, :, 8:D].unsqueeze(2).to_broadcast([P, G, 5, 24]), ALU.mult).then_inc(messaged, 1)
                        _stage(nc, k, staged, i * R + q + R - 1, (q + R - 1) % R).then_inc(indexed, 1)

            @block.tensor
            def _(pe):
                pe.sem_inc(added, LEAD)
                with pe.Fori(0, ITERS) as i:
                    for q in range(R):
                        tiles = _tile_registers(nc, pe, k, i * R + q)
                        pe.wait_ge(made, i * R + q + 1)
                        pe.wait_ge(messaged, i * R + q + R)
                        for g in range(G):
                            _add_step(nc, pe, tiles[g], accumulator, SH_WIDTH, cleared, added,
                                      onehot[q % 2][:, g, :], message[q % 2][:, g, :])

            @block.sync
            def _(sp):
                _save_tiles(sp, taken, dram["totals"], 2 * P, copied, saved, passed)


def tensor_product(nc, io, k, dram, out):
    v = nc.vector
    with ExitStack() as ctx:
        sb, _, _ = _scope(nc, ctx, "tp")
        with ExitStack() as inner:
            sbi, _, _ = _scope(nc, inner, "tph")
            h = sbi("h", [P, JP, D])
            norm_relu(nc, k, "tp_norm", h)
            store_table(nc, "tp_table", dram["tab32"], h, D)
        harmonic_pass(nc, k, dram)
        with ExitStack() as inner:
            sbi, psi, _ = _scope(nc, inner, "mix")
            pick = sbi("pick", [8, 2 * P])
            w_all = sbi("w_all", [8, 6 * 8])
            cg = sbi("cg", [P, 14])
            row_w = sbi("row_w", [P, 2, 6 * 8])
            mix = sbi("mix", [P, 2, D])
            delta = sbi("delta", [P, JP, D])
            picked = psi("picked", [P, 2, 64])
            load_rows(nc, "mix_in", [(pick[:], io["pick"]), (cg[:], io["cg"]),
                                     (w_all[:].rearrange("i (c o) -> i c o", o=8), io["L3_gnn_W"].rearrange("c i o -> i c o"))])
            with ExitStack() as inner2:
                _, _, sem = _scope(nc, inner2, "mix_pick")
                ready, taken = sem("ready"), sem("taken")
                with nc.Block() as block:
                    @block.tensor
                    def _(pe):
                        for c in range(2):
                            last = nc.tensor.matmul(picked[:, c, 0:48], pick[:, c * P:(c + 1) * P], w_all[:], start=True, stop=True)
                        last.then_inc(ready, 1)

                    @block.vector
                    def _(dve):
                        v.memset(mix[:], 0.0).then_inc(taken, 1)
                        v.memset(delta[:], 0.0).then_inc(taken, 1)
                        dve.wait_ge(ready, 1)
                        v.tensor_copy(row_w[:], picked[:, :, 0:48])

            def add(c, n, combo, lo):
                to = mix[:, c, 0:8] if lo is None else mix[:, c, 8:D].rearrange("p (o k) -> p o k", k=3)[:, :, lo]
                return lambda: v.scalar_tensor_tensor(out=to, in0=row_w[:, c, 8 * combo:8 * combo + 8], scalar=cg[:, n:n + 1], in1=to,
                                                      op0=ALU.mult, op1=ALU.add)
            on_vector(nc, "mix_add", [add(c, n, combo, lo) for n, (c, combo, lo) in enumerate(MIX_TERMS)])
            node_linear(nc, k, "mix_lin", dram["totals"], J, 2, mix, delta[:].rearrange("p j f -> p (j f)"), load=True)
            on_vector(nc, "mix_x", [lambda: v.tensor_tensor(k["x"][:], k["x"][:], delta[:], ALU.add)])
        with ExitStack() as inner:
            _, _, sem = _scope(nc, inner, "out")
            stored = sem("stored")
            with nc.Block() as block:
                @block.sync
                def _(sp):
                    sp.dma_start(_node_rows(out, 0, J - 1), k["x"][:, 0:J - 1, :]).then_inc(stored, DMA)
                    sp.dma_start(out[(J - 1) * P:N_NODES, :], k["x"][0:LAST_TILE_ROWS, J - 1, :]).then_inc(stored, DMA)
                    sp.wait_ge(stored, 2 * DMA)


def _clebsch_gordan(l1, l2, l3):
    def su2(j1, m1, j2, m2, j3, m3):
        if m3 != m1 + m2:
            return 0.0
        f = math.factorial
        low = max(0, j2 - j3 - m1, j1 + m2 - j3)
        high = min(j1 + j2 - j3, j1 - m1, j2 + m2)
        pref = (2 * j3 + 1) * f(j3 + j1 - j2) * f(j3 - j1 + j2) * f(j1 + j2 - j3) / f(j1 + j2 + j3 + 1)
        pref *= f(j3 + m3) * f(j3 - m3) * f(j1 - m1) * f(j1 + m1) * f(j2 - m2) * f(j2 + m2)
        return math.sqrt(pref) * sum((-1) ** n / (f(n) * f(j1 + j2 - j3 - n) * f(j1 - m1 - n) * f(j2 + m2 - n)
                                                 * f(j3 - j2 + m1 + n) * f(j3 - j1 - m2 + n)) for n in range(low, high + 1))

    def real(l):
        q = np.zeros((2 * l + 1, 2 * l + 1), complex)
        for m in range(-l, 0):
            q[l + m, l - m] = 1 / np.sqrt(2)
            q[l + m, l + m] = -1j / np.sqrt(2)
        q[l, l] = 1.0
        for m in range(1, l + 1):
            q[l + m, l + m] = (-1) ** m / np.sqrt(2)
            q[l + m, l - m] = 1j * (-1) ** m / np.sqrt(2)
        return (-1j) ** l * q

    c = np.zeros((2 * l1 + 1, 2 * l2 + 1, 2 * l3 + 1), complex)
    for m1 in range(-l1, l1 + 1):
        for m2 in range(-l2, l2 + 1):
            if -l3 <= m1 + m2 <= l3:
                c[m1 + l1, m2 + l2, m1 + m2 + l3] = su2(l1, m1, l2, m2, l3, m1 + m2)
    c = np.einsum("ij,kl,mn,ikn->jlm", real(l1), real(l2), np.conj(real(l3)).T, c).real
    return c / np.linalg.norm(c)


MIX_TERMS = ([(0, 0, None)] + [(0, 1, o) for o in range(3)] + [(0, 2, o) for o in range(3)] + [(0, 3, None)]
             + [(0, 4, o) for o in range(3)] + [(1, 5, o) for o in range(3)])


def mixing_constants():
    combos = [(0, 0, 0), (0, 1, 1), (1, 0, 1), (1, 1, 0), (1, 1, 1), (2, 1, 1)]
    coefficients = [_clebsch_gordan(*c) for c in combos]
    pick = np.zeros((8, 2 * P), np.float32)
    cg = np.zeros((P, len(MIX_TERMS)), np.float32)
    for row in range(2 * P):
        if row < P:
            part, f = divmod(row, D)
            degree, component = (0, 0) if part == 0 else (1, part - 1)
        else:
            if row >= P + 120:
                continue
            component, f = divmod(row - P, 24)
            degree, f = 2, f + 8
        vector = f >= 8
        channel, direction = divmod(f - 8, 3) if vector else (f, 0)
        pick[channel, row] = 1.0
        for n, (chunk, combo, o) in enumerate(MIX_TERMS):
            le, ln, _ = combos[combo]
            if chunk == row // P and le == degree and ln == int(vector):
                cg[row % P, n] = coefficients[combo][component, direction, o or 0]
    return pick, cg


def gnn_kernel(nc, io, out):
    dram = scratch(nc)
    with ExitStack() as ctx:
        k = tables(nc, ctx)
        constants(nc, k)
        edge_records(nc, io, dram)
        merge_path(nc, k, dram)
        with ExitStack() as inner:
            k["stat"] = inner.enter_context(nc.sbuf_tensor("k_stat", [P, S, 2], F32))
            step_tables(nc, k, dram)
            node_statistics(nc, k)
        load_x(nc, io, k)
        gcn(nc, io, k, dram)
        attention(nc, io, k, dram)
        relational(nc, io, k, dram)
        tensor_product(nc, io, k, dram, out)


def tables(nc, ctx):
    def sb(n, shape, dt=F32):
        return ctx.enter_context(nc.sbuf_tensor(f"k_{n}", shape, dt))
    k = {"iota": sb("iota", [P, P]), "ident": sb("ident", [P, P]), "ones": sb("ones", [P, P]),
         "step_no": sb("step_no", [P, BLOCKS]), "t_of": sb("t_of", [P, BLOCKS]), "j_of": sb("j_of", [P, BLOCKS]),
         "t_index": sb("t_index", [P, BLOCKS], U32), "ends": sb("ends", [1, P], I32),
         "words": sb("words", [1, GROUPS + 1], I32), "src": sb("src", [P, S + R * G], U32),
         "drel": sb("drel", [P, S + G]), "type": sb("type", [P, S + G]),
         "x": sb("x", [P, JP, D]), "degree": sb("degree", [P, JP]), "zeros": sb("zeros", [P, BANK]),
         "last_index": sb("last_index", [P, JP], U32), "dinv": sb("dinv", [P, JP])}
    return k


def scratch(nc):
    def d(n, shape, dt=F32):
        return nc.dram_tensor(f"scratch_{n}", shape, dt, kind="Internal").ap()
    return {"rec": d("rec", [T, P * REC]), "j": d("j", [1, S]), "ends": d("ends", [1, P], I32), "dst_t": d("dst_t", [P, S]), "drel_t": d("drel_t", [P, S]),
            "sh": d("sh", [P, (S + R * G) * N_SH]), "tab32": d("tab32", [J * P, D]), "tab64": d("tab64", [J * P, 2 * D]),
            "tab128": d("tab128", [J * P, HID]), "totals": d("totals", [P, JP * 512]), "kv": d("kv", [P, S * 2 * D])}


def kernel(**inputs):
    import concourse.bacc as bacc
    from concourse.bass_utils import run_bass_kernel_spmd as run

    nc = bacc.Bacc("TRN2", target_bir_lowering=False, num_devices=1)
    given = {n: np.ascontiguousarray(a) for n, a in inputs.items() if n not in ("L2_gnn_A1_w", "L2_gnn_A2_w")}
    given["A1_t"] = np.ascontiguousarray(np.asarray(inputs["L2_gnn_A1_w"]).T)
    given["A2_t"] = np.ascontiguousarray(np.asarray(inputs["L2_gnn_A2_w"]).T)
    given["pick"], given["cg"] = mixing_constants()
    arrays = {f"in_{n}": a for n, a in given.items()}
    io = {n: nc.dram_tensor(f"in_{n}", a.shape, mybir.dt.from_np(a.dtype), kind="ExternalInput").ap() for n, a in given.items()}
    out = nc.dram_tensor("out_x", (N_NODES, D), F32, kind="ExternalOutput").ap()
    gnn_kernel(nc, io, out)
    return run(nc, [arrays], core_ids=[0]).results[0]["out_x"]
```

```python
import math
from contextlib import ExitStack

import numpy as np
import concourse.bass as bass
from concourse import mybir

F32 = mybir.dt.float32
BF16 = mybir.dt.bfloat16
I32 = mybir.dt.int32
U32 = mybir.dt.uint32
ALU = mybir.AluOpType
ACT = mybir.ActivationFunctionType
AX_X = mybir.AxisListType.X

P = 128
N_NODES = 12500
N_EDGES = 200000
D = 32
HID = 128
HEADS, DHEAD = 4, 8
N_REL, N_BASES = 86, 16
J = -(-N_NODES // P)
JP = 104
T = -(-N_EDGES // P)
REC = 16
R_SRC, R_DST, R_NEXT, R_TYPE, R_SH, R_REL, R_LAST = 0, 1, 2, 3, 4, 13, 14
N_SH = 9
G = 8
R = 4
BLOCKS = -(-(T + J - 1) // P)
S = BLOCKS * P
ITERS = S // (G * R)
GROUPS = S // G
TILES = J + S - (T + J - 1)
LEAD = (R - 1) * G
CHUNK = 1024
CHUNKS = -(-T * P // CHUNK)
TB = 2 * CHUNK // P
BANKS = 4
BANK = 512
BIG = 1e30
LAST_TILE_ROWS = N_NODES - (J - 1) * P
PAD_DST = J * P - 1
DMA = 16


def _node_rows(table, j0, j1):
    return table[j0 * P:j1 * P, :].rearrange("(j p) f -> p j f", p=P)


class Chain:

    def __init__(self, engine, semaphore):
        self.engine, self.semaphore, self.value = engine, semaphore, 0

    def link(self, instruction):
        self.value += 1
        instruction.then_inc(self.semaphore, 1)
        self.engine.wait_ge(self.semaphore, self.value)


def _scope(nc, ctx, name):
    def sb(n, shape, dt=F32):
        return ctx.enter_context(nc.sbuf_tensor(f"{name}_{n}", shape, dt))

    def psum(n, shape, dt=F32):
        return ctx.enter_context(nc.psum_tensor(f"{name}_{n}", shape, dt))

    held = []

    def clear():
        nc.clear_and_free_semaphores(held)
        nc.all_engine_barrier()

    def sem(n):
        if not held:
            ctx.callback(clear)
        held.append(nc.alloc_semaphore(f"{name}_{n}"))
        return held[-1]

    return sb, psum, sem


def constants(nc, k):
    with ExitStack() as ctx:
        sb, _, sem = _scope(nc, ctx, "const")
        row = sb("row", [P, 1])
        made = sem("made")
        with nc.Block() as block:
            @block.gpsimd
            def _(pool):
                nc.gpsimd.iota(k["iota"][:], pattern=[[1, P]], base=0, channel_multiplier=0,
                               allow_small_or_imprecise_dtypes=True).then_inc(made, 1)
                nc.gpsimd.iota(row[:], pattern=[[0, 1]], base=0, channel_multiplier=1,
                               allow_small_or_imprecise_dtypes=True).then_inc(made, 1)
                nc.gpsimd.iota(k["step_no"][:], pattern=[[P, BLOCKS]], base=0, channel_multiplier=1,
                               allow_small_or_imprecise_dtypes=True).then_inc(made, 1)

            @block.vector
            def _(dve):
                nc.vector.memset(k["ones"][:], 1.0)
                nc.vector.memset(k["zeros"][:], 0.0)
                dve.wait_ge(made, 3)
                nc.vector.tensor_scalar(k["ident"][:], k["iota"][:], row[:, 0:1], None, ALU.is_equal)
                nc.vector.tensor_scalar(k["ident16"][:], k["iota"][:], row[:, 0:1], None, ALU.is_equal)


def edge_records(nc, io, k, dram):
    C = -(-T * P // P)
    LAST = N_EDGES - (P - 1) * C
    CH = C // 3
    assert C == T and CH * 3 == C
    with ExitStack() as ctx:
        sb, _, sem = _scope(nc, ctx, "rec")
        fields = [("src", I32, 1, 0, 0), ("dst", I32, 1, 0, PAD_DST), ("next", I32, 1, 1, PAD_DST),
                  ("type", I32, 1, 0, 0), ("sh0", F32, 1, 0, 0), ("sh1", F32, 3, 0, 0), ("sh2", F32, 5, 0, 0)]
        source = {"src": io["src"], "dst": io["dst"], "next": io["dst"], "type": io["edge_type_86"],
                  "sh0": io["edge_weight1"], "sh1": io["edge_attr_3"], "sh2": io["edge_attr_5"]}
        held = {n: sb(n, [P, C * w], dt) for n, dt, w, _, _ in fields}
        falls = sb("falls", [P, C])
        fallen = sb("fallen", [P, 1])
        total = ctx.enter_context(nc.psum_tensor("rec_total", [1, 1], F32))
        counted, totalled = sem("counted"), sem("totalled")
        rec = [sb(f"rec{i}", [P, CH, REC]) for i in range(2)]
        padded, loaded = sem("padded"), sem("loaded")
        joined_dve, joined_act = sem("joined_dve"), sem("joined_act")
        stored = [sem(f"stored{i}") for i in range(2)]
        out = dram["rec"].rearrange("t (e f) -> (t e f)", f=REC).rearrange("(p w) -> p w", p=P)
        with nc.Block() as block:
            @block.sync
            def _(sp):
                sp.wait_ge(padded, len(fields))
                n = 0
                for name, _, w, shift, _ in fields:
                    flat = source[name]
                    if len(flat.shape) == 2:
                        flat = flat.rearrange("e w -> (e w)")
                    for p0, p1 in ((0, 112), (112, P - 1)):
                        a, b = (p0 * C + shift) * w, (p1 * C + shift) * w
                        sp.dma_start(held[name][p0:p1, :], flat[a:b].rearrange("(p c) -> p c", p=p1 - p0)).then_inc(loaded, DMA)
                    a = ((P - 1) * C + shift) * w
                    sp.dma_start(held[name][P - 1:P, 0:(LAST - shift) * w],
                                 flat[a:N_EDGES * w].rearrange("(p c) -> p c", p=1)).then_inc(loaded, DMA)
                for i in range(3):
                    sp.wait_ge(joined_dve, i + 1)
                    sp.wait_ge(joined_act, i + 1)
                    sp.dma_start(out[:, i * CH * REC:(i + 1) * CH * REC],
                                 rec[i % 2][:].rearrange("p c f -> p (c f)")).then_inc(stored[i % 2], DMA)
                sp.wait_ge(stored[0], 2 * DMA)
                sp.wait_ge(stored[1], DMA)

            @block.vector
            def _(dve):
                for name, _, w, shift, value in fields:
                    nc.vector.memset(held[name][:, (LAST - shift) * w:C * w], value).then_inc(padded, 1)
                for i in range(2):
                    nc.vector.memset(rec[i][:, :, R_SH + N_SH:REC], 0.0)
                dve.wait_ge(loaded, 3 * len(fields) * DMA)
                for i in range(3):
                    if i >= 2:
                        dve.wait_ge(stored[i % 2], DMA)
                    for f, name in ((R_SRC, "src"), (R_DST, "dst"), (R_NEXT, "next"), (R_TYPE, "type"), (R_SH, "sh0")):
                        last = nc.vector.tensor_copy(rec[i % 2][:, :, f], held[name][:, i * CH:(i + 1) * CH])
                    last.then_inc(joined_dve, 1)
                nc.vector.tensor_tensor(falls[:], held["next"][:], held["dst"][:], ALU.is_lt).then_inc(counted, 1)
                dve.wait_ge(counted, 1)
                nc.vector.tensor_reduce(fallen[:], falls[:], axis=AX_X, op=ALU.add).then_inc(counted, 1)
                dve.wait_ge(totalled, 1)
                nc.vector.tensor_copy(k["unsorted"][:], total[:])

            @block.tensor
            def _(pe):
                pe.wait_ge(counted, 2)
                nc.tensor.matmul(total[:], fallen[:], k["ones"][:, 0:1], start=True, stop=True).then_inc(totalled, 1)

            @block.scalar
            def _(act):
                act.wait_ge(loaded, 3 * len(fields) * DMA)
                for i in range(3):
                    if i >= 2:
                        act.wait_ge(stored[i % 2], DMA)
                    nc.scalar.copy(rec[i % 2][:, :, R_SH + 1:R_SH + 4],
                                   held["sh1"][:, 3 * i * CH:3 * (i + 1) * CH].rearrange("p (c w) -> p c w", w=3))
                    nc.scalar.copy(rec[i % 2][:, :, R_SH + 4:R_SH + 9],
                                   held["sh2"][:, 5 * i * CH:5 * (i + 1) * CH].rearrange("p (c w) -> p c w", w=5)).then_inc(joined_act, 1)


def sort_records(nc, io, k, dram):
    C, CH, COLS = T, T // 3, CHUNKS * CHUNK // P
    FULL = N_EDGES // P
    LONG = CHUNKS * CHUNK - N_EDGES
    dst = io["dst"]
    with ExitStack() as ctx:
        sb, _, sem = _scope(nc, ctx, "sort")
        dst_i = sb("dst_i", [P, COLS], I32)
        dst_f = sb("dst_f", [P, COLS])
        own = sb("own", [P, COLS])
        limit = sb("limit", [P, COLS])
        count = sb("count", [P, COLS])
        rank = sb("rank", [P, COLS])
        place = sb("place", [P, COLS], U32)
        row_i = sb("row_i", [P, CHUNK], I32)
        row = sb("row", [P, CHUNK])
        order = sb("order", [P, CHUNK])
        before = sb("before", [P, TB, CHUNK])
        pad = sb("pad", [1, LONG], I32)
        record = sb("record", [P, REC])
        to = sb("to", [P, 1], U32)
        wide = sb("wide", [P, CH + 1, REC])
        numbered, padded, loaded, copied, row_in, row_used, chain_sem, stepped = (
            sem(n) for n in ("numbered", "padded", "loaded", "copied", "row_in", "row_used", "chain", "stepped"))
        fetched, picked, scattered, moved, linked, stored, checked, entered = (
            sem(n) for n in ("fetched", "picked", "scattered", "moved", "linked", "stored", "checked", "entered"))

        def unsorted(engine):
            return engine.value_load(k["unsorted"][0:1, 0:1], min_val=0, max_val=T * P) > 0

        with nc.Block() as block:
            @block.sync
            def _(sp):
                with sp.If(unsorted(sp)), nc.allow_non_contiguous_dma("dst by edge of the tile"):
                    sp.wait_ge(padded, 2)
                    for a in range(0, FULL, P):
                        b = min(a + P, FULL)
                        sp.dma_start(dst_i[:, a:b], dst[a * P:b * P].rearrange("(t e) -> e t", e=P)).then_inc(loaded, DMA)
                    sp.dma_start(dst_i[0:N_EDGES - FULL * P, FULL:FULL + 1],
                                 dst[FULL * P:N_EDGES].rearrange("(e o) -> e o", o=1)).then_inc(loaded, DMA)
                    sp.dma_start(dram["dst_row"][:, 0:N_EDGES], dst.unsqueeze(0)).then_inc(copied, DMA)
                    sp.dma_start(dram["dst_row"][:, N_EDGES:], pad[:]).then_inc(copied, DMA)
                    sp.dma_start(dram["sorted"][P * C:P * C + 1, :], k["zeros"][0:1, 0:REC]).then_inc(copied, DMA)
                    sp.wait_ge(copied, 3 * DMA)
                    with sp.Fori(0, CHUNKS) as c:
                        sp.wait_ge(row_used, c + 1)
                        sp.sem_inc(checked, 1)
                        sp.dma_start(row_i[:], dram["dst_row"][:, bass.ds(c * CHUNK, CHUNK)].to_broadcast([P, CHUNK])).then_inc(row_in, DMA)

            @block.gpsimd
            def _(pool):
                with pool.If(unsorted(pool)):
                    nc.gpsimd.iota(order[:], pattern=[[1, CHUNK]], base=0, channel_multiplier=0,
                                   allow_small_or_imprecise_dtypes=True).then_inc(numbered, 1)
                    nc.gpsimd.iota(own[:].rearrange("p (c t) -> p c t", t=CHUNK // P), pattern=[[0, CHUNKS], [P, CHUNK // P]], base=0,
                                   channel_multiplier=1, allow_small_or_imprecise_dtypes=True).then_inc(numbered, 1)

            @block.vector
            def _(dve):
                chain = Chain(dve, chain_sem)
                with dve.If(unsorted(dve)):
                    nc.vector.memset(dst_i[:], PAD_DST).then_inc(padded, 1)
                    nc.vector.memset(pad[:], PAD_DST).then_inc(padded, 1)
                    nc.vector.memset(rank[:], 0.0)
                    dve.sem_inc(row_used, 1)
                    dve.wait_ge(numbered, 2)
                    chain.link(nc.vector.tensor_single_scalar(order[:], order[:], 1.0 / CHUNK, op=ALU.mult))
                    dve.wait_ge(loaded, (-(-FULL // P) + 1) * DMA)
                    chain.link(nc.vector.tensor_copy(dst_f[:], dst_i[:]))
                    chain.link(nc.vector.tensor_single_scalar(limit[:], dst_f[:], 1.0, op=ALU.add))
                    chain.link(nc.vector.scalar_tensor_tensor(out=own[:], in0=own[:], scalar=1.0 / CHUNK, in1=dst_f[:],
                                                              op0=ALU.mult, op1=ALU.add))
                    with dve.Fori(0, CHUNKS) as c:
                        done = c * (2 * (COLS // TB) + 4)
                        mine = bass.ds(c * (CHUNK // P), CHUNK // P)
                        dve.wait_ge(row_in, (c + 1) * DMA)
                        nc.vector.tensor_copy(row[:], row_i[:]).then_inc(row_used, 1)
                        dve.wait_ge(row_used, c + 2)
                        nc.vector.tensor_tensor(row[:], row[:], order[:], ALU.add).then_inc(stepped, 1)
                        nc.vector.tensor_copy(limit[:, mine], own[:, mine]).then_inc(stepped, 1)
                        dve.wait_ge(stepped, done + 2)
                        dve.sem_inc(entered, 1)
                        with dve.Fori(0, COLS // TB) as u:
                            at = bass.ds(u * TB, TB)
                            nc.vector.tensor_tensor(before[:], row[:].unsqueeze(1).to_broadcast([P, TB, CHUNK]),
                                                    limit[:, at].unsqueeze(2).to_broadcast([P, TB, CHUNK]), ALU.is_lt).then_inc(stepped, 1)
                            dve.wait_ge(stepped, done + u * 2 + 3)
                            nc.vector.tensor_reduce(count[:, at], before[:], axis=AX_X, op=ALU.add).then_inc(stepped, 1)
                            dve.wait_ge(stepped, done + u * 2 + 4)
                        nc.vector.tensor_tensor(rank[:], rank[:], count[:], ALU.add).then_inc(stepped, 1)
                        nc.vector.tensor_copy(limit[:, mine], dst_f[:, mine]).then_inc(stepped, 1)
                        dve.wait_ge(stepped, done + 2 * (COLS // TB) + 4)
                    nc.vector.tensor_copy(place[:], rank[:])

        with nc.Block() as block:
            @block.gpsimd
            def _(pool):
                with pool.If(unsorted(pool)):
                    with pool.Fori(0, T) as t:
                        nc.gpsimd.tensor_copy(to[:], place[:, bass.ds(t, 1)]).then_inc(picked, 1)
                        pool.dma_start(record[:], dram["rec"][bass.ds(t, 1), :].rearrange("o (e f) -> (o e) f", f=REC)).then_inc(fetched, DMA)
                        pool.wait_ge(picked, t + 1)
                        pool.wait_ge(fetched, (t + 1) * DMA)
                        pool.sem_inc(checked, 1)
                        nc.gpsimd.indirect_dma_start(
                            out=dram["sorted"], out_offset=bass.IndirectOffsetOnAxis(ap=to[:, 0:1], axis=0),
                            in_=record[:], in_offset=None).then_inc(scattered, DMA)
                        pool.wait_ge(scattered, (t + 1) * DMA)
                        pool.sem_inc(checked, 1)

        whole = dram["rec"].rearrange("t (e f) -> (t e) f", f=REC).rearrange("(p c) f -> p c f", p=P)
        with nc.Block() as block:
            @block.sync
            def _(sp):
                with sp.If(unsorted(sp)), nc.allow_non_contiguous_dma("one record of each partition"):
                    for i in range(3):
                        if i:
                            sp.wait_ge(stored, i * DMA)
                        sp.dma_start(wide[:, 0:CH, :], dram["sorted"][0:P * C, :].rearrange("(p c) f -> p c f", c=C)
                                     [:, i * CH:(i + 1) * CH, :]).then_inc(moved, DMA)
                        off = (i + 1) * CH
                        sp.dma_start(wide[:, CH, :], dram["sorted"][off:off + P * C, :].rearrange("(p c) f -> p c f", c=C)
                                     [:, 0, :]).then_inc(moved, DMA)
                        sp.wait_ge(linked, i + 1)
                        sp.dma_start(whole[:, i * CH:(i + 1) * CH, :], wide[:, 0:CH, :]).then_inc(stored, DMA)
                    sp.wait_ge(stored, 3 * DMA)

            @block.vector
            def _(dve):
                with dve.If(unsorted(dve)):
                    for i in range(3):
                        dve.wait_ge(moved, 2 * (i + 1) * DMA)
                        nc.vector.tensor_copy(wide[:, 0:CH, R_NEXT], wide[:, 1:CH + 1, R_DST]).then_inc(linked, 1)


def merge_path(nc, k, dram):
    CUT = [(c, min(c + 512, T)) for c in range(0, T, 512)]
    with ExitStack() as ctx:
        sb, psum, sem = _scope(nc, ctx, "path")
        last_dst = sb("last_dst", [1, T])
        node_tile = sb("node_tile", [1, T], I32)
        done_at = sb("done_at", [1, T])
        tile_no = sb("tile_no", [1, T])
        done_all = sb("done_all", [P, T])
        before = sb("before", [P, T])
        j_row = sb("j_row", [1, S + 8])
        inc_row = sb("inc_row", [1, S + 8])
        weight = sb("weight", [1, G])
        parts = sb("parts", [1, GROUPS, G])
        word = sb("word", [1, GROUPS])
        j_int = sb("j_int", [1, S], I32)
        bank_int = sb("bank_int", [1, S], I32)
        bank_row = sb("bank_row", [1, S])
        bank_word = sb("bank_word", [1, GROUPS])
        places = sb("places", [1, 3, GROUPS], I32)
        tile_row = sb("tile_row", [1, T])
        tile_all = sb("tile_all", [P, T])
        ends = sb("ends", [P, 2])
        spread = psum("spread", [P, 4, BANK])
        spread_tile = psum("spread_tile", [P, 4, BANK])
        ends_int = sb("ends_int", [P, 1], I32)
        loaded, numbered, ready, shown, chain_sem, j_out, j_in = (
            sem(n) for n in ("loaded", "numbered", "ready", "shown", "chain", "j_out", "j_in"))
        with nc.Block() as block:
            @block.sync
            def _(sp):
                with nc.allow_non_contiguous_dma("one word of each edge tile"):
                    sp.dma_start(last_dst[:], dram["rec"][:, (P - 1) * REC + R_DST:(P - 1) * REC + R_DST + 1]
                                 .rearrange("t o -> o t")).then_inc(loaded, DMA)
                    sp.wait_ge(ready, 3)
                    sp.dma_start(dram["j"].rearrange("o (b p) -> p (o b)", p=P), k["j_of"][:]).then_inc(j_out, DMA)
                    sp.dma_start(dram["ends"].rearrange("o p -> p o"), ends_int[:]).then_inc(j_out, DMA)
                    sp.wait_ge(j_out, 2 * DMA)
                    sp.dma_start(j_row[:, 0:S], dram["j"]).then_inc(j_in, DMA)
                    sp.dma_start(k["ends"][:], dram["ends"]).then_inc(j_in, DMA)

            @block.gpsimd
            def _(pool):
                nc.gpsimd.iota(tile_no[:], pattern=[[1, T]], base=0, channel_multiplier=0,
                               allow_small_or_imprecise_dtypes=True).then_inc(numbered, 1)

            @block.vector
            def _(dve):
                chain = Chain(dve, chain_sem)
                dve.wait_ge(loaded, DMA)
                dve.wait_ge(numbered, 1)
                chain.link(nc.vector.tensor_copy(node_tile[:], last_dst[:]))
                chain.link(nc.vector.tensor_single_scalar(node_tile[:], node_tile[:], 7, op=ALU.arith_shift_right))
                nc.vector.tensor_copy(tile_row[:], node_tile[:])
                nc.vector.tensor_tensor(done_at[:], node_tile[:], tile_no[:], ALU.add).then_inc(ready, 1)
                dve.wait_ge(shown, 1)
                for n, (a, b) in enumerate(CUT):
                    nc.vector.tensor_copy(tile_all[:, a:b], spread_tile[:, n, 0:b - a])
                    last = nc.vector.tensor_copy(done_all[:, a:b], spread[:, n, 0:b - a])
                chain.link(last)
                chain.link(nc.vector.tensor_scalar(before[:], tile_all[:], k["step_no"][:, 0:1], 0.0,
                                                   ALU.is_le, ALU.add, accum_out=ends[:, 0:1]))
                chain.link(nc.vector.tensor_scalar(ends[:, 1:2], ends[:, 0:1], float(T - 1), float(LEAD + 1), ALU.min, ALU.add))
                chain.link(nc.vector.tensor_tensor(ends[:, 0:1], ends[:, 1:2], k["step_no"][:, 0:1], ALU.add))
                nc.vector.tensor_copy(ends_int[:], ends[:, 0:1]).then_inc(ready, 1)
                for b in range(BLOCKS):
                    chain.link(nc.vector.tensor_scalar(before[:], done_all[:], k["step_no"][:, b:b + 1], 0.0,
                                                       ALU.is_lt, ALU.add, accum_out=k["t_of"][:, b:b + 1]))
                chain.link(nc.vector.tensor_single_scalar(k["t_of"][:], k["t_of"][:], float(T - 1), op=ALU.min))
                nc.vector.tensor_copy(k["t_index"][:], k["t_of"][:])
                nc.vector.tensor_tensor(k["j_of"][:], k["step_no"][:], k["t_of"][:], ALU.subtract).then_inc(ready, 1)
                for g in range(G):
                    nc.vector.memset(weight[:, g:g + 1], float(2 ** (7 + g)))
                chain.link(nc.vector.memset(j_row[:, S:S + 8], float(S - T + 1)))
                dve.wait_ge(j_in, 2 * DMA)
                chain.link(nc.vector.tensor_tensor(inc_row[:, 0:S], j_row[:, 1:S + 1], j_row[:, 0:S], ALU.subtract))
                chain.link(nc.vector.tensor_tensor(parts[:], inc_row[:, 0:S].rearrange("o (g k) -> o g k", k=G),
                                                   weight[:].unsqueeze(1).to_broadcast([1, GROUPS, G]), ALU.mult))
                chain.link(nc.vector.tensor_reduce(word[:], parts[:], axis=AX_X, op=ALU.add))
                chain.link(nc.vector.tensor_tensor(word[:], word[:], j_row[:, 0:S].rearrange("o (g k) -> o g k", k=G)[:, :, 0], ALU.add))
                nc.vector.memset(k["words"][:, GROUPS:GROUPS + 2], 0)
                chain.link(nc.vector.tensor_copy(j_int[:], j_row[:, 0:S]))
                for banks, scale, out in ((2, 2.0 ** 15, k["words"][:, 0:GROUPS]), (BANKS, 1.0, places[:, 0, :])):
                    chain.link(nc.vector.tensor_single_scalar(bank_int[:], j_int[:], banks - 1, op=ALU.bitwise_and))
                    chain.link(nc.vector.tensor_copy(bank_row[:], bank_int[:]))
                    for g in range(G):
                        last = nc.vector.memset(weight[:, g:g + 1], scale * banks ** g)
                    chain.link(last)
                    chain.link(nc.vector.tensor_tensor(parts[:], bank_row[:].rearrange("o (g k) -> o g k", k=G),
                                                       weight[:].unsqueeze(1).to_broadcast([1, GROUPS, G]), ALU.mult))
                    chain.link(nc.vector.tensor_reduce(bank_word[:], parts[:], axis=AX_X, op=ALU.add))
                    if banks == 2:
                        chain.link(nc.vector.tensor_tensor(bank_word[:], bank_word[:], word[:], ALU.add))
                    chain.link(nc.vector.tensor_copy(out, bank_word[:]))
                by_group = j_row[:, 0:S].rearrange("o (g k) -> o g k", k=G)
                for n, (step, shift) in enumerate(((3, 16), (7, 23))):
                    chain.link(nc.vector.tensor_single_scalar(places[:, n + 1, :], by_group[:, :, step], 1.0, op=ALU.add))
                    chain.link(nc.vector.tensor_single_scalar(places[:, n + 1, :], places[:, n + 1, :], shift, op=ALU.logical_shift_left))
                    chain.link(nc.vector.tensor_tensor(places[:, 0, :], places[:, 0, :], places[:, n + 1, :], ALU.bitwise_or))
                nc.vector.tensor_copy(k["places"][:], places[:, 0, :])

            @block.tensor
            def _(pe):
                pe.wait_ge(ready, 1)
                for n, (a, b) in enumerate(CUT):
                    nc.tensor.matmul(spread_tile[:, n, 0:b - a], k["ones"][0:1, :], tile_row[:, a:b], start=True, stop=True)
                    last = nc.tensor.matmul(spread[:, n, 0:b - a], k["ones"][0:1, :], done_at[:, a:b], start=True, stop=True)
                last.then_inc(shown, 1)


def step_tables(nc, k, dram):
    with ExitStack() as ctx:
        sb, psum, sem = _scope(nc, ctx, "table")
        index = sb("index", [P, 1], U32)
        tile = sb("tile", [P, P, REC])
        flag = sb("flag", [P, P])
        j128 = sb("j128", [P, BLOCKS])
        sh = sb("sh", [P, P, N_SH])
        turned = psum("turned", [P, 4, P])
        turned_sh = psum("turned_sh", [P, 12, P])
        released, halved = sem("released"), sem("halved")
        indexed, gathered, filled, flipped, taken_dve, taken_act, chain_sem, sh_out, t_out = (
            sem(n) for n in ("indexed", "gathered", "filled", "flipped", "taken_dve", "taken_act", "chain", "sh_out", "t_out"))
        with nc.Block() as block:
            @block.gpsimd
            def _(pool):
                with pool.Fori(0, BLOCKS) as b:
                    pool.wait_ge(indexed, b + 1)
                    pool.wait_ge(flipped, b)
                    pool.wait_ge(t_out, b * 2 * DMA)
                    pool.sem_inc(released, 1)
                    nc.gpsimd.indirect_dma_start(
                        out=tile[:].rearrange("p e f -> p (e f)"), out_offset=None, in_=dram["rec"],
                        in_offset=bass.IndirectOffsetOnAxis(ap=index[:, 0:1], axis=0)).then_inc(gathered, DMA)

            @block.vector
            def _(dve):
                nc.vector.memset(k["stat"][:, :, 0], 1.0)
                split, low = sb("split", [P, P], I32), sb("low", [P, P], I32)
                nc.vector.memset(k["drel"][:, S:S + 2 * G], -1.0)
                nc.vector.memset(k["type"][:, S:S + 2 * G], 0.0)
                nc.vector.memset(k["src"][:, S:S + R * G], 0)
                nc.vector.tensor_single_scalar(j128[:], k["j_of"][:], float(P), op=ALU.mult).then_inc(chain_sem, 1)
                dve.wait_ge(chain_sem, 1)
                with dve.Fori(0, BLOCKS) as b:
                    dve.wait_ge(gathered, b * DMA)
                    nc.vector.tensor_copy(index[:], k["t_index"][:, bass.ds(b, 1)]).then_inc(indexed, 1)
                    dve.wait_ge(gathered, (b + 1) * DMA)
                    nc.vector.tensor_scalar(tile[:, :, R_REL], tile[:, :, R_DST], j128[:, bass.ds(b, 1)], None, ALU.subtract)
                    nc.vector.tensor_tensor(flag[:], tile[:, :, R_DST], tile[:, :, R_NEXT], ALU.not_equal).then_inc(chain_sem, 1)
                    dve.wait_ge(chain_sem, b + 2)
                    nc.vector.scalar_tensor_tensor(out=tile[:, :, R_LAST], in0=tile[:, :, R_SRC], scalar=1.0, in1=flag[:],
                                                   op0=ALU.add, op1=ALU.mult).then_inc(filled, 1)
                    dve.wait_ge(flipped, b + 1)
                    at = bass.ds(b * P, P)
                    nc.vector.tensor_copy(k["src"][:, at], turned[:, 0, :])
                    nc.vector.tensor_copy(k["drel"][:, at], turned[:, 1, :])
                    nc.vector.tensor_copy(k["type"][:, at], turned[:, 2, :])
                    nc.vector.tensor_copy(split[:], turned[:, 3, :]).then_inc(taken_dve, 1)
                    dve.wait_ge(taken_dve, b + 1)
                    nc.vector.tensor_single_scalar(low[:], split[:], P - 1, op=ALU.bitwise_and).then_inc(halved, 1)
                    dve.wait_ge(halved, b * 2 + 1)
                    nc.vector.tensor_copy(k["stat"][:, at, 2], low[:])
                    nc.vector.tensor_tensor(k["stat"][:, at, 1], split[:], low[:], ALU.subtract).then_inc(halved, 1)

            @block.tensor
            def _(pe):
                with pe.Fori(0, BLOCKS) as b:
                    pe.wait_ge(filled, b + 1)
                    pe.wait_ge(taken_dve, b)
                    pe.wait_ge(taken_act, b)
                    for n, f in enumerate((R_SRC, R_REL, R_TYPE, R_LAST)):
                        nc.tensor.transpose(turned[:, n, :], tile[:, :, f], k["ident"][:])
                    for f in range(N_SH):
                        last = nc.tensor.transpose(turned_sh[:, f, :], tile[:, :, R_SH + f], k["ident"][:])
                    last.then_inc(flipped, 1)

            @block.scalar
            def _(act):
                with act.Fori(0, BLOCKS) as b:
                    act.wait_ge(flipped, b + 1)
                    act.wait_ge(sh_out, b * DMA)
                    for f0, f1 in ((0, 4), (4, 8), (8, 9)):
                        last = nc.scalar.copy(sh[:, :, f0:f1].rearrange("p s f -> p f s"), turned_sh[:, f0:f1, :])
                    last.then_inc(taken_act, 1)

            @block.sync
            def _(sp):
                with sp.Fori(0, BLOCKS) as b, nc.allow_non_contiguous_dma("one field of the records"):
                    sp.wait_ge(filled, b + 1)
                    sp.dma_start(dram["dst_t"][:, bass.ds(b * P, P)], tile[:, :, R_DST]).then_inc(t_out, DMA)
                    sp.dma_start(dram["drel_t"][:, bass.ds(b * P, P)], tile[:, :, R_REL]).then_inc(t_out, DMA)
                    sp.wait_ge(taken_act, b + 1)
                    sp.dma_start(dram["sh"][:, bass.ds(b * P * N_SH, P * N_SH)], sh[:].rearrange("p s f -> p (s f)")).then_inc(sh_out, DMA)
                sp.dma_start(dram["sh"][:, S * N_SH:(S + R * G) * N_SH], k["zeros"][:, 0:R * G * N_SH]).then_inc(sh_out, DMA)
                sp.wait_ge(sh_out, (BLOCKS + 1) * DMA)
                sp.wait_ge(t_out, 2 * BLOCKS * DMA)


def _one_hot(nc, k, out, first, n=G):
    return nc.vector.tensor_tensor(out[:], k["iota"][:].unsqueeze(1).to_broadcast([P, n, P]),
                                   k["drel"][:, bass.ds(first, n)].unsqueeze(2).to_broadcast([P, n, P]), ALU.is_equal)


def _word(engine, k, group):
    return engine.value_load(k["words"][0:1, bass.ds(group, 1)], min_val=0, max_val=(1 << (7 + 2 * G)) - 1)


def _tile_registers(nc, engine, word):
    tiles = [engine.snap(nc.s_assert_within(word & 127, 0, JP - 1, skip_runtime_bounds_check_because="a node tile"))]
    for g in range(1, G + 1):
        tiles.append(engine.snap(nc.s_assert_within(tiles[-1] + ((word >> (6 + g)) & 1), 0, JP - 1,
                                                    skip_runtime_bounds_check_because="a node tile")))
    return tiles


class Adder:

    def __init__(self, nc, pe, k, group, banks, accumulator, width, cleared, added, word=None):
        self.nc, self.pe, self.banks, self.accumulator, self.width = nc, pe, banks, accumulator, width
        self.cleared, self.added, self.tile = cleared, added, None
        if banks == BANKS:
            word = pe.value_load(k["places"][0:1, bass.ds(group, 1)], min_val=0, max_val=(1 << 30) - 1)
        self.word = word

    def add(self, g, onehot, rows):
        word = self.word
        if self.banks == BANKS:
            if g % 4 == 0:
                self.pe.wait_ge(self.cleared, (word >> 23) if g else ((word >> 16) & 127))
            first = ((word >> (2 * g)) & (BANKS - 1)) * BANK
        else:
            if g % 2 == 0:
                increments = ((word >> (7 + g)) & 1) + (((word >> (6 + g)) & 1) if g else (word & 127))
                self.tile = self.pe.snap(increments + self.tile if g else increments)
                self.pe.wait_ge(self.cleared, self.tile + 1)
            first = (word >> (6 + g)) & BANK
        self.nc.tensor.matmul(self.accumulator[:, bass.ds(first, self.width)], onehot, rows,
                              start=False, stop=True, skip_group_check=True).then_inc(self.added, 1)


def _take_tiles(nc, act, k, accumulator, width, cleared, added, copied, checked, target):
    def take(tile, h):
        end = act.value_load(k["ends"][0:1, bass.ds(tile, 1)], min_val=1, max_val=S + LEAD)
        act.wait_ge(added, end)
        act.sem_inc(checked, 1)
        nc.scalar.copy(target(tile), accumulator[:, h * BANK:h * BANK + width]).then_inc(copied, 1)
        act.wait_ge(copied, tile + 1)
        nc.scalar.copy(accumulator[:, h * BANK:h * BANK + width], k["zeros"][:, 0:width]).then_inc(cleared, 1)

    for h in range(BANKS):
        nc.scalar.copy(accumulator[:, h * BANK:h * BANK + width], k["zeros"][:, 0:width]).then_inc(cleared, 1)
    with act.Fori(0, TILES // BANKS) as i:
        for h in range(BANKS):
            take(i * BANKS + h, h)
    for tile in range(TILES // BANKS * BANKS, TILES):
        take(tile, tile % BANKS)


def _take_if_last(nc, act, k, step, tile, ends, accumulator, taken, width, cleared, added, copied, checked, saved):
    with act.If(ends > 0):
        act.wait_ge(added, step + 1 + LEAD)
        act.wait_ge(saved, tile * DMA)
        act.sem_inc(checked, 1)
        nc.scalar.copy(taken[:, bass.ds((tile & 1) * BANK, width)],
                       accumulator[:, bass.ds((tile & 1) * BANK, width)]).then_inc(copied, 1)
        act.wait_ge(copied, tile + 1)
        act.sem_inc(checked, 1)
        nc.scalar.copy(accumulator[:, bass.ds((tile & 1) * BANK, width)], k["zeros"][:, 0:width]).then_inc(cleared, 1)


def _save_tiles(sp, taken, totals, width, copied, saved, passed):
    sp.sem_inc(saved, DMA)
    with sp.Fori(0, TILES // 2) as i:
        for h in range(2):
            sp.wait_ge(copied, i * 2 + h + 1)
            sp.dma_start(totals[:, bass.ds((i * 2 + h) * width, width)],
                         taken[:, h * BANK:h * BANK + width]).then_inc(saved, DMA)
            sp.wait_ge(saved, (i * 2 + h + 2) * DMA)
            sp.sem_inc(passed, 1)


def _stage(nc, k, staged, group, slot):
    return nc.vector.tensor_copy(staged[:, slot, :], k["src"][:, bass.ds(group * G, G)])


def _gather_rows(nc, pool, table, staged, ring, indexed, released, gathered, slot_waits):
    with pool.Fori(0, ITERS) as i:
        for q in range(R):
            pool.wait_ge(indexed, i * R + q + 1)
            slot_waits(i, q)
            pool.sem_inc(released, 1)
            for g in range(G):
                nc.gpsimd.indirect_dma_start(
                    out=ring[:, q, g, :], out_offset=None, in_=table,
                    in_offset=bass.IndirectOffsetOnAxis(ap=staged[:, q, g:g + 1], axis=0)).then_inc(gathered[q], DMA)


def sum_pass(nc, k, name, table, sums, width):
    with ExitStack() as ctx:
        sb, psum, sem = _scope(nc, ctx, name)
        staged = sb("staged", [P, R, G], U32)
        ring = sb("ring", [P, R, G, width])
        onehot = [sb(f"onehot{h}", [P, G, P]) for h in range(2)]
        accumulator = psum("accumulator", [P, BANKS * BANK])
        gathered = [sem(f"gathered{q}") for q in range(R)]
        indexed, made, released, added, cleared, copied, checked = (
            sem(n) for n in ("indexed", "made", "released", "added", "cleared", "copied", "checked"))
        with nc.Block() as block:
            @block.gpsimd
            def _(pool):
                _gather_rows(nc, pool, table, staged, ring, indexed, released, gathered,
                             lambda i, q: pool.wait_ge(added, (i * R + q) * G))

            @block.vector
            def _(dve):
                for q in range(R - 1):
                    _stage(nc, k, staged, q, q).then_inc(indexed, 1)
                _one_hot(nc, k, onehot[0], 0).then_inc(made, 1)
                with dve.Fori(0, ITERS) as i:
                    for q in range(R):
                        dve.wait_ge(added, (i * R + q) * G + LEAD)
                        _one_hot(nc, k, onehot[(q + 1) % 2], (i * R + q + 1) * G).then_inc(made, 1)
                        _stage(nc, k, staged, i * R + q + R - 1, (q + R - 1) % R).then_inc(indexed, 1)

            @block.tensor
            def _(pe):
                pe.sem_inc(added, LEAD)
                with pe.Fori(0, ITERS) as i:
                    for q in range(R):
                        adder = Adder(nc, pe, k, i * R + q, BANKS, accumulator, width, cleared, added)
                        pe.wait_ge(made, i * R + q + 1)
                        pe.wait_ge(gathered[q], (i + 1) * G * DMA)
                        for g in range(G):
                            adder.add(g, onehot[q % 2][:, g, :], ring[:, q, g, :])

            @block.scalar
            def _(act):
                _take_tiles(nc, act, k, accumulator, width, cleared, added, copied, checked,
                            lambda tile: sums[:, bass.ds(tile, 1), :].rearrange("p j f -> p (j f)"))


def node_statistics(nc, k):
    with ExitStack() as ctx:
        sb, psum, sem = _scope(nc, ctx, "stat")
        onehot = [sb(f"onehot{h}", [P, G, P], BF16) for h in range(2)]
        by_step = sb("by_step", [P, S, 3])
        running = sb("running", [P, 2, S])
        at_end = sb("at_end", [P, 2, TILES + 1])
        last = sb("last", [P, JP])
        partial = psum("partial", [P, R, BANK])
        made, summed, taken, chain_sem, inverted = (sem(n) for n in ("made", "summed", "taken", "chain", "inverted"))
        with nc.Block() as block:
            @block.tensor
            def _(pe):
                with pe.Fori(0, ITERS) as i:
                    for q in range(R):
                        pe.wait_ge(made, i * R + q + 1)
                        pe.wait_ge(taken, i * R + q)
                        for g in range(G):
                            done = nc.tensor.matmul(partial[:, q, 3 * g:3 * g + 3], onehot[q % 2][:, g, :],
                                                    k["stat"][:, bass.ds((i * R + q) * G + g, 1), :].rearrange("p s w -> p (s w)"),
                                                    start=True, stop=True)
                        done.then_inc(summed, 1)

            @block.vector
            def _(dve):
                for h in range(2):
                    _one_hot(nc, k, onehot[h], h * G).then_inc(made, 1)
                with dve.Fori(0, ITERS) as i:
                    for q in range(R):
                        dve.wait_ge(summed, i * R + q + 1)
                        _one_hot(nc, k, onehot[q % 2], (i * R + q + 2) * G).then_inc(made, 1)

            @block.scalar
            def _(act):
                act.sem_inc(taken, R - 1)
                with act.Fori(0, ITERS) as i:
                    for q in range(R):
                        act.wait_ge(summed, i * R + q + 1)
                        act.sem_inc(chain_sem, 1)
                        nc.scalar.copy(by_step[:, bass.ds((i * R + q) * G, G), :].rearrange("p s w -> p (s w)"),
                                       partial[:, q, 0:3 * G]).then_inc(taken, 1)

        with nc.Block() as block:
            @block.vector
            def _(dve):
                chain = Chain(dve, inverted)
                ones = k["ones"][:, 0:1].to_broadcast([P, S])
                chain.link(nc.vector.tensor_tensor(by_step[:, :, 1], by_step[:, :, 1], by_step[:, :, 2], ALU.add))
                for n in range(2):
                    chain.link(nc.vector.tensor_tensor_scan(running[:, n, :], ones, by_step[:, :, n], 0.0, ALU.mult, ALU.add))
                chain.link(nc.vector.memset(at_end[:], 0.0))
                with dve.Fori(0, TILES // 2) as i:
                    for h in range(2):
                        end = dve.value_load(k["ends"][0:1, bass.ds(i * 2 + h, 1)], min_val=LEAD + 1, max_val=S + LEAD)
                        at = nc.s_assert_within(end - (LEAD + 1), 0, S - 1, skip_runtime_bounds_check_because="a step")
                        nc.vector.tensor_copy(at_end[:, :, bass.ds(i * 2 + h + 1, 1)], running[:, :, bass.ds(at, 1)])

        with nc.Block() as block:
            @block.vector
            def _(dve):
                chain = Chain(dve, made)
                chain.value = GROUPS + 2
                chain.link(nc.vector.memset(k["degree"][:], 0.0))
                chain.link(nc.vector.memset(last[:], 1.0))
                chain.link(nc.vector.tensor_tensor(k["degree"][:, 0:TILES], at_end[:, 0, 1:], at_end[:, 0, 0:TILES], ALU.subtract))
                chain.link(nc.vector.tensor_tensor(last[:, 0:TILES], at_end[:, 1, 1:], at_end[:, 1, 0:TILES], ALU.subtract))
                chain.link(nc.vector.tensor_scalar(last[:], last[:], -1.0, 0.0, ALU.add, ALU.max))
                chain.link(nc.vector.tensor_copy(k["last_index"][:], last[:]))
                chain.link(nc.vector.tensor_single_scalar(k["dinv"][:], k["degree"][:], 1.0, op=ALU.add))
                chain.link(nc.vector.reciprocal(k["dinv"][:], k["dinv"][:]))

            @block.scalar
            def _(act):
                act.wait_ge(made, GROUPS + 10)
                nc.scalar.activation(k["dinv"][:], k["dinv"][:], ACT.Sqrt)


def load_x(nc, io, k):
    with ExitStack() as ctx:
        _, _, sem = _scope(nc, ctx, "x")
        cleared, loaded = sem("cleared"), sem("loaded")
        with nc.Block() as block:
            @block.vector
            def _(dve):
                nc.vector.memset(k["x"][:], 0.0).then_inc(cleared, 1)

            @block.sync
            def _(sp):
                sp.wait_ge(cleared, 1)
                sp.dma_start(k["x"][:, 0:J - 1, :], _node_rows(io["x"], 0, J - 1)).then_inc(loaded, DMA)
                sp.dma_start(k["x"][0:LAST_TILE_ROWS, J - 1, :], io["x"][(J - 1) * P:N_NODES, :]).then_inc(loaded, DMA)
                sp.wait_ge(loaded, 2 * DMA)


def _spread(a, n):
    return a.unsqueeze(2).to_broadcast([P, JP, n])


def norm_relu(nc, k, name, h):
    x = k["x"]
    with ExitStack() as ctx:
        sb, _, sem = _scope(nc, ctx, name)
        centered = sb("centered", [P, JP, D])
        mean = sb("mean", [P, JP])
        var = sb("var", [P, JP])
        rooted, chain_sem, summed = sem("rooted"), sem("chain"), sem("summed")
        with nc.Block() as block:
            @block.vector
            def _(dve):
                chain = Chain(dve, chain_sem)
                chain.link(nc.vector.tensor_reduce(mean[:], x[:], axis=AX_X, op=ALU.add))
                chain.link(nc.vector.tensor_single_scalar(mean[:], mean[:], 1.0 / D, op=ALU.mult))
                chain.link(nc.vector.tensor_tensor(centered[:], x[:], _spread(mean[:], D), ALU.subtract))
                chain.link(nc.vector.tensor_tensor(h[:], centered[:], centered[:], ALU.mult))
                chain.link(nc.vector.tensor_reduce(var[:], h[:], axis=AX_X, op=ALU.add))
                nc.vector.tensor_scalar(var[:], var[:], 1.0 / D, 1e-5, ALU.mult, ALU.add).then_inc(summed, 1)
                dve.wait_ge(rooted, 1)
                chain.link(nc.vector.reciprocal(var[:], var[:]))
                chain.link(nc.vector.tensor_tensor(centered[:], centered[:], _spread(var[:], D), ALU.mult))
                nc.vector.tensor_single_scalar(h[:], centered[:], 0.0, op=ALU.max)

            @block.scalar
            def _(act):
                act.wait_ge(summed, 1)
                nc.scalar.activation(var[:], var[:], ACT.Sqrt).then_inc(rooted, 1)


def store_table(nc, name, table, a, width):
    with ExitStack() as ctx:
        _, _, sem = _scope(nc, ctx, name)
        stored = sem("stored")
        with nc.Block() as block:
            @block.sync
            def _(sp):
                sp.dma_start(_node_rows(table, 0, J), a[:, 0:J, 0:width]).then_inc(stored, DMA)
                sp.wait_ge(stored, DMA)


def node_linear(nc, k, name, source, n, parts, weights, out, load=None):
    width = parts * P
    fo = weights.shape[2]
    assert n % 2 == 0
    from_dram = load
    with ExitStack() as ctx:
        sb, psum, sem = _scope(nc, ctx, name)
        chunk = [sb(f"chunk{h}", [P, width]) for h in range(2)]
        turned = [sb(f"turned{h}", [P, parts, P]) for h in range(2)]
        flipped_ps = psum("flipped_ps", [P, 2, 4, P])
        product = psum("product", [P, 2, 512])
        staged = [sem(f"staged{h}") for h in range(2)]
        flipped = [sem(f"flipped{h}") for h in range(2)]
        copied = [sem(f"copied{h}") for h in range(2)]
        multiplied = [sem(f"multiplied{h}") for h in range(2)]
        taken = [sem(f"taken{h}") for h in range(2)]
        per_stage = DMA if from_dram else 1
        with nc.Block() as block:
            if from_dram:
                @block.sync
                def _(sp):
                    with sp.Fori(0, n // 2) as i:
                        for h in range(2):
                            sp.wait_ge(flipped[h], i)
                            sp.dma_start(chunk[h][:], source[:, bass.ds((i * 2 + h) * width, width)]).then_inc(staged[h], DMA)
            else:
                @block.gpsimd
                def _(pool):
                    with pool.Fori(0, n // 2) as i:
                        for h in range(2):
                            pool.wait_ge(flipped[h], i)
                            nc.gpsimd.tensor_copy(chunk[h][:], source[:, bass.ds((i * 2 + h) * width, width)]).then_inc(staged[h], 1)

            @block.tensor
            def _(pe):
                with pe.Fori(0, n // 2) as i:
                    for h in range(2):
                        pe.wait_ge(staged[h], (i + 1) * per_stage)
                        pe.wait_ge(copied[h], i)
                        for c in range(parts):
                            last = nc.tensor.transpose(flipped_ps[:, h, c, :], chunk[h][:, c * P:(c + 1) * P], k["ident"][:])
                        last.then_inc(flipped[h], 1)
                    for h in range(2):
                        pe.wait_ge(copied[h], i + 1)
                        pe.wait_ge(taken[h], i)
                        for c in range(parts):
                            last = nc.tensor.matmul(product[:, h, 0:fo], turned[h][:, c, :], weights[:, c, :],
                                                    start=(c == 0), stop=(c == parts - 1))
                        last.then_inc(multiplied[h], 1)

            @block.scalar
            def _(act):
                with act.Fori(0, n // 2) as i:
                    for h in range(2):
                        act.wait_ge(flipped[h], i + 1)
                        act.wait_ge(multiplied[h], i)
                        nc.scalar.copy(turned[h][:], flipped_ps[:, h, 0:parts, :]).then_inc(copied[h], 1)

            @block.vector
            def _(dve):
                with dve.Fori(0, n // 2) as i:
                    for h in range(2):
                        dve.wait_ge(multiplied[h], i + 1)
                        nc.vector.tensor_copy(out[:, bass.ds((i * 2 + h) * fo, fo)], product[:, h, 0:fo]).then_inc(taken[h], 1)


def load_diagonal(nc, name, w, pieces):
    with ExitStack() as ctx:
        _, _, sem = _scope(nc, ctx, name)
        cleared, loaded = sem("cleared"), sem("loaded")
        with nc.Block() as block:
            @block.vector
            def _(dve):
                nc.vector.memset(w[:], 0.0).then_inc(cleared, 1)

            @block.sync
            def _(sp):
                sp.wait_ge(cleared, 1)
                for q in range(4):
                    at = 0
                    for piece in pieces:
                        f = piece.shape[1]
                        sp.dma_start(w[D * q:D * (q + 1), q, at:at + f], piece).then_inc(loaded, DMA)
                        at += f
                sp.wait_ge(loaded, 4 * len(pieces) * DMA)


def load_rows(nc, name, pairs):
    with ExitStack() as ctx:
        _, _, sem = _scope(nc, ctx, name)
        loaded = sem("loaded")
        with nc.Block() as block:
            @block.sync
            def _(sp):
                for a, b in pairs:
                    sp.dma_start(a, b).then_inc(loaded, DMA)
                sp.wait_ge(loaded, len(pairs) * DMA)


def on_vector(nc, name, steps):
    with ExitStack() as ctx:
        _, _, sem = _scope(nc, ctx, name)
        chain_sem = sem("chain")
        with nc.Block() as block:
            @block.vector
            def _(dve):
                chain = Chain(dve, chain_sem)
                for step in steps:
                    chain.link(step())


def gcn(nc, io, k, dram):
    v = nc.vector
    with ExitStack() as ctx:
        sb, _, _ = _scope(nc, ctx, "gcn")
        h = sb("h", [P, JP, D])
        norm_relu(nc, k, "gcn_norm", h)
        on_vector(nc, "gcn_scale0", [lambda: v.tensor_tensor(h[:], h[:], _spread(k["dinv"][:], D), ALU.mult)])
        store_table(nc, "gcn_table0", dram["tab32"], h, D)
        with ExitStack() as inner:
            sbi, _, _ = _scope(nc, inner, "gcn1")
            sums = sbi("sums", [P, JP, D])
            on_vector(nc, "gcn_clear0", [lambda: v.memset(sums[:, TILES:JP, :], 0.0)])
            sum_pass(nc, k, "gcn_sum0", dram["tab32"], sums, D)
            wide = sbi("wide", [P, JP, HID])
            w1 = sbi("w1", [P, 1, 4 * HID])
            b1 = sbi("b1", [P, HID])
            load_diagonal(nc, "gcn_w1", w1[:].rearrange("p o (q f) -> p (o q) f", q=4), [io["L0_gnn_W1"]])
            load_rows(nc, "gcn_b1", [(b1[:], io["L0_gnn_b1"].unsqueeze(0).to_broadcast([P, HID]))])
            on_vector(nc, "gcn_self0", [lambda: v.tensor_tensor(sums[:], sums[:], h[:], ALU.add)])
            node_linear(nc, k, "gcn_lin1", sums[:].rearrange("p j f -> p (j f)"), JP // 4, 1, w1, wide[:].rearrange("p j f -> p (j f)"))
            on_vector(nc, "gcn_act1", [
                lambda: v.tensor_tensor(wide[:], wide[:], _spread(k["dinv"][:], HID), ALU.mult),
                lambda: v.tensor_tensor(wide[:], wide[:], b1[:].unsqueeze(1).to_broadcast([P, JP, HID]), ALU.add),
                lambda: v.tensor_single_scalar(wide[:], wide[:], 0.0, op=ALU.max),
                lambda: v.tensor_tensor(wide[:], wide[:], _spread(k["dinv"][:], HID), ALU.mult)])
            store_table(nc, "gcn_table1", dram["tab128"], wide, HID)
        with ExitStack() as inner:
            sbi, _, _ = _scope(nc, inner, "gcn2")
            sums = sbi("sums", [P, JP, HID])
            on_vector(nc, "gcn_clear1", [lambda: v.memset(sums[:, TILES:JP, :], 0.0)])
            sum_pass(nc, k, "gcn_sum1", dram["tab128"], sums, HID)
            w2 = sbi("w2", [P, 1, HID])
            w3 = sbi("w3", [P, 1, D])
            b2 = sbi("b2", [P, HID])
            load_rows(nc, "gcn_w2", [(w2[:, 0, :], io["L0_gnn_W2"]), (w3[:, 0, :], io["L0_gnn_W3"]),
                                     (b2[:], io["L0_gnn_b2"].unsqueeze(0).to_broadcast([P, HID]))])
            load_wide = sbi("own", [P, 14, HID])
            with ExitStack() as inner2:
                _, _, sem = _scope(nc, inner2, "gcn_self1")
                fetched, added = sem("fetched"), sem("added")
                with nc.Block() as block:
                    @block.sync
                    def _(sp):
                        for c in range(J // 14):
                            sp.wait_ge(added, c)
                            sp.dma_start(load_wide[:], _node_rows(dram["tab128"], 14 * c, 14 * (c + 1))).then_inc(fetched, DMA)

                    @block.vector
                    def _(dve):
                        for c in range(J // 14):
                            dve.wait_ge(fetched, (c + 1) * DMA)
                            at = slice(14 * c, 14 * (c + 1))
                            v.tensor_tensor(sums[:, at, :], sums[:, at, :], load_wide[:], ALU.add).then_inc(added, 1)
            flat = sums[:].rearrange("p j f -> p (j f)")
            node_linear(nc, k, "gcn_lin2", flat, J, 1, w2, flat)
            on_vector(nc, "gcn_act2", [
                lambda: v.tensor_tensor(sums[:], sums[:], _spread(k["dinv"][:], HID), ALU.mult),
                lambda: v.tensor_tensor(sums[:], sums[:], b2[:].unsqueeze(1).to_broadcast([P, JP, HID]), ALU.add),
                lambda: v.tensor_single_scalar(sums[:], sums[:], 0.0, op=ALU.max),
                lambda: v.tensor_tensor(sums[:], sums[:], _spread(k["dinv"][:], HID), ALU.mult),
                lambda: v.memset(h[:], 0.0)])
            node_linear(nc, k, "gcn_lin3", flat, J, 1, w3, h[:].rearrange("p j f -> p (j f)"))
            store_table(nc, "gcn_table2", dram["tab32"], h, D)
        sums = sb("sums2", [P, JP, D])
        on_vector(nc, "gcn_clear2", [lambda: v.memset(sums[:, TILES:JP, :], 0.0)])
        sum_pass(nc, k, "gcn_sum2", dram["tab32"], sums, D)
        b3 = sb("b3", [P, D])
        load_rows(nc, "gcn_b3", [(b3[:], io["L0_gnn_b3"].unsqueeze(0).to_broadcast([P, D]))])
        on_vector(nc, "gcn_out", [
            lambda: v.tensor_tensor(sums[:], sums[:], h[:], ALU.add),
            lambda: v.tensor_tensor(sums[:], sums[:], _spread(k["dinv"][:], D), ALU.mult),
            lambda: v.tensor_tensor(sums[:], sums[:], b3[:].unsqueeze(1).to_broadcast([P, JP, D]), ALU.add),
            lambda: v.tensor_single_scalar(sums[:], sums[:], 0.0, op=ALU.max),
            lambda: v.tensor_tensor(k["x"][:], k["x"][:], sums[:], ALU.add)])


def score_pass(nc, k, dram, q_nodes, score):
    with ExitStack() as ctx:
        sb, psum, sem = _scope(nc, ctx, "score")
        staged = sb("staged", [P, R, G], U32)
        ring = sb("ring", [P, R, G, 2 * D])
        onehot = [sb(f"onehot{h}", [P, G, P]) for h in range(2)]
        onehot_t = [sb(f"onehot_t{h}", [P, G, P]) for h in range(2)]
        product = [sb(f"product{h}", [P, G, D]) for h in range(2)]
        flipped_ps = psum("flipped_ps", [P, 2, G, P])
        q_edge = psum("q_edge", [P, 2, 512])
        indexed, made, reduced, released = sem("indexed"), sem("made"), sem("reduced"), sem("released")
        looked_up = [sem(f"looked_up{q}") for q in range(R)]
        gathered = [sem(f"gathered{q}") for q in range(R)]
        flipped = [sem(f"flipped{q}") for q in range(R)]
        turned = [sem(f"turned{q}") for q in range(R)]
        used = [sem(f"used{q}") for q in range(R)]
        spilled = [sem(f"spilled{q}") for q in range(R)]
        with nc.Block() as block:
            @block.scalar
            def _(act):
                with act.Fori(0, ITERS) as i:
                    for q in range(R):
                        act.wait_ge(flipped[q], i + 1)
                        act.wait_ge(looked_up[(q - 2) % R], i + (q >= 2))
                        nc.scalar.copy(onehot_t[q % 2][:], flipped_ps[:, q % 2, :, :]).then_inc(turned[q], 1)

            @block.gpsimd
            def _(pool):
                with pool.Fori(0, ITERS) as i:
                    for q in range(R):
                        pool.wait_ge(indexed, i * R + q + 1)
                        pool.wait_ge(used[q], i)
                        pool.wait_ge(spilled[q], i * DMA)
                        pool.sem_inc(released, 1)
                        for g in range(G):
                            nc.gpsimd.indirect_dma_start(
                                out=ring[:, q, g, :], out_offset=None, in_=dram["tab64"],
                                in_offset=bass.IndirectOffsetOnAxis(ap=staged[:, q, g:g + 1], axis=0)).then_inc(gathered[q], DMA)

            @block.vector
            def _(dve):
                for q in range(R - 1):
                    _stage(nc, k, staged, q, q).then_inc(indexed, 1)
                _one_hot(nc, k, onehot[0], 0).then_inc(made, 1)
                with dve.Fori(0, ITERS) as i:
                    for q in range(R):
                        dve.wait_ge(flipped[(q - 1) % R], i + (q >= 1))
                        _one_hot(nc, k, onehot[(q + 1) % 2], (i * R + q + 1) * G).then_inc(made, 1)
                        _stage(nc, k, staged, i * R + q + R - 1, (q + R - 1) % R).then_inc(indexed, 1)
                        dve.wait_ge(looked_up[q], i + 1)
                        dve.wait_ge(gathered[q], (i + 1) * G * DMA)
                        nc.vector.tensor_tensor(product[q % 2][:], q_edge[:, q % 2, 0:G * D].rearrange("p (g f) -> p g f", f=D),
                                                ring[:, q, :, 0:D], ALU.mult).then_inc(used[q], 1)
                        dve.wait_ge(used[q], i + 1)
                        nc.vector.tensor_reduce(score[:, bass.ds((i * R + q) * G, G), :],
                                                product[q % 2][:].rearrange("p g (h d) -> p g h d", d=DHEAD),
                                                axis=AX_X, op=ALU.add).then_inc(reduced, 1)

            @block.tensor
            def _(pe):
                with pe.Fori(0, ITERS) as i:
                    for q in range(R):
                        pe.wait_ge(made, i * R + q + 1)
                        pe.wait_ge(turned[(q - 2) % R], i + (q >= 2))
                        for g in range(G):
                            last = nc.tensor.transpose(flipped_ps[:, q % 2, g, :], onehot[q % 2][:, g, :], k["ident"][:])
                        last.then_inc(flipped[q], 1)
                        tiles = _tile_registers(nc, pe, _word(pe, k, i * R + q))
                        pe.wait_ge(turned[q], i + 1)
                        pe.wait_ge(used[(q - 2) % R], i + (q >= 2))
                        for g in range(G):
                            last = nc.tensor.matmul(q_edge[:, q % 2, g * D:(g + 1) * D], onehot_t[q % 2][:, g, :],
                                                    q_nodes[:, bass.ds(tiles[g] * D, D)], start=True, stop=True)
                        last.then_inc(looked_up[q], 1)

            @block.sync
            def _(sp):
                with sp.Fori(0, ITERS) as i:
                    for q in range(R):
                        sp.wait_ge(gathered[q], (i + 1) * G * DMA)
                        sp.dma_start(dram["kv"][:, bass.ds((i * R + q) * G * 2 * D, G * 2 * D)],
                                     ring[:, q, :, :].rearrange("p g f -> p (g f)")).then_inc(spilled[q], DMA)
                for q in range(R):
                    sp.wait_ge(spilled[q], ITERS * DMA)


def softmax_weights(nc, k, dram, score):
    SE = BLOCKS * P
    with ExitStack() as ctx:
        sb, psum, sem = _scope(nc, ctx, "softmax")
        dst = sb("dst", [P, BLOCKS, P])
        rel = sb("rel", [P, BLOCKS, P])
        reset = sb("reset", [P, BLOCKS, P])
        by_step = sb("by_step", [P, HEADS, BLOCKS, P])
        back = sb("back", [P, BLOCKS, P])
        edge_of = sb("edge_of", [P, BLOCKS, 4, HEADS])
        carry = [sb(f"carry{n}", [HEADS, S]) for n in range(4)]
        resets = [sb(f"resets{n}", [HEADS, S]) for n in range(3)]
        spread = sb("spread", [P, BLOCKS, 2, HEADS])
        loaded = sem("loaded")
        with nc.Block() as block:
            @block.sync
            def _(sp):
                sp.dma_start(dst[:].rearrange("p b e -> p (b e)"), dram["dst_t"]).then_inc(loaded, DMA)
                sp.dma_start(rel[:].rearrange("p b e -> p (b e)"), dram["drel_t"]).then_inc(loaded, DMA)
                sp.wait_ge(loaded, 2 * DMA)
        v = nc.vector

        def limits(a):
            return lambda: v.tensor_scalar(a, a, 2 * BIG, -BIG, ALU.mult, ALU.add)

        on_vector(nc, "softmax_valid", [
            lambda: v.tensor_single_scalar(reset[:], rel[:], 0.0, op=ALU.is_ge),
            lambda: v.tensor_single_scalar(back[:], rel[:], float(P), op=ALU.is_lt),
            lambda: v.tensor_tensor(rel[:], reset[:], back[:], ALU.mult), limits(rel[:])])
        with ExitStack() as inner:
            _, psum_in, sem_in = _scope(nc, inner, "softmax_turn")
            turned = psum_in("turned", [P, 2, HEADS, P])
            flipped, taken = sem_in("flipped"), sem_in("taken")
            with nc.Block() as block:
                @block.tensor
                def _(pe):
                    for b in range(BLOCKS):
                        if b >= 2:
                            pe.wait_ge(taken, b - 1)
                        for h in range(HEADS):
                            last = nc.tensor.transpose(turned[:, b % 2, h, :], score[:, b * P:(b + 1) * P, h], k["ident"][:])
                        last.then_inc(flipped, 1)

                @block.vector
                def _(dve):
                    for b in range(BLOCKS):
                        dve.wait_ge(flipped, b + 1)
                        v.scalar_tensor_tensor(out=by_step[:, :, b, :], in0=turned[:, b % 2, :, :], scalar=1.0 / math.sqrt(DHEAD),
                                               in1=rel[:, b, :].unsqueeze(1).to_broadcast([P, HEADS, P]),
                                               op0=ALU.mult, op1=ALU.min).then_inc(taken, 1)
        tops = sb("tops", [P, HEADS, BLOCKS, P])
        flat = lambda a: a.rearrange("p b e -> p (b e)")
        steps = [lambda: v.memset(reset[:], 0.0),
                 lambda: v.tensor_tensor(reset[:, :, 1:P], dst[:, :, 1:P], dst[:, :, 0:P - 1], ALU.is_equal), limits(reset[:])]
        steps += [lambda h=h: v.tensor_tensor_scan(flat(tops[:, h]), flat(reset[:]), flat(by_step[:, h]), -BIG, ALU.min, ALU.max)
                  for h in range(HEADS)]
        steps += [lambda h=h: v.tensor_copy(edge_of[:, :, 0, h], tops[:, h, :, P - 1]) for h in range(HEADS)]
        steps += [lambda: v.memset(reset[:], 0.0),
                  lambda: v.tensor_tensor(reset[:, :, 0:P - 1], dst[:, :, 1:P], dst[:, :, 0:P - 1], ALU.is_equal), limits(reset[:])]
        for h in range(HEADS):
            steps += [lambda h=h: v.tensor_tensor_scan(flat(back[:])[:, ::-1], flat(reset[:])[:, ::-1], flat(by_step[:, h])[:, ::-1],
                                                       -BIG, ALU.min, ALU.max),
                      lambda h=h: v.tensor_copy(edge_of[:, :, 1, h], back[:, :, 0]),
                      lambda h=h: v.tensor_tensor(tops[:, h], tops[:, h], back[:], ALU.max),
                      lambda h=h: v.tensor_copy(edge_of[:, :, 2, h], dst[:, :, 0]),
                      lambda h=h: v.tensor_copy(edge_of[:, :, 3, h], dst[:, :, P - 1])]
        on_vector(nc, "softmax_scan", steps)
        with ExitStack() as inner:
            _, psum_in, sem_in = _scope(nc, inner, "softmax_rows")
            rows = psum_in("rows", [HEADS, 4, 4, P])
            flipped, taken = sem_in("flipped"), sem_in("taken")
            with nc.Block() as block:
                @block.tensor
                def _(pe):
                    for n in range(4):
                        if n:
                            pe.wait_ge(taken, n)
                        for b in range(BLOCKS):
                            last = nc.tensor.transpose(rows[:, b // 4, b % 4, :], edge_of[:, b, n, :], k["ident"][:])
                        last.then_inc(flipped, 1)

                @block.vector
                def _(dve):
                    for n in range(4):
                        dve.wait_ge(flipped, n + 1)
                        v.tensor_copy(carry[n][:], rows[:].rearrange("h a b e -> h (a b e)")[:, 0:S]).then_inc(taken, 1)
        last_max, first_max, first_dst, last_dst = (c[:] for c in carry)
        cont, whole, limit = (c[:] for c in resets)
        on_vector(nc, "softmax_carry", [
            lambda: v.tensor_tensor(whole, first_dst, last_dst, ALU.is_equal),
            lambda: v.memset(cont, 0.0),
            lambda: v.tensor_tensor(cont[:, 1:S], first_dst[:, 1:S], last_dst[:, 0:S - 1], ALU.is_equal),
            lambda: v.tensor_tensor(limit, whole, cont, ALU.mult), limits(limit),
            lambda: v.tensor_tensor_scan(first_dst, limit, last_max, -BIG, ALU.min, ALU.max),
            lambda: v.tensor_copy(limit, whole),
            lambda: v.memset(limit[:, S - 1:S], 0.0),
            lambda: v.tensor_tensor(limit[:, 0:S - 1], whole[:, 0:S - 1], cont[:, 1:S], ALU.mult), limits(limit),
            lambda: v.tensor_tensor_scan(last_dst[:, ::-1], limit[:, ::-1], first_max[:, ::-1], -BIG, ALU.min, ALU.max),
            limits(cont),
            lambda: v.memset(last_max, -BIG), lambda: v.memset(first_max, -BIG),
            lambda: v.tensor_tensor(last_max[:, 1:S], first_dst[:, 0:S - 1], cont[:, 1:S], ALU.min),
            lambda: v.tensor_tensor(first_max[:, 0:S - 1], last_dst[:, 1:S], cont[:, 1:S], ALU.min)])
        with ExitStack() as inner:
            _, psum_in, sem_in = _scope(nc, inner, "softmax_columns")
            columns = psum_in("columns", [P, BLOCKS, 2, HEADS])
            flipped = sem_in("flipped")
            with nc.Block() as block:
                @block.tensor
                def _(pe):
                    for b in range(BLOCKS):
                        for n in range(2):
                            last = nc.tensor.transpose(columns[:, b, n, :], carry[n][:, b * P:(b + 1) * P], k["ident"][0:HEADS, 0:HEADS])
                    last.then_inc(flipped, 1)

                @block.vector
                def _(dve):
                    dve.wait_ge(flipped, 1)
                    v.tensor_copy(spread[:], columns[:])
        steps = []
        for n, e in ((0, 0), (1, P - 1)):
            steps += [lambda e=e: v.tensor_tensor(reset[:], dst[:], dst[:, :, e:e + 1].to_broadcast([P, BLOCKS, P]), ALU.is_equal),
                      limits(reset[:])]
            steps += [lambda b=b, h=h, n=n: v.scalar_tensor_tensor(out=tops[:, h, b, :], in0=reset[:, b, :], scalar=spread[:, b, n, h:h + 1],
                                                                   in1=tops[:, h, b, :], op0=ALU.min, op1=ALU.max)
                      for b in range(BLOCKS) for h in range(HEADS)]
        steps += [lambda: v.tensor_tensor(by_step[:], by_step[:], tops[:], ALU.subtract)]
        on_vector(nc, "softmax_top", steps)
        with ExitStack() as inner:
            _, psum_in, sem_in = _scope(nc, inner, "softmax_exp")
            turned = psum_in("turned", [P, 2, HEADS, P])
            raised, flipped, taken = sem_in("raised"), sem_in("flipped"), sem_in("taken")
            with nc.Block() as block:
                @block.scalar
                def _(act):
                    for b in range(BLOCKS):
                        nc.scalar.activation(tops[:, :, b, :], by_step[:, :, b, :], ACT.Exp).then_inc(raised, 1)

                @block.tensor
                def _(pe):
                    for b in range(BLOCKS):
                        pe.wait_ge(raised, b + 1)
                        if b >= 2:
                            pe.wait_ge(taken, b - 1)
                        for h in range(HEADS):
                            last = nc.tensor.transpose(turned[:, b % 2, h, :], tops[:, h, b, :], k["ident"][:])
                        last.then_inc(flipped, 1)

                @block.vector
                def _(dve):
                    for b in range(BLOCKS):
                        dve.wait_ge(flipped, b + 1)
                        v.tensor_copy(score[:, b * P:(b + 1) * P, :], turned[:, b % 2, :, :].rearrange("p h e -> p e h")).then_inc(taken, 1)


def value_pass(nc, k, dram, weight, sums):
    width = D + HEADS
    with ExitStack() as ctx:
        sb, psum, sem = _scope(nc, ctx, "value")
        ring = sb("ring", [P, R, G, 2 * D])
        message = [sb(f"message{h}", [P, G, width]) for h in range(2)]
        onehot = [sb(f"onehot{h}", [P, G, P]) for h in range(2)]
        accumulator = psum("accumulator", [P, BANKS * BANK])
        made, added, cleared, copied, checked, messaged = (
            sem(n) for n in ("made", "added", "cleared", "copied", "checked", "messaged"))
        loaded = [sem(f"loaded{q}") for q in range(R)]
        used = [sem(f"used{q}") for q in range(R)]
        with nc.Block() as block:
            @block.scalar
            def _(act):
                _take_tiles(nc, act, k, accumulator, width, cleared, added, copied, checked,
                            lambda tile: sums[:, bass.ds(tile, 1), :].rearrange("p j f -> p (j f)"))

            @block.sync
            def _(sp):
                with sp.Fori(0, ITERS) as i:
                    for q in range(R):
                        sp.wait_ge(used[q], i)
                        sp.dma_start(ring[:, q, :, :].rearrange("p g f -> p (g f)"),
                                     dram["kv"][:, bass.ds((i * R + q) * G * 2 * D, G * 2 * D)]).then_inc(loaded[q], DMA)

            @block.gpsimd
            def _(pool):
                with pool.Fori(0, ITERS) as i:
                    for q in range(R):
                        pool.wait_ge(added, (i * R + q + 2) * G)
                        pool.wait_ge(loaded[q], (i + 1) * DMA)
                        nc.gpsimd.tensor_tensor(
                            message[q % 2][:, :, 0:D].rearrange("p g (h d) -> p g h d", d=DHEAD),
                            ring[:, q, :, D:2 * D].rearrange("p g (h d) -> p g h d", d=DHEAD),
                            weight[:, bass.ds((i * R + q) * G, G), :].unsqueeze(3).to_broadcast([P, G, HEADS, DHEAD]),
                            ALU.mult).then_inc(used[q], 1)
                        nc.gpsimd.tensor_copy(message[q % 2][:, :, D:width],
                                              weight[:, bass.ds((i * R + q) * G, G), :]).then_inc(messaged, 1)

            @block.vector
            def _(dve):
                _one_hot(nc, k, onehot[0], 0).then_inc(made, 1)
                with dve.Fori(0, ITERS) as i:
                    for q in range(R):
                        dve.wait_ge(added, (i * R + q) * G + LEAD)
                        _one_hot(nc, k, onehot[(q + 1) % 2], (i * R + q + 1) * G).then_inc(made, 1)

            @block.tensor
            def _(pe):
                pe.sem_inc(added, LEAD)
                with pe.Fori(0, ITERS) as i:
                    for q in range(R):
                        adder = Adder(nc, pe, k, i * R + q, BANKS, accumulator, width, cleared, added)
                        pe.wait_ge(made, i * R + q + 1)
                        pe.wait_ge(messaged, i * R + q + 1)
                        for g in range(G):
                            adder.add(g, onehot[q % 2][:, g, :], message[q % 2][:, g, :])


def attention(nc, io, k, dram):
    v = nc.vector
    with ExitStack() as ctx:
        sb, _, _ = _scope(nc, ctx, "att")
        h = sb("h", [P, JP, D])
        flat_h = h[:].rearrange("p j f -> p (j f)")
        norm_relu(nc, k, "att_norm", h)
        on_vector(nc, "att_add_h", [lambda: v.tensor_tensor(k["x"][:], k["x"][:], h[:], ALU.add)])
        score = sb("score", [P, S, HEADS])
        with ExitStack() as inner:
            sbi, _, _ = _scope(nc, inner, "qkv")
            qkv = sbi("qkv", [P, JP, 3 * D])
            w = sbi("w", [P, 1, 4 * 3 * D])
            load_diagonal(nc, "qkv_w", w[:].rearrange("p o (q f) -> p (o q) f", q=4), [io["L1_gnn_Wq"], io["L1_gnn_Wk"], io["L1_gnn_Wv"]])
            node_linear(nc, k, "qkv_lin", flat_h, JP // 4, 1, w, qkv[:].rearrange("p j f -> p (j f)"))
            on_vector(nc, "qkv_q", [lambda: v.tensor_copy(h[:], qkv[:, :, 0:D])])
            store_table(nc, "qkv_table", dram["tab64"], qkv[:, :, D:3 * D], 2 * D)
        score_pass(nc, k, dram, flat_h, score)
        softmax_weights(nc, k, dram, score)
        with ExitStack() as inner:
            sbi, _, _ = _scope(nc, inner, "wo")
            sums = sbi("sums", [P, JP, D + HEADS])
            on_vector(nc, "wo_clear", [lambda: v.memset(sums[:, TILES:JP, :], 0.0)])
            value_pass(nc, k, dram, score, sums)
            w = sbi("w", [P, 1, 4 * D])
            load_diagonal(nc, "wo_w", w[:].rearrange("p o (q f) -> p (o q) f", q=4), [io["L1_gnn_Wo"]])
            on_vector(nc, "wo_divide", [
                lambda: v.tensor_single_scalar(sums[:, :, D:D + HEADS], sums[:, :, D:D + HEADS], 1e-16, op=ALU.max),
                lambda: v.reciprocal(sums[:, :, D:D + HEADS], sums[:, :, D:D + HEADS]),
                lambda: v.tensor_tensor(h[:].rearrange("p j (h d) -> p j h d", d=DHEAD),
                                        sums[:, :, 0:D].rearrange("p j (h d) -> p j h d", d=DHEAD),
                                        sums[:, :, D:D + HEADS].unsqueeze(3).to_broadcast([P, JP, HEADS, DHEAD]), ALU.mult)])
            out = sums[:].rearrange("p j f -> p (j f)")[:, 0:JP * D]
            node_linear(nc, k, "wo_lin", flat_h, JP // 4, 1, w, out)
            on_vector(nc, "wo_add", [lambda: v.tensor_tensor(k["x"][:].rearrange("p j f -> p (j f)"),
                                                             k["x"][:].rearrange("p j f -> p (j f)"), out, ALU.add)])


def split_steps(v, parts, rest, a):
    steps = []
    for n in range(3):
        part = parts(n)
        steps.append(lambda part=part: v.tensor_copy(part, a))
        if n < 2:
            steps.append(lambda part=part: v.tensor_copy(rest, part))
            steps.append(lambda: v.tensor_tensor(a, a, rest, ALU.subtract))
    return steps


def relation_pass(nc, k, dram, y_nodes, relations, current):
    H, WIDTH, LOOK = G // 2, N_BASES * D, D + N_BASES
    EARLY = R * G - G
    with ExitStack() as ctx:
        sb, psum, sem = _scope(nc, ctx, "rel")
        staged = sb("staged", [P, R, G], U32)
        ring = sb("ring", [P, R, G, 2 * D])
        onehot = [sb(f"onehot{m}", [P, H, P]) for m in range(8)]
        onehot_t = [sb(f"onehot_t{m}", [P, H, P], BF16) for m in range(2)]
        kind = [sb(f"kind{m}", [P, H, N_REL], BF16) for m in range(2)]
        kind_t = [sb(f"kind_t{m}", [N_REL, H, P], BF16) for m in range(2)]
        dots = sb("dots", [P, H, D])
        logits = [sb(f"logits{m}", [P, H]) for m in range(2)]
        gate = [sb(f"gate{m}", [P, H]) for m in range(2)]
        weights = [sb(f"weights{m}", [P, H, N_BASES]) for m in range(2)]
        coef = [sb(f"coef{m}", [P, H, N_BASES]) for m in range(2)]
        message = [sb(f"message{m}", [P, H, WIDTH]) for m in range(2)]
        taken = sb("taken", [P, 2 * BANK])
        flipped_ps = psum("flipped_ps", [P, 2, H, P])
        flipped_kind = psum("flipped_kind", [P, 1, H, P], BF16)
        looked = psum("looked", [P, 2, BANK])
        accumulator = psum("accumulator", [P, 2 * BANK])
        (indexed, released, made, flipped, turned, looked_up, logit, gated, weighed, messaged, added, cleared, copied,
         checked, passed, work, own, freed) = (
            sem(n) for n in ("indexed", "released", "made", "flipped", "turned", "looked_up", "logit", "gated", "weighed",
                             "messaged", "added", "cleared", "copied", "checked", "passed", "work", "own", "freed"))
        gathered = [sem(f"gathered{q}") for q in range(R)]
        saved = sem("saved")

        def make_one_hots(dve, n, m):
            _one_hot(nc, k, onehot[m], n * H, H)
            nc.vector.tensor_tensor(kind[m % 2][:], k["iota"][:, 0:N_REL].unsqueeze(1).to_broadcast([P, H, N_REL]),
                                    k["type"][:, bass.ds(n * H, H)].unsqueeze(2).to_broadcast([P, H, N_REL]),
                                    ALU.is_equal).then_inc(made, 1)

        def make_logits(dve, n, m, q, h):
            dve.wait_ge(looked_up, n + 1)
            seen = looked[:, m % 2, 0:H * LOOK].rearrange("p (g f) -> p g f", f=LOOK)
            nc.vector.tensor_tensor(dots[:], seen[:, :, 0:D], ring[:, q, h * H:(h + 1) * H, D:2 * D], ALU.mult).then_inc(work, 1)
            dve.wait_ge(work, n * 2 + 1)
            nc.vector.tensor_reduce(logits[m % 2][:], dots[:], axis=AX_X, op=ALU.add).then_inc(work, 1)
            nc.vector.tensor_copy(weights[m % 2][:], seen[:, :, D:LOOK]).then_inc(freed, 1)
            dve.wait_ge(work, n * 2 + 2)
            nc.vector.tensor_single_scalar(logits[m % 2][:], logits[m % 2][:], 0.0, op=ALU.max).then_inc(logit, 1)

        def make_messages(dve, n, m, q, h):
            dve.wait_ge(gated, n + 1)
            dve.wait_ge(freed, n + 1)
            nc.vector.tensor_tensor(coef[m % 2][:], weights[m % 2][:], gate[m % 2][:].unsqueeze(2).to_broadcast([P, H, N_BASES]),
                                    ALU.mult).then_inc(weighed, 1)
            dve.wait_ge(weighed, n + 1)
            for g in range(H):
                nc.vector.tensor_tensor(
                    message[m % 2][:, g, :].rearrange("p (b f) -> p b f", f=D),
                    coef[m % 2][:, g, :].unsqueeze(2).to_broadcast([P, N_BASES, D]),
                    ring[:, q, h * H + g, 0:D].unsqueeze(1).to_broadcast([P, N_BASES, D]), ALU.mult).then_inc(messaged, 1)

        def flip(pe, n, m):
            pe.wait_ge(made, n + 1)
            for g in range(H):
                nc.tensor.transpose(flipped_ps[:, m % 2, g, :], onehot[m][:, g, :], k["ident"][:])
            for g in range(H):
                last = nc.tensor.transpose(flipped_kind[0:N_REL, 0, g, :], kind[m % 2][:, g, :], k["ident16"][:])
            last.then_inc(flipped, 1)

        def look_up(pe, n, m, tiles):
            pe.wait_ge(turned, n + 1)
            if not isinstance(n, int) or n >= 2:
                pe.wait_ge(freed, n - 1)
            for g in range(H):
                out = looked[:, m % 2, g * LOOK:(g + 1) * LOOK]
                for c in range(3):
                    nc.tensor.matmul(out, kind_t[m % 2][:, g, :], relations[:, c, :], start=(c == 0), stop=(c == 2))
                rows = pe.snap(tiles[g] * (3 * D))
                for c in range(3):
                    last = nc.tensor.matmul(out[:, 0:D], onehot_t[m % 2][:, g, :], y_nodes[:, bass.ds(rows + c * D, D)],
                                            start=False, stop=True, skip_group_check=True)
            last.then_inc(looked_up, 1)

        def turn(act, n, m):
            act.wait_ge(flipped, n + 1)
            nc.scalar.copy(onehot_t[m % 2][:], flipped_ps[:, m % 2, :, :])
            nc.scalar.copy(kind_t[m % 2][:], flipped_kind[0:N_REL, 0, :, :]).then_inc(turned, 1)

        def close_gate(act, n, m):
            act.wait_ge(logit, n + 1)
            nc.scalar.activation(gate[m % 2][:], logits[m % 2][:], ACT.Tanh, scale=1.0 / math.sqrt(D)).then_inc(gated, 1)

        with nc.Block() as block:
            @block.scalar
            def _(act):
                for h in range(2):
                    nc.scalar.copy(accumulator[:, h * BANK:(h + 1) * BANK], k["zeros"][:]).then_inc(cleared, 1)
                for n in range(3):
                    if n == 2:
                        act.wait_ge(looked_up, 1)
                    turn(act, n, n)
                close_gate(act, 0, 0)
                with act.Fori(0, ITERS) as i:
                    for q in range(R):
                        tiles = _tile_registers(nc, act, _word(act, k, i * R + q))
                        for h in range(2):
                            n, m = (i * R + q) * 2 + h, q * 2 + h
                            act.wait_ge(looked_up, n + 2)
                            turn(act, n + 3, m + 3)
                            close_gate(act, n + 1, m + 1)
                            for g in range(h * H, h * H + H):
                                _take_if_last(nc, act, k, (i * R + q) * G + g, tiles[g], tiles[g + 1] - tiles[g], accumulator, taken,
                                              WIDTH, cleared, added, copied, checked, saved)

            @block.gpsimd
            def _(pool):
                _gather_rows(nc, pool, dram["tab64"], staged, ring, indexed, released, gathered,
                             lambda i, q: pool.wait_ge(messaged, (i * R + q) * G))
                pool.wait_ge(indexed, GROUPS + 1)
                for g in range(G):
                    nc.gpsimd.indirect_dma_start(
                        out=ring[:, 0, g, :], out_offset=None, in_=dram["tab64"],
                        in_offset=bass.IndirectOffsetOnAxis(ap=staged[:, 0, g:g + 1], axis=0)).then_inc(gathered[0], DMA)
                for j in range(J):
                    nc.gpsimd.indirect_dma_start(
                        out=current[:, j, :], out_offset=None, in_=dram["tab32"],
                        in_offset=bass.IndirectOffsetOnAxis(ap=k["last_index"][:, j:j + 1], axis=0)).then_inc(own, DMA)
                pool.wait_ge(own, J * DMA)
                pool.wait_ge(gathered[0], (ITERS + 1) * G * DMA)

            @block.vector
            def _(dve):
                dve.sem_inc(messaged, EARLY)
                for q in range(R - 1):
                    _stage(nc, k, staged, q, q).then_inc(indexed, 1)
                for n in range(3):
                    if n == 2:
                        dve.wait_ge(flipped, 1)
                    make_one_hots(dve, n, n)
                dve.wait_ge(gathered[0], G * DMA)
                make_logits(dve, 0, 0, 0, 0)
                with dve.Fori(0, ITERS) as i:
                    for q in range(R):
                        for h in range(2):
                            n, m = (i * R + q) * 2 + h, q * 2 + h
                            dve.wait_ge(added, n * H + LEAD - H)
                            dve.wait_ge(flipped, n + 2)
                            make_one_hots(dve, n + 3, (m + 3) % 8)
                            if h == 1:
                                dve.wait_ge(gathered[(q + 1) % R], (i + 1 + (q == R - 1)) * G * DMA)
                            make_logits(dve, n + 1, m + 1, (q + h) % R, 1 - h)
                            make_messages(dve, n, m, q, h)
                            if h == 0:
                                _stage(nc, k, staged, i * R + q + R - 1, (q + R - 1) % R).then_inc(indexed, 1)

            @block.tensor
            def _(pe):
                pe.sem_inc(added, LEAD)
                first = _tile_registers(nc, pe, _word(pe, k, 0))[:G] + _tile_registers(nc, pe, _word(pe, k, 1))[:H]
                for n in range(3):
                    if n:
                        pe.wait_ge(turned, n)
                    flip(pe, n, n)
                    look_up(pe, n, n, first[n * H:(n + 1) * H])
                with pe.Fori(0, ITERS) as i:
                    words = [_word(pe, k, i * R + q) for q in range(R + 2)]
                    for q in range(R):
                        adder = Adder(nc, pe, k, i * R + q, 2, accumulator, WIDTH, cleared, added, words[q])
                        for h in range(2):
                            n, m = (i * R + q) * 2 + h, q * 2 + h
                            ahead = _tile_registers(nc, pe, words[q + 1 + h])[(1 - h) * H:(2 - h) * H]
                            pe.wait_ge(turned, n + 3)
                            flip(pe, n + 3, (m + 3) % 8)
                            for g in range(H):
                                pe.wait_ge(messaged, n * H + g + 1 + EARLY)
                                adder.add(h * H + g, onehot[m][:, g, :], message[m % 2][:, g, :])
                            look_up(pe, n + 3, m + 3, ahead)

            @block.sync
            def _(sp):
                _save_tiles(sp, taken, dram["totals"], WIDTH, copied, saved, passed)


def relational(nc, io, k, dram):
    v = nc.vector
    with ExitStack() as ctx:
        sb, _, _ = _scope(nc, ctx, "rl")
        h = sb("h", [P, JP, D])
        flat_h = h[:].rearrange("p j f -> p (j f)")
        LOOK = D + N_BASES
        y_nodes = sb("y", [P, JP, 3, D], BF16)
        relations = sb("relations", [N_REL, 3, LOOK], BF16)
        current = sb("current", [P, JP, D])
        norm_relu(nc, k, "rl_norm", h)
        with ExitStack() as inner:
            sbi, _, _ = _scope(nc, inner, "hat")
            both = sbi("both", [P, JP, 2 * D])
            w = sbi("w", [P, 1, 8 * D])
            bias = sbi("bias", [P, 2 * D])
            table = sbi("table", [N_REL, LOOK])
            table_rest = sbi("table_rest", [N_REL, LOOK])
            y = sbi("y32", [P, JP, D])
            y_rest = sbi("y_rest", [P, JP, D])
            load_diagonal(nc, "hat_w", w[:].rearrange("p o (q f) -> p (o q) f", q=4), [io["A1_t"], io["A2_t"]])
            load_rows(nc, "hat_b", [(bias[:, 0:D], io["L2_gnn_A1_b"].unsqueeze(0).to_broadcast([P, D])),
                                    (bias[:, D:2 * D], io["L2_gnn_A2_b"].unsqueeze(0).to_broadcast([P, D])),
                                    (table[:, 0:D], io["L2_gnn_rel_emb"]), (table[:, D:LOOK], io["L2_gnn_w_comp"])])
            node_linear(nc, k, "hat_lin", flat_h, JP // 4, 1, w, both[:].rearrange("p j f -> p (j f)"))
            on_vector(nc, "hat_bias", [
                lambda: v.tensor_tensor(both[:], both[:], bias[:].unsqueeze(1).to_broadcast([P, JP, 2 * D]), ALU.add),
                lambda: v.tensor_copy(y[:], both[:, :, D:2 * D]),
                lambda: v.tensor_copy(both[:, :, D:2 * D], both[:, :, 0:D]),
                lambda: v.tensor_copy(both[:, :, 0:D], h[:]),
                lambda: v.memset(current[:], 0.0)]
                + split_steps(v, lambda c: y_nodes[:, :, c, :], y_rest[:], y[:])
                + split_steps(v, lambda c: relations[:, c, :], table_rest[:], table[:]))
            store_table(nc, "hat_table", dram["tab64"], both, 2 * D)
            store_table(nc, "hat_rows", dram["tab32"], h, D)
        relation_pass(nc, k, dram, y_nodes[:].rearrange("p j c f -> p (j c f)"), relations, current)
        with ExitStack() as inner:
            sbi, _, _ = _scope(nc, inner, "rlo")
            own_w = sbi("own_w", [P, 1, 4 * D])
            w = sbi("w", [P, 4, D])
            out = sbi("out", [P, JP, D])
            has = sbi("has", [P, JP])
            load_diagonal(nc, "rlo_own_w", own_w[:].rearrange("p o (q f) -> p (o q) f", q=4), [io["L2_gnn_self_loop_weight"]])
            load_rows(nc, "rlo_w", [(w[:], io["L2_gnn_weight"].rearrange("b i o -> (b i) o").rearrange("(c p) o -> p c o", p=P))])
            node_linear(nc, k, "rlo_own", current[:].rearrange("p j f -> p (j f)"), JP // 4, 1, own_w, flat_h)
            on_vector(nc, "rlo_clear", [lambda: v.memset(out[:], 0.0)])
            node_linear(nc, k, "rlo_lin", dram["totals"], J, 4, w, out[:].rearrange("p j f -> p (j f)"), load=True)
            on_vector(nc, "rlo_out", [
                lambda: v.tensor_tensor(out[:], out[:], h[:], ALU.add),
                lambda: v.tensor_single_scalar(has[:], k["degree"][:], 0.0, op=ALU.is_gt),
                lambda: v.tensor_tensor(out[:], out[:], _spread(has[:], D), ALU.mult),
                lambda: v.tensor_single_scalar(out[:], out[:], 0.0, op=ALU.max),
                lambda: v.tensor_tensor(k["x"][:], k["x"][:], out[:], ALU.add)])


SH_WIDTH = 4 * D + 5 * 24


def harmonic_pass(nc, k, dram):
    with ExitStack() as ctx:
        sb, psum, sem = _scope(nc, ctx, "sh")
        staged = sb("staged", [P, R, G], U32)
        ring = sb("ring", [P, R, G, D])
        parts = sb("parts", [P, R, G, N_SH])
        onehot = [sb(f"onehot{h}", [P, G, P]) for h in range(2)]
        message = [sb(f"message{h}", [P, G, SH_WIDTH]) for h in range(2)]
        taken = sb("taken", [P, 2 * BANK])
        accumulator = psum("accumulator", [P, 2 * BANK])
        indexed, released, made, messaged, added, cleared, copied, checked, passed, saved = (
            sem(n) for n in ("indexed", "released", "made", "messaged", "added", "cleared", "copied", "checked", "passed", "saved"))
        gathered = [sem(f"gathered{q}") for q in range(R)]
        loaded = [sem(f"loaded{q}") for q in range(R)]

        def load_parts(act, group, slot):
            act.dma_start(parts[:, slot, :, :].rearrange("p g f -> p (g f)"),
                          dram["sh"][:, bass.ds(group * G * N_SH, G * N_SH)]).then_inc(loaded[slot], DMA)

        with nc.Block() as block:
            @block.scalar
            def _(act):
                for h in range(2):
                    nc.scalar.copy(accumulator[:, h * BANK:(h + 1) * BANK], k["zeros"][:]).then_inc(cleared, 1)
                for q in range(R - 1):
                    load_parts(act, q, q)
                with act.Fori(0, ITERS) as i:
                    for q in range(R):
                        act.wait_ge(messaged, i * R + q + R - 1)
                        act.sem_inc(checked, 1)
                        load_parts(act, i * R + q + R - 1, (q + R - 1) % R)
                        tiles = _tile_registers(nc, act, _word(act, k, i * R + q))
                        for g in range(G):
                            _take_if_last(nc, act, k, (i * R + q) * G + g, tiles[g], tiles[g + 1] - tiles[g], accumulator, taken,
                                          SH_WIDTH, cleared, added, copied, checked, saved)
                for q in range(R - 1):
                    act.wait_ge(loaded[q], (ITERS + 1) * DMA)

            @block.gpsimd
            def _(pool):
                _gather_rows(nc, pool, dram["tab32"], staged, ring, indexed, released, gathered,
                             lambda i, q: pool.wait_ge(messaged, i * R + q))

            @block.vector
            def _(dve):
                dve.sem_inc(messaged, R - 1)
                nc.vector.memset(taken[:], 0.0)
                for q in range(R - 1):
                    _stage(nc, k, staged, q, q).then_inc(indexed, 1)
                with dve.Fori(0, ITERS) as i:
                    for q in range(R):
                        dve.wait_ge(added, (i * R + q) * G + LEAD - G)
                        _one_hot(nc, k, onehot[q % 2], (i * R + q) * G).then_inc(made, 1)
                        dve.wait_ge(loaded[q], (i + 1) * DMA)
                        dve.wait_ge(gathered[q], (i + 1) * G * DMA)
                        m = message[q % 2]
                        nc.vector.tensor_tensor(m[:, :, 0:4 * D].rearrange("p g (c f) -> p g c f", f=D),
                                                parts[:, q, :, 0:4].unsqueeze(3).to_broadcast([P, G, 4, D]),
                                                ring[:, q, :, :].unsqueeze(2).to_broadcast([P, G, 4, D]), ALU.mult)
                        nc.vector.tensor_tensor(m[:, :, 4 * D:SH_WIDTH].rearrange("p g (c f) -> p g c f", f=24),
                                                parts[:, q, :, 4:N_SH].unsqueeze(3).to_broadcast([P, G, 5, 24]),
                                                ring[:, q, :, 8:D].unsqueeze(2).to_broadcast([P, G, 5, 24]), ALU.mult).then_inc(messaged, 1)
                        _stage(nc, k, staged, i * R + q + R - 1, (q + R - 1) % R).then_inc(indexed, 1)

            @block.tensor
            def _(pe):
                pe.sem_inc(added, LEAD)
                with pe.Fori(0, ITERS) as i:
                    for q in range(R):
                        adder = Adder(nc, pe, k, i * R + q, 2, accumulator, SH_WIDTH, cleared, added, _word(pe, k, i * R + q))
                        pe.wait_ge(made, i * R + q + 1)
                        pe.wait_ge(messaged, i * R + q + R)
                        for g in range(G):
                            adder.add(g, onehot[q % 2][:, g, :], message[q % 2][:, g, :])

            @block.sync
            def _(sp):
                _save_tiles(sp, taken, dram["totals"], 2 * P, copied, saved, passed)


def tensor_product(nc, io, k, dram, out):
    v = nc.vector
    with ExitStack() as ctx:
        sb, _, _ = _scope(nc, ctx, "tp")
        with ExitStack() as inner:
            sbi, _, _ = _scope(nc, inner, "tph")
            h = sbi("h", [P, JP, D])
            norm_relu(nc, k, "tp_norm", h)
            store_table(nc, "tp_table", dram["tab32"], h, D)
        harmonic_pass(nc, k, dram)
        with ExitStack() as inner:
            sbi, psi, _ = _scope(nc, inner, "mix")
            pick = sbi("pick", [8, 2 * P])
            w_all = sbi("w_all", [8, 6 * 8])
            cg = sbi("cg", [P, 14])
            row_w = sbi("row_w", [P, 2, 6 * 8])
            mix = sbi("mix", [P, 2, D])
            delta = sbi("delta", [P, JP, D])
            picked = psi("picked", [P, 2, 64])
            load_rows(nc, "mix_in", [(pick[:], io["pick"]), (cg[:], io["cg"]),
                                     (w_all[:].rearrange("i (c o) -> i c o", o=8), io["L3_gnn_W"].rearrange("c i o -> i c o"))])
            with ExitStack() as inner2:
                _, _, sem = _scope(nc, inner2, "mix_pick")
                ready, taken = sem("ready"), sem("taken")
                with nc.Block() as block:
                    @block.tensor
                    def _(pe):
                        for c in range(2):
                            last = nc.tensor.matmul(picked[:, c, 0:48], pick[:, c * P:(c + 1) * P], w_all[:], start=True, stop=True)
                        last.then_inc(ready, 1)

                    @block.vector
                    def _(dve):
                        v.memset(mix[:], 0.0).then_inc(taken, 1)
                        v.memset(delta[:], 0.0).then_inc(taken, 1)
                        dve.wait_ge(ready, 1)
                        v.tensor_copy(row_w[:], picked[:, :, 0:48])

            def add(c, n, combo, lo):
                to = mix[:, c, 0:8] if lo is None else mix[:, c, 8:D].rearrange("p (o k) -> p o k", k=3)[:, :, lo]
                return lambda: v.scalar_tensor_tensor(out=to, in0=row_w[:, c, 8 * combo:8 * combo + 8], scalar=cg[:, n:n + 1], in1=to,
                                                      op0=ALU.mult, op1=ALU.add)
            on_vector(nc, "mix_add", [add(c, n, combo, lo) for n, (c, combo, lo) in enumerate(MIX_TERMS)])
            node_linear(nc, k, "mix_lin", dram["totals"], J, 2, mix, delta[:].rearrange("p j f -> p (j f)"), load=True)
            on_vector(nc, "mix_x", [lambda: v.tensor_tensor(k["x"][:], k["x"][:], delta[:], ALU.add)])
        with ExitStack() as inner:
            _, _, sem = _scope(nc, inner, "out")
            stored = sem("stored")
            with nc.Block() as block:
                @block.sync
                def _(sp):
                    sp.dma_start(_node_rows(out, 0, J - 1), k["x"][:, 0:J - 1, :]).then_inc(stored, DMA)
                    sp.dma_start(out[(J - 1) * P:N_NODES, :], k["x"][0:LAST_TILE_ROWS, J - 1, :]).then_inc(stored, DMA)
                    sp.wait_ge(stored, 2 * DMA)


def _clebsch_gordan(l1, l2, l3):
    def su2(j1, m1, j2, m2, j3, m3):
        if m3 != m1 + m2:
            return 0.0
        f = math.factorial
        low = max(0, j2 - j3 - m1, j1 + m2 - j3)
        high = min(j1 + j2 - j3, j1 - m1, j2 + m2)
        pref = (2 * j3 + 1) * f(j3 + j1 - j2) * f(j3 - j1 + j2) * f(j1 + j2 - j3) / f(j1 + j2 + j3 + 1)
        pref *= f(j3 + m3) * f(j3 - m3) * f(j1 - m1) * f(j1 + m1) * f(j2 - m2) * f(j2 + m2)
        return math.sqrt(pref) * sum((-1) ** n / (f(n) * f(j1 + j2 - j3 - n) * f(j1 - m1 - n) * f(j2 + m2 - n)
                                                 * f(j3 - j2 + m1 + n) * f(j3 - j1 - m2 + n)) for n in range(low, high + 1))

    def real(l):
        q = np.zeros((2 * l + 1, 2 * l + 1), complex)
        for m in range(-l, 0):
            q[l + m, l - m] = 1 / np.sqrt(2)
            q[l + m, l + m] = -1j / np.sqrt(2)
        q[l, l] = 1.0
        for m in range(1, l + 1):
            q[l + m, l + m] = (-1) ** m / np.sqrt(2)
            q[l + m, l - m] = 1j * (-1) ** m / np.sqrt(2)
        return (-1j) ** l * q

    c = np.zeros((2 * l1 + 1, 2 * l2 + 1, 2 * l3 + 1), complex)
    for m1 in range(-l1, l1 + 1):
        for m2 in range(-l2, l2 + 1):
            if -l3 <= m1 + m2 <= l3:
                c[m1 + l1, m2 + l2, m1 + m2 + l3] = su2(l1, m1, l2, m2, l3, m1 + m2)
    c = np.einsum("ij,kl,mn,ikn->jlm", real(l1), real(l2), np.conj(real(l3)).T, c).real
    return c / np.linalg.norm(c)


MIX_TERMS = ([(0, 0, None)] + [(0, 1, o) for o in range(3)] + [(0, 2, o) for o in range(3)] + [(0, 3, None)]
             + [(0, 4, o) for o in range(3)] + [(1, 5, o) for o in range(3)])


def mixing_constants():
    combos = [(0, 0, 0), (0, 1, 1), (1, 0, 1), (1, 1, 0), (1, 1, 1), (2, 1, 1)]
    coefficients = [_clebsch_gordan(*c) for c in combos]
    pick = np.zeros((8, 2 * P), np.float32)
    cg = np.zeros((P, len(MIX_TERMS)), np.float32)
    for row in range(2 * P):
        if row < P:
            part, f = divmod(row, D)
            degree, component = (0, 0) if part == 0 else (1, part - 1)
        else:
            if row >= P + 120:
                continue
            component, f = divmod(row - P, 24)
            degree, f = 2, f + 8
        vector = f >= 8
        channel, direction = divmod(f - 8, 3) if vector else (f, 0)
        pick[channel, row] = 1.0
        for n, (chunk, combo, o) in enumerate(MIX_TERMS):
            le, ln, _ = combos[combo]
            if chunk == row // P and le == degree and ln == int(vector):
                cg[row % P, n] = coefficients[combo][component, direction, o or 0]
    return pick, cg


def gnn_kernel(nc, io, out):
    dram = scratch(nc)
    with ExitStack() as ctx:
        k = tables(nc, ctx)
        constants(nc, k)
        edge_records(nc, io, k, dram)
        sort_records(nc, io, k, dram)
        merge_path(nc, k, dram)
        with ExitStack() as inner:
            k["stat"] = inner.enter_context(nc.sbuf_tensor("k_stat", [P, S, 3], BF16))
            step_tables(nc, k, dram)
            node_statistics(nc, k)
        load_x(nc, io, k)
        gcn(nc, io, k, dram)
        attention(nc, io, k, dram)
        relational(nc, io, k, dram)
        tensor_product(nc, io, k, dram, out)


def tables(nc, ctx):
    def sb(n, shape, dt=F32):
        return ctx.enter_context(nc.sbuf_tensor(f"k_{n}", shape, dt))
    k = {"iota": sb("iota", [P, P]), "ident": sb("ident", [P, P]), "ident16": sb("ident16", [P, P], BF16), "ones": sb("ones", [P, P]),
         "step_no": sb("step_no", [P, BLOCKS]), "t_of": sb("t_of", [P, BLOCKS]), "j_of": sb("j_of", [P, BLOCKS]),
         "t_index": sb("t_index", [P, BLOCKS], U32), "ends": sb("ends", [1, P], I32),
         "places": sb("places", [1, GROUPS], I32),
         "words": sb("words", [1, GROUPS + 2], I32), "src": sb("src", [P, S + R * G], U32),
         "drel": sb("drel", [P, S + 2 * G]), "type": sb("type", [P, S + 2 * G]),
         "x": sb("x", [P, JP, D]), "degree": sb("degree", [P, JP]), "zeros": sb("zeros", [P, BANK]),
         "unsorted": sb("unsorted", [1, 1], I32),
         "last_index": sb("last_index", [P, JP], U32), "dinv": sb("dinv", [P, JP])}
    return k


def scratch(nc):
    def d(n, shape, dt=F32):
        return nc.dram_tensor(f"scratch_{n}", shape, dt, kind="Internal").ap()
    return {"sorted": d("sorted", [(P + 1) * T, REC]), "dst_row": d("dst_row", [1, CHUNKS * CHUNK], I32), "rec": d("rec", [T, P * REC]), "j": d("j", [1, S]), "ends": d("ends", [1, P], I32), "dst_t": d("dst_t", [P, S]), "drel_t": d("drel_t", [P, S]),
            "sh": d("sh", [P, (S + R * G) * N_SH]), "tab32": d("tab32", [J * P, D]), "tab64": d("tab64", [J * P, 2 * D]),
            "tab128": d("tab128", [J * P, HID]), "totals": d("totals", [P, JP * 512]), "kv": d("kv", [P, S * 2 * D])}


def kernel(**inputs):
    import concourse.bacc as bacc
    from concourse.bass_utils import run_bass_kernel_spmd as run

    nc = bacc.Bacc("TRN2", target_bir_lowering=False, num_devices=1)
    given = {n: np.ascontiguousarray(a) for n, a in inputs.items() if n not in ("L2_gnn_A1_w", "L2_gnn_A2_w")}
    given["A1_t"] = np.ascontiguousarray(np.asarray(inputs["L2_gnn_A1_w"]).T)
    given["A2_t"] = np.ascontiguousarray(np.asarray(inputs["L2_gnn_A2_w"]).T)
    given["pick"], given["cg"] = mixing_constants()
    arrays = {f"in_{n}": a for n, a in given.items()}
    io = {n: nc.dram_tensor(f"in_{n}", a.shape, mybir.dt.from_np(a.dtype), kind="ExternalInput").ap() for n, a in given.items()}
    out = nc.dram_tensor("out_x", (N_NODES, D), F32, kind="ExternalOutput").ap()
    gnn_kernel(nc, io, out)
    return run(nc, [arrays], core_ids=[0]).results[0]["out_x"]
```
